# Optimizing a Trainium2 kernel written in Bass

```python
import numpy as np
import jax
import jax.numpy as jnp

def _softmax(x, axis=-1):
    return jax.nn.softmax(x, axis=axis)

def _gelu(x):
    return jax.nn.gelu(x, approximate=True)

def _silu(x):
    return jax.nn.silu(x)

def _sigmoid(x):
    return jax.nn.sigmoid(x)

def _layernorm(x, axis=-1, eps=1e-05):
    m = jnp.mean(x, axis=axis, keepdims=True)
    v = jnp.var(x, axis=axis, keepdims=True)
    return (x - m) / jnp.sqrt(v + eps)

def _scatter_add(tgt, idx, src, axis=0):
    return tgt.at[idx].add(src)

def _segment_sum(src, seg, n):
    return jax.ops.segment_sum(src, seg, n)
kernel_name = 'mk_adaln_d2_jaxref_r8_978674'

def setup_inputs(seed: int=0):
    np.random.seed(seed)
    _w = jnp.asarray

    def _L0_attn_setup():
        import jax, jax.numpy as jnp
        import numpy as np
        import math
        D_MODEL = 128
        N_HEADS = 16
        D_HEAD = D_MODEL // N_HEADS
        LSR_RANK = 32
        B, T = (4, 256)
        key = jax.random.key(seed)
        ks = jax.random.split(key, 11)
        s = 1.0 / math.sqrt(D_MODEL)
        x = jax.random.normal(ks[0], (B, T, D_MODEL), dtype=jnp.float32)
        Wq = jax.random.uniform(ks[1], (D_MODEL, D_MODEL), minval=-s, maxval=s)
        bq = jax.random.uniform(ks[2], (D_MODEL,), minval=-s, maxval=s)
        Wk = jax.random.uniform(ks[3], (D_MODEL, D_MODEL), minval=-s, maxval=s)
        bk = jax.random.uniform(ks[4], (D_MODEL,), minval=-s, maxval=s)
        Wv = jax.random.uniform(ks[5], (D_MODEL, D_MODEL), minval=-s, maxval=s)
        bv = jax.random.uniform(ks[6], (D_MODEL,), minval=-s, maxval=s)
        Wo = jax.random.uniform(ks[7], (D_MODEL, D_MODEL), minval=-s, maxval=s)
        bo = jax.random.uniform(ks[8], (D_MODEL,), minval=-s, maxval=s)
        Wq_lsr = jax.random.normal(ks[9], (N_HEADS, D_HEAD, LSR_RANK)) / math.sqrt(D_HEAD)
        Wk_lsr = jax.random.normal(ks[10], (N_HEADS, D_HEAD, LSR_RANK)) / math.sqrt(D_HEAD)
        return {'x': x, 'Wq': Wq, 'bq': bq, 'Wk': Wk, 'bk': bk, 'Wv': Wv, 'bv': bv, 'Wo': Wo, 'bo': bo, 'Wq_lsr': Wq_lsr, 'Wk_lsr': Wk_lsr}
    _L0_attn_in = _L0_attn_setup()

    def _L0_ffn_setup():
        import jax, jax.numpy as jnp
        import numpy as np
        H = 128
        I = 256
        E = 8
        B, S = (2, 512)
        EPS = 1e-05
        INIT = 0.02

        def _layernorm(x, w, b):
            mu = jnp.mean(x, axis=-1, keepdims=True)
            var = jnp.mean(jnp.square(x - mu), axis=-1, keepdims=True)
            return (x - mu) * jax.lax.rsqrt(var + EPS) * w + b
        key = jax.random.key(seed)
        ks = jax.random.split(key, 9)
        return {'hidden_states': jax.random.normal(ks[0], (B, S, H), jnp.float32), 'ln_w': jnp.ones((H,), jnp.float32), 'ln_b': jnp.zeros((H,), jnp.float32), 'router_w': jax.random.normal(ks[1], (H, E), jnp.float32) * INIT, 'gate_w': jax.random.normal(ks[2], (E, H, I), jnp.float32) * INIT, 'up_w': jax.random.normal(ks[3], (E, H, I), jnp.float32) * INIT, 'down_w': jax.random.normal(ks[4], (E, I, H), jnp.float32) * INIT, 'sh_gate': jax.random.normal(ks[5], (H, I), jnp.float32) * INIT, 'sh_up': jax.random.normal(ks[6], (H, I), jnp.float32) * INIT, 'sh_down': jax.random.normal(ks[7], (I, H), jnp.float32) * INIT}
    _L0_ffn_in = _L0_ffn_setup()
    _L0_c = _w((lambda *s: np.random.randn(*s).astype(np.float32) * 0.05)(8, 128))
    _L0_wmod = _w((lambda *s: np.random.randn(*s).astype(np.float32) * 0.05)(128, 6 * 128) * 128 ** (-0.5))

    def _L1_attn_setup():
        import math
        import jax, jax.numpy as jnp
        import numpy as np
        HIDDEN = 128
        NUM_LAYERS = 24
        LAYER_ID = 4

        def _time_params():
            h = HIDDEN
            ratio_0_to_1 = LAYER_ID / (NUM_LAYERS - 1)
            ratio_1_to_almost_0 = 1.0 - LAYER_ID / NUM_LAYERS
            zigzag = 0.5 * (jnp.arange(1, h + 1) % 3 - 1)
            time_first = jnp.full(h, math.log(0.3)) + zigzag
            idx = jnp.arange(0, h)
            time_decay = -5 + 8 * (idx / (h - 1)) ** (0.7 + 1.3 * ratio_0_to_1)
            x = jnp.arange(h) / h
            time_mix_key = jnp.power(x, ratio_1_to_almost_0)
            time_mix_value = time_mix_key + 0.3 * ratio_0_to_1
            time_mix_receptance = jnp.power(x, 0.5 * ratio_1_to_almost_0)
            return (time_decay.astype(jnp.float32), time_first.astype(jnp.float32), time_mix_key.astype(jnp.float32), time_mix_value.astype(jnp.float32), time_mix_receptance.astype(jnp.float32))

        def _wkv(time_decay, time_first, k, v):
            B, T, H = k.shape
            td = -jnp.exp(time_decay.astype(jnp.float32))
            tf = time_first.astype(jnp.float32)
            kT = jnp.swapaxes(k, 0, 1).astype(jnp.float32)
            vT = jnp.swapaxes(v, 0, 1).astype(jnp.float32)

            def step(carry, kv):
                num, den, mx = carry
                ck, cv = kv
                max_out = jnp.maximum(mx, ck + tf)
                e1 = jnp.exp(mx - max_out)
                e2 = jnp.exp(ck + tf - max_out)
                out = (e1 * num + e2 * cv) / (e1 * den + e2)
                max_st = jnp.maximum(mx + td, ck)
                e1s = jnp.exp(mx + td - max_st)
                e2s = jnp.exp(ck - max_st)
                return ((e1s * num + e2s * cv, e1s * den + e2s, max_st), out)
            init = (jnp.zeros((B, H), jnp.float32), jnp.zeros((B, H), jnp.float32), jnp.full((B, H), -1e+38, jnp.float32))
            _, outT = jax.lax.scan(step, init, (kT, vT))
            return jnp.swapaxes(outT, 0, 1).astype(k.dtype)
        key = jax.random.key(seed)
        k0, k1, k2, k3, k4 = jax.random.split(key, 5)
        B, T, H = (4, 512, HIDDEN)
        td, tf, tmk, tmv, tmr = _time_params()
        scale = 0.02
        return {'hidden': jax.random.normal(k0, (B, T, H), dtype=jnp.float32), 'Wk': jax.random.normal(k1, (H, H), dtype=jnp.float32) * scale, 'Wv': jax.random.normal(k2, (H, H), dtype=jnp.float32) * scale, 'Wr': jax.random.normal(k3, (H, H), dtype=jnp.float32) * scale, 'Wo': jax.random.normal(k4, (H, H), dtype=jnp.float32) * scale, 'time_decay': td, 'time_first': tf, 'time_mix_key': tmk, 'time_mix_value': tmv, 'time_mix_receptance': tmr}
    _L1_attn_in = _L1_attn_setup()

    def _L1_ffn_setup():
        import jax, jax.numpy as jnp
        import numpy as np
        D_MODEL = 128
        M = 64
        INNER = 16
        key = jax.random.key(seed)
        ks = jax.random.split(key, 9)

        def init(k, shape, fan_in):
            bound = 1.0 / np.sqrt(fan_in)
            return jax.random.uniform(k, shape, jnp.float32, -bound, bound)
        x = jax.random.normal(ks[0], (16, 512, D_MODEL), dtype=jnp.float32)
        Win = init(ks[1], (D_MODEL, M), D_MODEL)
        bin_ = init(ks[2], (M,), D_MODEL)
        W1 = init(ks[3], (M, INNER), 1)
        b1 = init(ks[4], (M, INNER), 1)
        W2 = init(ks[5], (M, INNER), INNER)
        b2 = init(ks[6], (M,), INNER)
        Wout = init(ks[7], (M, D_MODEL), M)
        bout = init(ks[8], (D_MODEL,), M)
        return {'x': x, 'Win': Win, 'bin_': bin_, 'W1': W1, 'b1': b1, 'W2': W2, 'b2': b2, 'Wout': Wout, 'bout': bout}
    _L1_ffn_in = _L1_ffn_setup()
    _L1_c = _w((lambda *s: np.random.randn(*s).astype(np.float32) * 0.05)(8, 128))
    _L1_wmod = _w((lambda *s: np.random.randn(*s).astype(np.float32) * 0.05)(128, 6 * 128) * 128 ** (-0.5))
    _d = {'L0_attn_x': _L0_attn_in['x'], 'L0_attn_Wq': _L0_attn_in['Wq'], 'L0_attn_bq': _L0_attn_in['bq'], 'L0_attn_Wk': _L0_attn_in['Wk'], 'L0_attn_bk': _L0_attn_in['bk'], 'L0_attn_Wv': _L0_attn_in['Wv'], 'L0_attn_bv': _L0_attn_in['bv'], 'L0_attn_Wo': _L0_attn_in['Wo'], 'L0_attn_bo': _L0_attn_in['bo'], 'L0_attn_Wq_lsr': _L0_attn_in['Wq_lsr'], 'L0_attn_Wk_lsr': _L0_attn_in['Wk_lsr'], 'L0_ffn_ln_w': _L0_ffn_in['ln_w'], 'L0_ffn_ln_b': _L0_ffn_in['ln_b'], 'L0_ffn_router_w': _L0_ffn_in['router_w'], 'L0_ffn_gate_w': _L0_ffn_in['gate_w'], 'L0_ffn_up_w': _L0_ffn_in['up_w'], 'L0_ffn_down_w': _L0_ffn_in['down_w'], 'L0_ffn_sh_gate': _L0_ffn_in['sh_gate'], 'L0_ffn_sh_up': _L0_ffn_in['sh_up'], 'L0_ffn_sh_down': _L0_ffn_in['sh_down'], 'L0_c': _L0_c, 'L0_wmod': _L0_wmod, 'L1_attn_Wk': _L1_attn_in['Wk'], 'L1_attn_Wv': _L1_attn_in['Wv'], 'L1_attn_Wr': _L1_attn_in['Wr'], 'L1_attn_Wo': _L1_attn_in['Wo'], 'L1_attn_time_decay': _L1_attn_in['time_decay'], 'L1_attn_time_first': _L1_attn_in['time_first'], 'L1_attn_time_mix_key': _L1_attn_in['time_mix_key'], 'L1_attn_time_mix_value': _L1_attn_in['time_mix_value'], 'L1_attn_time_mix_receptance': _L1_attn_in['time_mix_receptance'], 'L1_ffn_Win': _L1_ffn_in['Win'], 'L1_ffn_bin_': _L1_ffn_in['bin_'], 'L1_ffn_W1': _L1_ffn_in['W1'], 'L1_ffn_b1': _L1_ffn_in['b1'], 'L1_ffn_W2': _L1_ffn_in['W2'], 'L1_ffn_b2': _L1_ffn_in['b2'], 'L1_ffn_Wout': _L1_ffn_in['Wout'], 'L1_ffn_bout': _L1_ffn_in['bout'], 'L1_c': _L1_c, 'L1_wmod': _L1_wmod}
    _x0 = _d['L0_attn_x']
    _d['L0_attn_x'] = jax.random.normal(jax.random.fold_in(jax.random.key(seed), 1), (8, 512, 128), dtype=_x0.dtype)
    del _x0
    return _d

def reference(L0_attn_x, L0_attn_Wq, L0_attn_bq, L0_attn_Wk, L0_attn_bk, L0_attn_Wv, L0_attn_bv, L0_attn_Wo, L0_attn_bo, L0_attn_Wq_lsr, L0_attn_Wk_lsr, L0_ffn_ln_w, L0_ffn_ln_b, L0_ffn_router_w, L0_ffn_gate_w, L0_ffn_up_w, L0_ffn_down_w, L0_ffn_sh_gate, L0_ffn_sh_up, L0_ffn_sh_down, L0_c, L0_wmod, L1_attn_Wk, L1_attn_Wv, L1_attn_Wr, L1_attn_Wo, L1_attn_time_decay, L1_attn_time_first, L1_attn_time_mix_key, L1_attn_time_mix_value, L1_attn_time_mix_receptance, L1_ffn_Win, L1_ffn_bin_, L1_ffn_W1, L1_ffn_b1, L1_ffn_W2, L1_ffn_b2, L1_ffn_Wout, L1_ffn_bout, L1_c, L1_wmod):

    def _L0_attn_ref(x, Wq, bq, Wk, bk, Wv, bv, Wo, bo, Wq_lsr, Wk_lsr):
        import jax, jax.numpy as jnp
        import numpy as np
        import math
        D_MODEL = 128
        N_HEADS = 16
        D_HEAD = D_MODEL // N_HEADS
        LSR_RANK = 32
        B, T = (4, 256)
        Bq, Tq, _ = x.shape

        def split_heads(y):
            return y.reshape(Bq, Tq, N_HEADS, D_HEAD).transpose(0, 2, 1, 3)
        q = split_heads(x @ Wq.T + bq)
        k = split_heads(x @ Wk.T + bk)
        v = split_heads(x @ Wv.T + bv)
        q_lr = jnp.einsum('bhtd,hdr->bhtr', q, Wq_lsr)
        k_lr = jnp.einsum('bhtd,hdr->bhtr', k, Wk_lsr)
        scale = 1.0 / math.sqrt(max(LSR_RANK, 1))
        scores = jnp.einsum('bhir,bhjr->bhij', q_lr, k_lr) * scale
        causal_mask = jnp.triu(jnp.ones((Tq, Tq), dtype=bool), k=1)
        scores = jnp.where(causal_mask, jnp.float32(-jnp.inf), scores)
        attn = jax.nn.softmax(scores, axis=-1)
        y = jnp.einsum('bhij,bhjd->bhid', attn, v)
        y = y.transpose(0, 2, 1, 3).reshape(Bq, Tq, D_MODEL)
        return y @ Wo.T + bo

    def _L0_ffn_ref(hidden_states, ln_w, ln_b, router_w, gate_w, up_w, down_w, sh_gate, sh_up, sh_down):
        import jax, jax.numpy as jnp
        import numpy as np
        H = 128
        I = 256
        E = 8
        B, S = (2, 512)
        EPS = 1e-05
        INIT = 0.02

        def _layernorm(x, w, b):
            mu = jnp.mean(x, axis=-1, keepdims=True)
            var = jnp.mean(jnp.square(x - mu), axis=-1, keepdims=True)
            return (x - mu) * jax.lax.rsqrt(var + EPS) * w + b
        b, s, h = hidden_states.shape
        normed = _layernorm(hidden_states, ln_w, ln_b)
        xf = normed.reshape(-1, h)
        logits = xf @ router_w
        top_idx = jnp.argmax(logits, axis=-1)
        top_score = jax.nn.sigmoid(jnp.max(logits, axis=-1))

        def body(acc, ew):
            g, u, d, e = ew
            w = jnp.where(top_idx == e, top_score, 0.0)[:, None]
            xe = xf * w
            hmid = jax.nn.silu(xe @ g) * (xe @ u)
            return (acc + hmid @ d, None)
        routed, _ = jax.lax.scan(body, jnp.zeros_like(xf), (gate_w, up_w, down_w, jnp.arange(E)))
        shared = jax.nn.silu(xf @ sh_gate) * (xf @ sh_up) @ sh_down
        moe_out = (routed + shared).reshape(b, s, h)
        return hidden_states + moe_out

    def _L1_attn_ref(hidden, Wk, Wv, Wr, Wo, time_decay, time_first, time_mix_key, time_mix_value, time_mix_receptance):
        import math
        import jax, jax.numpy as jnp
        import numpy as np
        HIDDEN = 128
        NUM_LAYERS = 24
        LAYER_ID = 4

        def _time_params():
            h = HIDDEN
            ratio_0_to_1 = LAYER_ID / (NUM_LAYERS - 1)
            ratio_1_to_almost_0 = 1.0 - LAYER_ID / NUM_LAYERS
            zigzag = 0.5 * (jnp.arange(1, h + 1) % 3 - 1)
            time_first = jnp.full(h, math.log(0.3)) + zigzag
            idx = jnp.arange(0, h)
            time_decay = -5 + 8 * (idx / (h - 1)) ** (0.7 + 1.3 * ratio_0_to_1)
            x = jnp.arange(h) / h
            time_mix_key = jnp.power(x, ratio_1_to_almost_0)
            time_mix_value = time_mix_key + 0.3 * ratio_0_to_1
            time_mix_receptance = jnp.power(x, 0.5 * ratio_1_to_almost_0)
            return (time_decay.astype(jnp.float32), time_first.astype(jnp.float32), time_mix_key.astype(jnp.float32), time_mix_value.astype(jnp.float32), time_mix_receptance.astype(jnp.float32))

        def _wkv(time_decay, time_first, k, v):
            B, T, H = k.shape
            td = -jnp.exp(time_decay.astype(jnp.float32))
            tf = time_first.astype(jnp.float32)
            kT = jnp.swapaxes(k, 0, 1).astype(jnp.float32)
            vT = jnp.swapaxes(v, 0, 1).astype(jnp.float32)

            def step(carry, kv):
                num, den, mx = carry
                ck, cv = kv
                max_out = jnp.maximum(mx, ck + tf)
                e1 = jnp.exp(mx - max_out)
                e2 = jnp.exp(ck + tf - max_out)
                out = (e1 * num + e2 * cv) / (e1 * den + e2)
                max_st = jnp.maximum(mx + td, ck)
                e1s = jnp.exp(mx + td - max_st)
                e2s = jnp.exp(ck - max_st)
                return ((e1s * num + e2s * cv, e1s * den + e2s, max_st), out)
            init = (jnp.zeros((B, H), jnp.float32), jnp.zeros((B, H), jnp.float32), jnp.full((B, H), -1e+38, jnp.float32))
            _, outT = jax.lax.scan(step, init, (kT, vT))
            return jnp.swapaxes(outT, 0, 1).astype(k.dtype)
        shifted = jnp.pad(hidden, ((0, 0), (1, 0), (0, 0)))[:, :-1]
        k_in = hidden * time_mix_key + shifted * (1 - time_mix_key)
        v_in = hidden * time_mix_value + shifted * (1 - time_mix_value)
        r_in = hidden * time_mix_receptance + shifted * (1 - time_mix_receptance)
        k = k_in @ Wk
        v = v_in @ Wv
        r = jax.nn.sigmoid(r_in @ Wr)
        rwkv = _wkv(time_decay, time_first, k, v)
        return r * rwkv @ Wo

    def _L1_ffn_ref(x, Win, bin_, W1, b1, W2, b2, Wout, bout):
        import jax, jax.numpy as jnp
        import numpy as np
        D_MODEL = 128
        M = 64
        INNER = 16
        s = jnp.einsum('btd,dm->btm', x, Win) + bin_
        h = jax.nn.relu(s[..., None] * W1 + b1)
        g = jnp.einsum('btmh,mh->btm', h, W2) + b2
        out = jnp.einsum('btm,md->btd', g, Wout) + bout
        return out
    x = L0_attn_x
    mod = (_silu(L0_c) @ L0_wmod).reshape(L0_c.shape[0], 6, 1, -1)
    sa, ca, ga, sb, cb, gb = (mod[:, 0], mod[:, 1], mod[:, 2], mod[:, 3], mod[:, 4], mod[:, 5])
    ga = (2 * (ga >= 0) - 1) * jnp.maximum(jnp.abs(ga), 0.25)
    gb = (2 * (gb >= 0) - 1) * jnp.maximum(jnp.abs(gb), 0.25)
    h = _layernorm(x, axis=-1) * (1 + ca) + sa
    x = x + ga * _L0_attn_ref(h, L0_attn_Wq, L0_attn_bq, L0_attn_Wk, L0_attn_bk, L0_attn_Wv, L0_attn_bv, L0_attn_Wo, L0_attn_bo, L0_attn_Wq_lsr, L0_attn_Wk_lsr)
    h = _layernorm(x, axis=-1) * (1 + cb) + sb
    x = x + gb * _L0_ffn_ref(h, L0_ffn_ln_w, L0_ffn_ln_b, L0_ffn_router_w, L0_ffn_gate_w, L0_ffn_up_w, L0_ffn_down_w, L0_ffn_sh_gate, L0_ffn_sh_up, L0_ffn_sh_down)
    mod = (_silu(L1_c) @ L1_wmod).reshape(L1_c.shape[0], 6, 1, -1)
    sa, ca, ga, sb, cb, gb = (mod[:, 0], mod[:, 1], mod[:, 2], mod[:, 3], mod[:, 4], mod[:, 5])
    ga = (2 * (ga >= 0) - 1) * jnp.maximum(jnp.abs(ga), 0.25)
    gb = (2 * (gb >= 0) - 1) * jnp.maximum(jnp.abs(gb), 0.25)
    h = _layernorm(x, axis=-1) * (1 + ca) + sa
    x = x + ga * _L1_attn_ref(h, L1_attn_Wk, L1_attn_Wv, L1_attn_Wr, L1_attn_Wo, L1_attn_time_decay, L1_attn_time_first, L1_attn_time_mix_key, L1_attn_time_mix_value, L1_attn_time_mix_receptance)
    h = _layernorm(x, axis=-1) * (1 + cb) + sb
    x = x + gb * _L1_ffn_ref(h, L1_ffn_Win, L1_ffn_bin_, L1_ffn_W1, L1_ffn_b1, L1_ffn_W2, L1_ffn_b2, L1_ffn_Wout, L1_ffn_bout)
    return x

_drawn_inputs = setup_inputs


def setup_inputs(seed=0):
    import zlib

    import numpy as np

    out = dict(_drawn_inputs(seed))
    spreads = {'L0_ffn_ln_w': (1.0, 0.6), 'L0_ffn_ln_b': (0.0, 0.8)}
    factors = {'L0_attn_Wq': 8.0,
     'L0_attn_bq': 8.0,
     'L0_attn_Wk': 8.0,
     'L0_attn_bk': 64.0,
     'L0_attn_Wv': 5.702,
     'L0_attn_bv': 7.376,
     'L0_attn_Wo': 4.552,
     'L0_attn_bo': 4.169,
     'L0_attn_Wq_lsr': 8.0,
     'L0_attn_Wk_lsr': 8.0,
     'L0_ffn_router_w': 8.0,
     'L0_ffn_gate_w': 8.0,
     'L0_ffn_up_w': 8.0,
     'L0_ffn_down_w': 8.0,
     'L0_ffn_sh_gate': 8.0,
     'L0_ffn_sh_up': 8.0,
     'L0_ffn_sh_down': 8.0,
     'L1_attn_Wk': 8.0,
     'L1_attn_Wv': 8.0,
     'L1_attn_Wr': 8.0,
     'L1_attn_Wo': 8.0,
     'L1_attn_time_decay': 8.0,
     'L1_attn_time_first': 8.0,
     'L1_attn_time_mix_key': 8.0,
     'L1_attn_time_mix_value': 8.0,
     'L1_attn_time_mix_receptance': 8.0,
     'L1_ffn_Win': 3.427,
     'L1_ffn_bin_': 64.0,
     'L1_ffn_W1': 3.362,
     'L1_ffn_bout': 20.506,
     'L1_ffn_b1': 8.0,
     'L1_ffn_b2': 8.0}
    for name, (base, spread) in spreads.items():
        noise = np.random.default_rng([zlib.crc32(name.encode()), seed]).standard_normal(out[name].shape)
        drawn = base * np.exp(spread * noise) if base else spread * noise
        out[name] = jnp.asarray(drawn.astype(out[name].dtype))
    for name, factor in factors.items():
        out[name] = (out[name] * factor).astype(out[name].dtype)
    return out
```

```python
from contextlib import ExitStack

import concourse.bass as bass
from concourse import mybir

F32 = mybir.dt.float32
BF16 = mybir.dt.bfloat16
ALU = mybir.AluOpType
ACT = mybir.ActivationFunctionType
AX_X = mybir.AxisListType.X

P = 128
D = 128
B, T = 8, 512
NB = T // P
H, DH, RANK = 16, 8, 32
HG = 4
NG = H // HG
SLOTS = 9
NPART = 3
MAX_ROW = 96
E, HID = 8, 256
HC = HID // P
M, INNER = 64, 16
HP = INNER // 2
EPS = 1e-5
NEG = -1.0e30
SCALE = 1.0 / RANK ** 0.5
TINY_MX = -1.0e38
GATE_MIN = 0.25

SHIFT, SCALE1, GATE = 0, 1, 2


def wait(eng, sem, value):
    if not (isinstance(value, int) and value <= 0):
        eng.wait_ge(sem, value)


def wait_apart(eng, sem, value, passed):
    if isinstance(value, int):
        wait(eng, sem, value)
    else:
        eng.wait_ge(sem, value)
        eng.sem_inc(passed, 1)


def adaln_kernel(nc, a, out):
    with ExitStack() as ctx:
        build(nc, ctx, a, out)


def build(nc, ctx, a, out):
    def sb(name, shape, dt=F32, c=ctx):
        return c.enter_context(nc.sbuf_tensor(name, shape, dt))

    def sem(name):
        return ctx.enter_context(nc.semaphore(name))

    ps = ctx.enter_context(nc.psum_tensor("ps", [P, 8, 512], F32))

    xT = sb("xT", [D, B, T])
    ident = sb("ident", [P, P])
    identb = sb("identb", [P, P], BF16)
    neghalf = sb("neghalf", [P, NB])
    one_col = sb("one_col", [P, 1])
    mod = [sb(f"mod{l}", [D, 6, B]) for l in range(2)]
    NAMES = ["bq", "bk", "bv", "bo", "ln_w", "ln_b", "td", "tf", "mk", "mv", "mr", "bout",
             "bin", "b2", "bqP", "bkP", "bo2", "cst", "ntd"]
    vec = sb("vec", [P, len(NAMES)])

    def col(name):
        i = NAMES.index(name)
        return vec[:, i:i + 1]

    WqP = sb("WqP", [D, DH, H])
    WkP = sb("WkP", [D, DH, H])
    WvT = sb("WvT", [D, D])
    WoT = sb("WoT", [D, D])
    gab = sb("gab", [D, B])
    gate_w = sb("gate_w", [D, E, HID])
    up_w = sb("up_w", [D, E, HID])
    down_w = sb("down_w", [P, E, HC, D])
    shg_w = sb("shg_w", [D, HID])
    shu_w = sb("shu_w", [D, HID])
    shd_w = sb("shd_w", [P, HC, D])
    router_w = sb("router_w", [D, E])
    Wmix = sb("Wmix", [D, 6, D])
    WoR = sb("WoR", [D, D])
    Win2 = sb("Win2", [D, 2, M])
    Wc = sb("Wc", [P, HP, D])
    w1p = sb("w1p", [P, HP])
    b1p = sb("b1p", [P, HP])

    setup(nc, a, sb, sem, ps, xT, ident, identb, neghalf, one_col, mod, col, WqP, WkP, WvT, WoT, gab,
          gate_w, up_w, down_w, shg_w, shu_w, shd_w, router_w, Wmix, WoR, Win2, Wc, w1p, b1p)
    with ExitStack() as c:
        attention(nc, a, lambda n, s, dt=F32: sb(n, s, dt, c), sem, ps, xT, ident, identb, neghalf,
                  mod[0], col, WqP, WkP, WvT, WoT, gab)
    with ExitStack() as c:
        moe(nc, lambda n, s, dt=F32: sb(n, s, dt, c), sem, ps, xT, ident, identb, neghalf, mod[0], col,
            gate_w, up_w, down_w, shg_w, shu_w, shd_w, router_w)
    with ExitStack() as c:
        mixing(nc, out, lambda n, s, dt=F32: sb(n, s, dt, c), sem, ps, xT, ident, neghalf, mod[1],
               col, Wmix, WoR, Win2, Wc, w1p, b1p)


def setup(nc, a, sb0, sem, ps, xT, ident, identb, neghalf, one_col, mod, col, WqP, WkP, WvT, WoT, gab,
          gate_w, up_w, down_w, shg_w, shu_w, shd_w, router_w, Wmix, WoR, Win2, Wc, w1p, b1p):
    with ExitStack() as c:
        def sb(name, shape, dt=F32):
            return sb0(name, shape, dt, c)

        raw = sb("raw", [P, 4, D])
        identP = sb("identP", [P, DH, H])
        lsr = sb("lsr", [P, 2, RANK])
        lsrT = sb("lsrT", [RANK, 2, P])
        bdmask = sb("bdmask", [P, H, DH])
        BD = sb("BD", [P, DH, H])
        c_in = sb("c_in", [B, 2, D])
        cT = sb("cT", [D, 2, B])
        th = sb("th", [D, 2, B])
        scT = sb("scT", [D, 2, B])
        wmod = sb("wmod", [D, 2, 6 * D])
        gtmp = sb("gtmp", [D, 2, 2, B])
        gabs = sb("gabs", [D, 2, 2, B])
        mixw = sb("mixw", [D, 3, D])
        omm = sb("omm", [D, 3])
        Wout2 = sb("Wout2", [P, D])
        w2p = sb("w2p", [P, HP])
        inner = sb("inner", [P, 3, INNER])
        small_loaded, weights_loaded, moe_loaded = sem("small_loaded"), sem("weights_loaded"), sem("moe_loaded")
        consts_ready, turned, folded, copied = sem("consts_ready"), sem("turned"), sem("folded"), sem("copied")
        tanh_ready, td_ready = sem("tanh_ready"), sem("td_ready")

        def column(name):
            return a[name].rearrange("(p o) -> p o", o=1)

        smalls = [(col("bq"), column("L0_attn_bq")), (col("bk"), column("L0_attn_bk")),
                  (col("bv"), column("L0_attn_bv")), (col("bo"), column("L0_attn_bo")),
                  (col("ln_w"), column("L0_ffn_ln_w")), (col("ln_b"), column("L0_ffn_ln_b")),
                  (col("td"), column("L1_attn_time_decay")), (col("tf"), column("L1_attn_time_first")),
                  (col("mk"), column("L1_attn_time_mix_key")), (col("mv"), column("L1_attn_time_mix_value")),
                  (col("mr"), column("L1_attn_time_mix_receptance")), (col("bout"), column("L1_ffn_bout")),
                  (c_in[:, 0, :], a["L0_c"]), (c_in[:, 1, :], a["L1_c"]),
                  (lsr[:, 0, :], a["L0_attn_Wq_lsr"].rearrange("h d r -> (h d) r")),
                  (lsr[:, 1, :], a["L0_attn_Wk_lsr"].rearrange("h d r -> (h d) r"))]
        for q in range(2):
            half = slice(M * q, M * (q + 1))
            smalls += [(col("bin")[half, :], column("L1_ffn_bin_")), (col("b2")[half, :], column("L1_ffn_b2"))]
            for k, name in enumerate(("L1_ffn_W1", "L1_ffn_b1", "L1_ffn_W2")):
                smalls.append((inner[half, k, :], a[name]))
            smalls += [(Wout2[half, :], a["L1_ffn_Wout"]), (Win2[:, q, :], a["L1_ffn_Win"])]
        bigs = [(raw[:, 0, :], a["L0_attn_Wq"]), (raw[:, 1, :], a["L0_attn_Wk"]),
                (raw[:, 2, :], a["L0_attn_Wv"]), (raw[:, 3, :], a["L0_attn_Wo"]),
                (wmod[:, 0, :], a["L0_wmod"]), (wmod[:, 1, :], a["L1_wmod"]),
                (mixw[:, 0, :], a["L1_attn_Wk"]), (mixw[:, 1, :], a["L1_attn_Wv"]),
                (mixw[:, 2, :], a["L1_attn_Wr"]), (WoR[:, :], a["L1_attn_Wo"])]
        moes = [(gate_w[:, :, :], a["L0_ffn_gate_w"].rearrange("e p f -> p e f")),
                (up_w[:, :, :], a["L0_ffn_up_w"].rearrange("e p f -> p e f")),
                (down_w[:, :, :, :], a["L0_ffn_down_w"].rearrange("e (c p) f -> p e c f", p=P)),
                (shg_w[:, :], a["L0_ffn_sh_gate"]), (shu_w[:, :], a["L0_ffn_sh_up"]),
                (shd_w[:, :, :], a["L0_ffn_sh_down"].rearrange("(c p) f -> p c f", p=P)),
                (router_w[:, :], a["L0_ffn_router_w"])]
        NSMALL, NBIG, NMOE = 16 * len(smalls), 16 * len(bigs), 16 * len(moes)

        with nc.Block() as block:
            @block.sync
            def _(sp):
                for dst, src in bigs:
                    sp.dma_start(dst, src).then_inc(weights_loaded, 16)
                for dst, src in moes:
                    sp.dma_start(dst, src).then_inc(moe_loaded, 16)
                sp.wait_ge(moe_loaded, NMOE)

            @block.gpsimd
            def _(pool):
                pool.memset(ident[:], 0.0).then_inc(consts_ready, 1)
                pool.memset(bdmask[:], 1.0).then_inc(consts_ready, 1)
                pool.memset(neghalf[:], -0.5).then_inc(consts_ready, 1)
                pool.memset(one_col[:], 1.0).then_inc(consts_ready, 1)
                pool.wait_ge(consts_ready, 4)
                pool.affine_select(out=ident[:], in_=ident[:], compare_op=ALU.not_equal, fill=1.0, base=0,
                                   pattern=[[-1, P]], channel_multiplier=1).then_inc(consts_ready, 1)
                pool.affine_select(out=bdmask[:], in_=bdmask[:], compare_op=ALU.is_ge, fill=0.0, base=0,
                                   pattern=[[-DH, H], [0, DH]], channel_multiplier=1).then_inc(consts_ready, 1)
                pool.wait_ge(consts_ready, 6)
                pool.affine_select(out=bdmask[:], in_=bdmask[:], compare_op=ALU.is_ge, fill=0.0, base=DH - 1,
                                   pattern=[[DH, H], [0, DH]], channel_multiplier=-1).then_inc(consts_ready, 1)
                pool.tensor_copy(identP[:].rearrange("p d h -> p h d"),
                                 ident[:].rearrange("p (h d) -> p h d", d=DH)).then_inc(consts_ready, 1)

            @block.tensor
            def _(pe):
                pe.wait_ge(consts_ready, 8)
                pe.wait_ge(small_loaded, NSMALL)
                for k in range(2):
                    pe.transpose(ps[0:RANK, 0, k * P:(k + 1) * P], lsr[:, k, :], ident[:])
                    pe.transpose(ps[:, 0, 256 + k * B:256 + (k + 1) * B], c_in[:, k, :], ident[0:B, 0:B])
                pe.matmul(ps[:, 0, 300:301], identP[:].rearrange("p d h -> p (d h)"), col("bk"),
                          start=True, stop=True)
                pe.matmul(ps[:, 0, 302:303], Wout2[0:M, :], col("b2")[0:M, :],
                          start=True, stop=True).then_inc(turned, 1)
                pe.wait_ge(weights_loaded, NBIG)
                for k in range(3):
                    last = pe.transpose(ps[:, 1, k * P:(k + 1) * P], raw[:, k + 1, :], ident[:])
                last.then_inc(turned, 1)
                pe.wait_ge(copied, 1)
                pe.matmul(ps[:, 2, 0:P], lsrT[:, 0, :], lsrT[:, 1, :], start=True, stop=True).then_inc(folded, 1)
                pe.wait_ge(copied, 2)
                pe.matmul(ps[:, 3, 0:1], WoT[:], col("bv"), start=True, stop=True).then_inc(folded, 1)
                pe.wait_ge(copied, 3)
                for l in range(2):
                    for j in range(6):
                        last = pe.matmul(ps[:, 4 + l, j * B:(j + 1) * B], wmod[:, l, j * D:(j + 1) * D],
                                         scT[:, l, :], start=True, stop=True)
                last.then_inc(folded, 1)
                pe.wait_ge(copied, 4)
                pe.matmul(ps[:, 6, 0:P], raw[:, 0, :], BD[:].rearrange("p d h -> p (d h)"), start=True, stop=True)
                pe.matmul(ps[:, 6, P:P + 1], BD[:].rearrange("p d h -> p (d h)"), col("bq"),
                          start=True, stop=True).then_inc(folded, 1)

            @block.scalar
            def _(act):
                for dst, src in smalls:
                    act.dma_start(dst, src).then_inc(small_loaded, 16)
                act.wait_ge(small_loaded, NSMALL)
                act.activation(col("ntd"), col("td"), ACT.Exp).then_inc(td_ready, 1)
                act.wait_ge(turned, 1)
                act.activation(th[:].rearrange("p l b -> p (l b)"), ps[:, 0, 256:256 + 2 * B], ACT.Tanh,
                               scale=0.5).then_inc(tanh_ready, 1)

            @block.vector
            def _(dve):
                dve.wait_ge(consts_ready, 8)
                dve.tensor_copy(identb[:], ident[:]).then_inc(td_ready, 1)
                dve.wait_ge(turned, 1)
                dve.wait_ge(tanh_ready, 1)
                dve.tensor_copy(lsrT[:].rearrange("p k n -> p (k n)"), ps[0:RANK, 0, 0:256]).then_inc(copied, 1)
                dve.scalar_tensor_tensor(scT[:].rearrange("p l b -> p (l b)"), th[:].rearrange("p l b -> p (l b)"),
                                         1.0, ps[:, 0, 256:256 + 2 * B], ALU.add, ALU.mult).then_inc(td_ready, 1)
                dve.tensor_copy(col("bkP"), ps[:, 0, 300:301])
                dve.tensor_tensor(col("cst"), col("bout"), ps[:, 0, 302:303], ALU.add)
                dve.wait_ge(turned, 2)
                dve.tensor_copy(WkP[:].rearrange("p d h -> p h d"),
                                ps[:, 1, 0:P].rearrange("p (h d) -> p h d", d=DH))
                dve.tensor_copy(WvT[:], ps[:, 1, P:2 * P])
                dve.tensor_copy(WoT[:], ps[:, 1, 2 * P:3 * P]).then_inc(copied, 1)
                dve.wait_ge(td_ready, 3)
                dve.tensor_scalar(scT[:], scT[:], 0.5, None, ALU.mult).then_inc(copied, 1)
                dve.wait_ge(folded, 1)
                dve.scalar_tensor_tensor(BD[:].rearrange("p d h -> p h d"),
                                         ps[:, 2, 0:P].rearrange("p (h d) -> p h d", d=DH), SCALE, bdmask[:],
                                         ALU.mult, ALU.mult).then_inc(copied, 1)
                dve.tensor_scalar(col("ntd"), col("ntd"), -1.0, None, ALU.mult)
                for k, m in enumerate(("mk", "mv", "mr")):
                    dve.tensor_scalar(omm[:, k:k + 1], col(m), -1.0, 1.0, ALU.mult, ALU.add).then_inc(td_ready, 1)
                for k, dst in enumerate((w1p, b1p, w2p)):
                    for q in range(2):
                        half = slice(M * q, M * (q + 1))
                        dve.tensor_copy(dst[half, :], inner[half, k, :].rearrange("m (p q) -> m q p", q=2)[:, q, :]).then_inc(td_ready, 1)
                dve.wait_ge(td_ready, 12)
                for k, m in enumerate(("mk", "mv", "mr")):
                    dve.tensor_scalar(Wmix[:, 2 * k, :], mixw[:, k, :], col(m), None, ALU.mult)
                    dve.tensor_scalar(Wmix[:, 2 * k + 1, :], mixw[:, k, :], omm[:, k:k + 1], None, ALU.mult)
                for p in range(HP):
                    dve.tensor_scalar(Wc[:, p, :], Wout2[:], w2p[:, p:p + 1], None, ALU.mult)
                dve.wait_ge(folded, 2)
                dve.tensor_tensor(col("bo2"), col("bo"), ps[:, 3, 0:1], ALU.add).then_inc(td_ready, 1)
                dve.wait_ge(folded, 3)
                for l in range(2):
                    dve.tensor_copy(mod[l][:].rearrange("p j b -> p (j b)"), ps[:, 4 + l, 0:6 * B]).then_inc(td_ready, 1)
                dve.wait_ge(td_ready, 15)
                for l in range(2):
                    for s in range(2):
                        g = mod[l][:, 3 * s + GATE, :]
                        dve.tensor_scalar(mod[l][:, 3 * s + SCALE1, :], mod[l][:, 3 * s + SCALE1, :], 1.0, None, ALU.add)
                        dve.tensor_scalar(gtmp[:, l, s, :], g, 0.0, 2.0, ALU.is_ge, ALU.mult)
                        dve.tensor_scalar(gabs[:, l, s, :], g, -1.0, None, ALU.mult).then_inc(td_ready, 1)
                dve.wait_ge(td_ready, 19)
                for l in range(2):
                    for s in range(2):
                        dve.tensor_tensor(gabs[:, l, s, :], gabs[:, l, s, :], mod[l][:, 3 * s + GATE, :],
                                          ALU.max).then_inc(td_ready, 1)
                dve.wait_ge(td_ready, 23)
                dve.tensor_scalar(gabs[:], gabs[:], GATE_MIN, None, ALU.max).then_inc(td_ready, 1)
                dve.wait_ge(td_ready, 24)
                for l in range(2):
                    for s in range(2):
                        dve.scalar_tensor_tensor(mod[l][:, 3 * s + GATE, :], gtmp[:, l, s, :], -1.0,
                                                 gabs[:, l, s, :], ALU.add, ALU.mult).then_inc(td_ready, 1)
                dve.wait_ge(td_ready, 28)
                dve.tensor_scalar(gab[:], mod[0][:, GATE, :], col("bo2"), None, ALU.mult)
                dve.wait_ge(folded, 4)
                dve.tensor_copy(WqP[:].rearrange("p d h -> p (d h)"), ps[:, 6, 0:P])
                dve.tensor_copy(col("bqP"), ps[:, 6, P:P + 1]).then_inc(td_ready, 1)


def attention(nc, a, sb, sem, ps, xT, ident, identb, neghalf, mod, col, WqP, WkP, WvT, WoT, gab):
    x_in = [sb(f"x_in{p}", [P, NB, D]) for p in range(2)]
    xn = sb("xn", [P, NB, D])
    hT = sb("hT", [D, T])
    mv = sb("mv_a", [P, NB, 2])
    stats = sb("stats_a", [P, NB, 6])
    rstd = sb("rstd_a", [P, NB])
    full = sb("full", [P, 2, T])
    rest = sb("rest", [P, 2, T])
    part = sb("part", [P, 2, NPART, T], BF16)
    Qs = [sb(f"Qs{p}", [P, H, T], BF16) for p in range(2)]
    Ks = [sb(f"Ks{p}", [P, H, T], BF16) for p in range(2)]
    V = [sb(f"V{p}", [P, NB, D]) for p in range(2)]
    Vg = sb("Vg", [P, NB, HG, 32])
    mask4 = sb("mask4", [P, HG, P], BF16)
    maskT = sb("maskT", [P, 2, P], BF16)
    mask_f = sb("mask_f", [P, P])
    nmax = [sb(f"nmax{p}", [P, NB, H]) for p in range(2)]
    nrest = sb("nrest", [P, NB, H])
    npart_wide = sb("npart", [P, NB, P], BF16)
    npart = npart_wide[:, :, 0:NPART * H].rearrange("p n (k h) -> p n k h", k=NPART)
    nmT = sb("nmT", [NPART * H, T], BF16)
    zero48 = sb("zero48", [NPART * H, T], BF16)
    PR = sb("PR", [P, HG, 1280])
    yT = sb("yT", [P, NG, T])
    rec = sb("rec", [P, NG, NB, HG])
    yn = sb("yn", [P, NB, H, DH])
    ynT = sb("ynT", [D, T])
    SEG = {0: (0, 512), 1: (512, 384), 3: (896, 128), 2: (1024, 256)}

    A = [ps[:, 0:2, :], ps[:, 2:4, :]]
    X2 = [ps[:, 4, :], ps[:, 5, :]]
    Y, C = ps[:, 6, :], ps[:, 7, :]

    x_loaded, qk_moved, nm_moved = sem("x_loaded"), sem("qk_moved"), sem("nm_moved")
    init_done, mask_done = sem("init_done"), sem("mask_done")
    stats_chain, pool_chain, xn_ready = sem("stats_chain"), sem("pool_chain"), sem("xn_ready")
    xt_filled, xt_copied, ht_filled, ht_ready = sem("xt_filled"), sem("xt_copied"), sem("ht_filled"), sem("ht_ready")
    qk_filled, v_filled, v_copied = sem("qk_filled"), sem("v_filled"), sem("v_copied")
    full_ready, rest_ready, part1_ready, split_done = sem("full_ready"), sem("rest_ready"), sem("part1_ready"), sem("split_done")
    s1_filled, max_taken, s2_filled, exp_done = sem("s1_filled"), sem("max_taken"), sem("s2_filled"), sem("exp_done")
    vg_ready, pv_done, y_copied = sem("vg_ready"), sem("pv_done"), sem("y_copied")
    nm_chain, nm_filled, nm_copied = sem("nm_chain"), sem("nm_filled"), sem("nm_copied")
    yt_filled, rec_ready, yn_ready = sem("yt_filled"), sem("rec_ready"), sem("yn_ready")
    ynt_filled, ynt_ready, o_filled, x_done = sem("ynt_filled"), sem("ynt_ready"), sem("o_filled"), sem("x_done")

    INIT = 10
    RING = 2
    passed = sem("a_passed")
    QK_DMAS = 16 * (2 * SLOTS + 1)

    ORDER = [2, 2, 1, 2, 2, 1, 2, 2, 1, 2, 2, 1, 2, 2, 1, 1]
    UNITS1 = [(0, range(0, 4), 4), (1, range(0, 4), 2), (2, range(0, 2), 1), (2, range(2, 4), 1),
              (3, range(0, 2), 1), (3, range(2, 4), 1)]
    UNITS2 = []
    for h0 in (0, 2):
        for h in (h0, h0 + 1):
            UNITS2 += [[(h, 0, 0)], [(h, 1, 0), (h, 3, 384)]]
        UNITS2.append([(h0, 2, 0), (h0 + 1, 2, 256)])
    N1, N2 = len(UNITS1), len(UNITS2)

    def s1_banks(u):
        ib, heads, per = UNITS1[u]
        n = (ib + 1) * P
        banks = A[u % 2][:, 0:len(heads) // per, :]
        return banks[:, :, 0:n * per].rearrange("p k (h n) -> p k h n", h=per)

    with nc.Block() as block:
        @block.sync
        def _(sp):
            def load_x(b, par):
                if not isinstance(b, int) or b >= 2:
                    wait_apart(sp, xt_filled, b - 1, passed)
                    wait_apart(sp, xn_ready, b - 1, passed)
                wait(sp, x_loaded, 16 * b)
                sp.dma_start(x_in[par][:], a["L0_attn_x"][b].rearrange("(n p) f -> p n f", p=P)).then_inc(x_loaded, 16)

            def move_qk(b, par):
                wait_apart(sp, split_done, 2 * b + 2, passed)
                if not isinstance(b, int) or b >= 2:
                    wait_apart(sp, pv_done, NG * (b - 1), passed)
                else:
                    sp.wait_ge(init_done, INIT)
                wait(sp, qk_moved, QK_DMAS * b)
                for s in range(SLOTS):
                    rows = slice(DH * s, DH * (s + 1))
                    sp.dma_start(Qs[par][rows, :, :], part[:, 0, s // NPART, :]).then_inc(qk_moved, 16)
                    sp.dma_start(Ks[par][rows, :, :], part[:, 1, s % NPART, :]).then_inc(qk_moved, 16)
                sp.dma_start(Qs[par][MAX_ROW:MAX_ROW + NPART, :, :], zero48[:]).then_inc(qk_moved, 16)

            def move_nm(b, par):
                sp.wait_ge(nm_copied, b + 1)
                sp.dma_start(Qs[par][MAX_ROW:MAX_ROW + NPART, :, :], nmT[:]).then_inc(nm_moved, 16)

            load_x(0, 0)
            load_x(1, 1)
            move_qk(0, 0)
            move_qk(1, 1)
            move_nm(0, 0)
            with sp.Fori(0, B // 2 - 1) as i:
                for par in range(2):
                    b = 2 * i + par
                    load_x(b + 2, par)
                    move_nm(b + 1, 1 - par)
                    move_qk(b + 2, par)
            move_nm(B - 1, 1)

        @block.gpsimd
        def _(pool):
            pool.memset(mask_f[:], 0.0).then_inc(mask_done, 1)
            pool.wait_ge(mask_done, 1)
            pool.affine_select(out=mask_f[:], in_=mask_f[:], compare_op=ALU.is_ge, fill=NEG, base=0,
                               pattern=[[-1, P]], channel_multiplier=1).then_inc(mask_done, 1)
            pool.wait_ge(mask_done, 2)
            for h in range(HG):
                pool.tensor_copy(mask4[:, h, :], mask_f[:]).then_inc(mask_done, 1)
            pool.memset(xn[:, 0, :], 0.0).then_inc(mask_done, 1)
            pool.wait_ge(mask_done, 7)
            pool.affine_select(out=xn[:, 0, :], in_=xn[:, 0, :], compare_op=ALU.is_ge, fill=NEG, base=0,
                               pattern=[[1, P]], channel_multiplier=-1).then_inc(mask_done, 1)
            pool.wait_ge(mask_done, 8)
            for h in range(2):
                pool.tensor_copy(maskT[:, h, :], xn[:, 0, :]).then_inc(mask_done, 1)

            def rstd_of(b):
                wait_apart(pool, stats_chain, 2 * NB * (b + 1), passed)
                pool.tensor_scalar(rstd[:], mv[:, :, 1], EPS, None, ALU.add).then_inc(pool_chain, 1)
                pool.wait_ge(pool_chain, 2 * b + 1)
                pool.tensor_tensor(rstd[:], rstd[:], neghalf[:], ALU.pow).then_inc(pool_chain, 1)

            rstd_of(0)
            rstd_of(1)
            with pool.Fori(0, B // 2 - 1) as i:
                for par in range(2):
                    rstd_of(2 * i + par + 2)

        @block.tensor
        def _(pe):
            def project(b, par, first=False):
                pe.wait_ge(x_loaded, 16 * (b + 1))
                if not first:
                    pe.wait_ge(exp_done, NG * N2 * (b - 1) + RING)
                for n in range(NB):
                    last = pe.transpose(X2[1][:, n * P:(n + 1) * P], x_in[par][:, n, :], ident[:])
                last.then_inc(xt_filled, 1)
                pe.wait_ge(xn_ready, b + 1)
                for n in range(NB):
                    last = pe.transpose(A[0][:, 0, n * P:(n + 1) * P], xn[:, n, :], ident[:])
                last.then_inc(ht_filled, 1)

            def project2(b, par, first=False):
                pe.wait_ge(ht_ready, b + 1)
                pe.matmul(A[0][:, 1, :], WqP[:].rearrange("p d h -> p (d h)"), hT[:], start=True, stop=True)
                pe.matmul(A[1][:, 0, :], WkP[:].rearrange("p d h -> p (d h)"), hT[:],
                          start=True, stop=True).then_inc(qk_filled, 1)
                if not first:
                    pe.wait_ge(nm_copied, b)
                elif b > 0:
                    pe.wait_ge(v_copied, b)
                for n in range(NB):
                    last = pe.matmul(X2[0][:, n * P:(n + 1) * P], hT[:, n * P:(n + 1) * P], WvT[:],
                                     start=True, stop=True)
                last.then_inc(v_filled, 1)

            def unit1(b, g, par, u):
                ib, heads, per = UNITS1[u]
                n = (ib + 1) * P
                t = NG * b + g
                pe.wait_ge(max_taken, N1 * t + (u + 1))
                banks = s1_banks(u)
                for k in range(banks.shape[1]):
                    for j in range(per):
                        h = g * HG + heads[k * per + j]
                        pe.matmul(banks[:, k, j, :], Qs[par][:, h, ib * P:(ib + 1) * P], Ks[par][:, h, 0:n],
                                  start=(j == 0), stop=False, skip_group_check=True)
                    last = pe.matmul(banks[:, k, :, n - P:n], identb[:], mask4[:, 0:per, :],
                                     start=False, stop=True, skip_group_check=True)
                last.then_inc(s1_filled, 1)

            def unit2(b, g, par, u):
                t = NG * b + g
                pe.wait_ge(exp_done, N2 * t + (u + 1))
                bank = X2[u % 2]
                for k, (hh, jb, at) in enumerate(UNITS2[u]):
                    h = g * HG + hh
                    last = pe.matmul(bank[:, at:at + T - jb * P], Ks[par][:, h, jb * P:(jb + 1) * P],
                                     Qs[par][:, h, jb * P:T], start=(k == 0), stop=False, skip_group_check=True)
                ats = [at for _, _, at in UNITS2[u]]
                if len(ats) == 1:
                    last = pe.matmul(bank[:, 0:P], identb[:], maskT[:, 0, :], start=False, stop=True,
                                     skip_group_check=True)
                elif ats[1] == 256:
                    last = pe.matmul(bank.rearrange("p (k n) -> p k n", k=2)[:, :, 0:P], identb[:], maskT[:],
                                     start=False, stop=True, skip_group_check=True)
                else:
                    last = pe.matmul(bank.rearrange("p (k n) -> p k n", k=4)[:, 0:4:3, :], identb[:], maskT[:],
                                     start=False, stop=True, skip_group_check=True)
                last.then_inc(s2_filled, 1)

            def pv(b, g):
                t = NG * b + g
                pe.wait_ge(vg_ready, t + 1)
                pe.wait_ge(exp_done, N2 * (t + 1) + RING)
                pe.wait_ge(y_copied, t + 1)
                pe.wait_ge(x_done, b + 1)
                for jb in range(NB):
                    at, n = SEG[jb]
                    for hh in range(HG):
                        last = pe.matmul(Y[32 * hh:32 * hh + 32, jb * P:T], Vg[:, jb, hh, :], PR[:, hh, at:at + n],
                                         start=(jb == 0), stop=(jb == NB - 1), skip_group_check=True)
                last.then_inc(pv_done, 1)

            def groups(b, par, with1, with2):
                if with2:
                    wait_apart(pe, nm_moved, 16 * (b + 1), passed)
                if with1:
                    wait_apart(pe, qk_moved, QK_DMAS * (b + 2), passed)
                with pe.Fori(0, NG) as g:
                    u1 = u2 = 0
                    for kind in ORDER:
                        if kind == 1:
                            if with1:
                                unit1(b + 1, g, 1 - par, u1)
                            u1 += 1
                        else:
                            if with2:
                                unit2(b, g, par, u2)
                            u2 += 1
                    if with2:
                        pv(b, g)

            def turn_maxima(b, par):
                pe.wait_ge(nm_chain, 4 * (b + 1))
                if not isinstance(b, int) or b > 0:
                    pe.wait_ge(exp_done, NG * N2 * b + RING)
                bank = X2[0].bitcast(BF16)
                for n in range(NB):
                    last = pe.transpose(bank[:, n * P:(n + 1) * P], npart_wide[:, n, :], identb[:])
                last.then_inc(nm_filled, 1)

            def turn_y(b):
                pe.wait_ge(y_copied, NG * (b + 1) + 1)
                last_one = isinstance(b, int) and b == B - 1
                pe.wait_ge(max_taken, NG * N1 * (B if last_one else b + 2) + RING)
                for g in range(NG):
                    for n in range(NB):
                        last = pe.transpose(ps[:, g, n * P:(n + 1) * P], yT[:, g, n * P:(n + 1) * P], ident[:])
                last.then_inc(yt_filled, 1)

            def output(b):
                pe.wait_ge(yn_ready, NB * (b + 1))
                for n in range(NB):
                    last = pe.transpose(C[:, n * P:(n + 1) * P], yn[:, n, :, :].rearrange("p h d -> p (h d)"), ident[:])
                last.then_inc(ynt_filled, 1)

            def output2(b):
                pe.wait_ge(ynt_ready, b + 1)
                pe.matmul(Y, WoT[:], ynT[:], start=True, stop=True).then_inc(o_filled, 1)

            pe.wait_ge(mask_done, 10)
            pe.wait_ge(init_done, INIT)
            project(0, 0, True)
            project2(0, 0, True)
            pe.wait_ge(xt_copied, 1)
            pe.wait_ge(full_ready, 4)
            project(1, 1, True)
            project2(1, 1, True)
            pe.wait_ge(full_ready, 8)
            pe.wait_ge(v_copied, 2)
            pe.wait_ge(xt_copied, 2)
            groups(-1, 1, True, False)
            turn_maxima(0, 0)

            def sequence(b, par, nxt, nxt2):
                groups(b, par, nxt, True)
                if nxt:
                    turn_maxima(b + 1, 1 - par)
                turn_y(b)
                output(b)
                if nxt2:
                    project(b + 2, par)
                output2(b)
                if nxt2:
                    project2(b + 2, par)
                    pe.wait_ge(full_ready, 4 * (b + 3))
                    pe.wait_ge(v_copied, b + 3)
                    pe.wait_ge(xt_copied, b + 3)

            with pe.Fori(0, B // 2 - 1) as i:
                for par in range(2):
                    sequence(2 * i + par, par, True, True)
            sequence(B - 2, 0, True, False)
            pe.wait_ge(nm_copied, B)
            sequence(B - 1, 1, False, False)


        @block.scalar
        def _(act):
            act.sem_inc(exp_done, RING)
            act.sem_inc(y_copied, 1)

            def one(b):
                return slice(b, b + 1) if isinstance(b, int) else bass.ds(b, 1)

            def copy_x(b):
                act.wait_ge(xt_filled, b + 1)
                act.activation(xT[:, b, :], X2[1], ACT.Identity, bias=gab[:, one(b)]).then_inc(xt_copied, 1)

            def copy_h(b):
                act.wait_ge(ht_filled, b + 1)
                wait(act, v_filled, b)
                act.activation(hT[:], A[0][:, 0, :], ACT.Identity, bias=mod[:, SHIFT, one(b)],
                               scale=mod[:, SCALE1, one(b)]).then_inc(ht_ready, 1)

            def split(b):
                act.wait_ge(qk_filled, b + 1)
                wait(act, qk_moved, QK_DMAS * b)
                for k, (bank, bias) in enumerate(((A[0][:, 1, :], "bqP"), (A[1][:, 0, :], "bkP"))):
                    act.activation(full[:, k, :], bank, ACT.Identity, bias=col(bias)).then_inc(full_ready, 1)
                    act.activation(part[:, k, 0, :], bank, ACT.Identity, bias=col(bias)).then_inc(full_ready, 1)
                for k in range(2):
                    act.wait_ge(rest_ready, 2 * b + k + 1)
                    act.activation(part[:, k, 1, :], rest[:, k, :], ACT.Copy).then_inc(part1_ready, 1)

            def groups(b, par):
                with act.Fori(0, NG) as g:
                    t = NG * b + g
                    act.activation(Vg[:, :, :, 0:DH],
                                   V[par][:, :, bass.ds(g * (HG * DH), HG * DH)].rearrange("p n (h d) -> p n h d", h=HG),
                                   ACT.Copy).then_inc(vg_ready, 1)
                    for u in range(N2):
                        act.wait_ge(s2_filled, N2 * t + u + 1)
                        bank, todo = X2[u % 2], UNITS2[u]
                        h, jb, _ = todo[0]
                        if jb == 2:
                            dst = PR[:, h:h + 2, SEG[2][0]:1280]
                            src = bank.rearrange("p (k n) -> p k n", k=2)
                        else:
                            dst, src = PR[:, h, SEG[jb][0]:SEG[jb][0] + 512], bank
                        act.activation(dst, src, ACT.Exp).then_inc(exp_done, 1)
                    act.wait_ge(pv_done, t + 1)
                    act.activation(yT[:, g, :], Y, ACT.Copy).then_inc(y_copied, 1)

            def copy_maxima(b):
                act.wait_ge(nm_filled, b + 1)
                wait(act, nm_moved, 16 * b)
                act.activation(nmT[:], X2[0].bitcast(BF16)[0:NPART * H, 0:T], ACT.Copy).then_inc(nm_copied, 1)

            def copy_y(b):
                act.wait_ge(ynt_filled, b + 1)
                act.activation(ynT[:], C, ACT.Copy).then_inc(ynt_ready, 1)

            act.wait_ge(init_done, INIT)
            for b in range(2):
                copy_x(b)
                copy_h(b)
                split(b)
                act.wait_ge(v_copied, b + 1)
            copy_maxima(0)

            def sequence(b, par, nxt, nxt2):
                act.wait_ge(v_copied, b + 1)
                groups(b, par)
                if nxt:
                    copy_maxima(b + 1)
                copy_y(b)
                if nxt2:
                    copy_x(b + 2)
                    copy_h(b + 2)
                    split(b + 2)

            with act.Fori(0, B // 2 - 1) as i:
                for par in range(2):
                    sequence(2 * i + par, par, True, True)
            sequence(B - 2, 0, True, False)
            sequence(B - 1, 1, False, False)

        @block.vector
        def _(dve):
            dve.sem_inc(max_taken, RING)
            dve.sem_inc(x_done, 1)
            for p in range(2):
                dve.memset(Qs[p][:].rearrange("p h t -> p (h t)").bitcast(mybir.dt.uint32), 0).then_inc(init_done, 1)
                dve.memset(Ks[p][:].rearrange("p h t -> p (h t)").bitcast(mybir.dt.uint32), 0).then_inc(init_done, 1)
            dve.memset(zero48[:], 0.0).then_inc(init_done, 1)
            dve.memset(Vg[:], 0.0).then_inc(init_done, 1)
            dve.memset(npart_wide[:], 0.0).then_inc(init_done, 1)
            dve.wait_ge(init_done, 7)
            for p in range(2):
                dve.memset(Ks[p][MAX_ROW:MAX_ROW + NPART, :, :], 1.0).then_inc(init_done, 1)
            dve.memset(Vg[:, :, :, DH:DH + 1], 1.0).then_inc(init_done, 1)

            def norm_stats(b, par):
                dve.wait_ge(x_loaded, 16 * (b + 1))
                for n in range(NB):
                    dve.bn_stats(stats[:, n, :], x_in[par][:, n, :]).then_inc(stats_chain, 1)
                dve.wait_ge(stats_chain, 2 * NB * b + NB)
                wait(dve, pool_chain, 2 * b)
                wait_apart(dve, xn_ready, b, passed)
                for n in range(NB):
                    dve.bn_aggr(mv[:, n, :], stats[:, n, :]).then_inc(stats_chain, 1)

            def normalize(b, par):
                dve.wait_ge(pool_chain, 2 * b + 2)
                dve.wait_ge(stats_chain, 2 * NB * (b + 1))
                wait(dve, ht_filled, b)
                for n in range(NB):
                    last = dve.tensor_scalar(xn[:, n, :], x_in[par][:, n, :], mv[:, n, 0:1], rstd[:, n:n + 1],
                                             ALU.subtract, ALU.mult)
                last.then_inc(xn_ready, 1)

            def split(b, par):
                for k in range(2):
                    dve.wait_ge(full_ready, 4 * b + 2 * k + 2)
                    wait(dve, split_done, 2 * b)
                    dve.tensor_tensor(rest[:, k, :], full[:, k, :], part[:, k, 0, :], ALU.subtract).then_inc(rest_ready, 1)
                dve.wait_ge(v_filled, b + 1)
                if not isinstance(b, int) or b >= 2:
                    dve.wait_ge(vg_ready, NG * (b - 1))
                dve.tensor_copy(V[par][:].rearrange("p n f -> p (n f)"), X2[0]).then_inc(v_copied, 1)
                for k in range(2):
                    dve.wait_ge(part1_ready, 2 * b + k + 1)
                    dve.tensor_tensor(part[:, k, 2, :], rest[:, k, :], part[:, k, 1, :], ALU.subtract).then_inc(split_done, 1)

            def maxima(b, par):
                with dve.Fori(0, NG) as g:
                    for u, (ib, heads, per) in enumerate(UNITS1):
                        t = NG * b + g
                        dve.wait_ge(s1_filled, N1 * t + u + 1)
                        banks = s1_banks(u)
                        dst = nmax[par][:, ib, bass.ds(g * HG + heads[0], len(heads))]
                        if per > 1:
                            dst = dst.rearrange("p (k h) -> p k h", h=per)
                            if banks.shape[1] == 1:
                                dst, banks = dst[:, 0, :], banks[:, 0, :, :]
                        else:
                            banks = banks[:, :, 0, :]
                        dve.tensor_reduce(dst, banks, AX_X, ALU.max, negate=True).then_inc(max_taken, 1)

            def split_maxima(b, par):
                dve.wait_ge(max_taken, NG * N1 * (b + 1) + RING)
                wait(dve, nm_filled, b)
                dve.tensor_copy(npart[:, :, 0, :], nmax[par][:]).then_inc(nm_chain, 1)
                dve.wait_ge(nm_chain, 4 * b + 1)
                dve.tensor_tensor(nrest[:], nmax[par][:], npart[:, :, 0, :], ALU.subtract).then_inc(nm_chain, 1)
                dve.wait_ge(nm_chain, 4 * b + 2)
                dve.tensor_copy(npart[:, :, 1, :], nrest[:]).then_inc(nm_chain, 1)
                dve.wait_ge(nm_chain, 4 * b + 3)
                dve.tensor_tensor(npart[:, :, 2, :], nrest[:], npart[:, :, 1, :], ALU.subtract).then_inc(nm_chain, 1)

            def divide(b):
                dve.wait_ge(yt_filled, b + 1)
                turned = ps[:, 0:NG, :].rearrange("p g (n h r) -> p g n h r", n=NB, h=HG)
                wait(dve, yn_ready, NB * b)
                for g in range(NG):
                    dve.reciprocal(rec[:, g, :, :], turned[:, g, :, :, DH]).then_inc(rec_ready, 1)
                dve.wait_ge(rec_ready, NG * (b + 1))
                wait(dve, ynt_filled, b)
                for n in range(NB):
                    dve.tensor_tensor(yn[:, n, :, :].rearrange("p (g h) d -> p g h d", g=NG), turned[:, :, n, :, 0:DH],
                                      rec[:, :, n, :].unsqueeze(3).to_broadcast([P, NG, HG, DH]),
                                      ALU.mult).then_inc(yn_ready, 1)

            def add_output(b):
                dve.wait_ge(o_filled, b + 1)
                one = slice(b, b + 1) if isinstance(b, int) else bass.ds(b, 1)
                dve.scalar_tensor_tensor(xT[:, b, :], Y, mod[:, GATE, one], xT[:, b, :],
                                         ALU.mult, ALU.add).then_inc(x_done, 1)

            for b in range(2):
                norm_stats(b, b)
                normalize(b, b)
                split(b, b)
            maxima(0, 0)
            split_maxima(0, 0)

            def sequence(b, par, nxt, nxt2):
                if nxt:
                    maxima(b + 1, 1 - par)
                    split_maxima(b + 1, 1 - par)
                if nxt2:
                    norm_stats(b + 2, par)
                divide(b)
                if nxt2:
                    normalize(b + 2, par)
                add_output(b)
                if nxt2:
                    split(b + 2, par)

            with dve.Fori(0, B // 2 - 1) as i:
                for par in range(2):
                    sequence(2 * i + par, par, True, True)
            sequence(B - 2, 0, True, False)
            sequence(B - 1, 1, False, False)


def moe(nc, sb, sem, ps, xT, ident, identb, neghalf, mod, col, gate_w, up_w, down_w, shg_w, shu_w, shd_w,
        router_w):
    ITEMS = E + 1
    FIRST = 3

    xc = [sb(f"xc{p}", [D, T]) for p in range(2)]
    hT = [sb(f"hTm{p}", [D, T]) for p in range(2)]
    nT = [sb(f"nTm{p}", [D, T]) for p in range(2)]
    xn = sb("xnm", [P, NB, D])
    stats, mv, rstd = sb("stats_m", [P, NB, 6]), sb("mv_m", [P, NB, 2]), sb("rstd_m", [P, NB])
    prio = sb("prio", [P, NB, E])
    prio_i = sb("prio_i", [P, NB, E], mybir.dt.int32)
    top = sb("top", [P, NB])
    equal = sb("equal", [P, NB, E])
    topkey = sb("topkey", [P, NB])
    th_top = sb("th_top", [P, NB])
    score = sb("score", [P, NB])
    wsc = sb("wsc", [P, NB, E])
    wrest = sb("wrest", [P, NB, E])
    wpart_wide = sb("wpart", [P, NB, P], BF16)
    wpart = wpart_wide[:, :, 0:NPART * E].rearrange("p n (k e) -> p n k e", k=NPART)
    wT = [sb(f"wT{p}", [P, T], BF16) for p in range(2)]
    sel = sb("sel", [P, E, P], BF16)
    xe = [sb(f"xe{p}", [D, T]) for p in range(2)]
    th = [sb(f"thm{c}", [P, T]) for c in range(HC)]
    sil = [sb(f"sil{c}", [P, T]) for c in range(HC)]
    hid = [sb(f"hid{p}", [P, HC, T]) for p in range(2)]
    total = sb("total", [D, T])

    G, U = [ps[:, 0, :], ps[:, 1, :]], [ps[:, 2, :], ps[:, 3, :]]
    OUT, BC, PA, PB = ps[:, 4, :], ps[:, 5, :], ps[:, 6, :], ps[:, 7, :]

    sel_done, xc_ready, turned, stats_chain = sem("m_sel_done"), sem("m_xc_ready"), sem("m_turned"), sem("m_stats")
    rstd_chain, xn_ready, affine_done = sem("m_rstd"), sem("m_xn_ready"), sem("m_affine")
    logits_filled, score_chain, th_ready = sem("m_logits"), sem("m_score"), sem("m_th")
    w_turned, w_ready, bc_filled, xe_ready = sem("m_w_turned"), sem("m_w_ready"), sem("m_bc"), sem("m_xe")
    gu_filled, tanh_ready, silu_ready, hid_ready = sem("m_gu"), sem("m_tanh"), sem("m_silu"), sem("m_hid")
    out_filled, total_ready, x_done = sem("m_out"), sem("m_total"), sem("m_x_done")
    down_done = sem("m_down")
    passed = sem("m_passed")
    SCORE = 11
    SEL = 6 + NPART

    def one(b):
        return slice(b, b + 1) if isinstance(b, int) else bass.ds(b, 1)

    with nc.Block() as block:
        @block.gpsimd
        def _(pool):
            pool.iota(prio_i[:], pattern=[[0, NB], [-1, E]], base=E, channel_multiplier=0).then_inc(sel_done, 1)
            pool.memset(wT[0][:], 0.0).then_inc(sel_done, 1)
            pool.memset(wT[1][:], 0.0).then_inc(sel_done, 1)
            pool.memset(wpart_wide[:], 0.0).then_inc(sel_done, 1)
            pool.memset(sel[:], 0.0).then_inc(sel_done, 1)
            pool.wait_ge(sel_done, 5)
            pool.tensor_copy(prio[:], prio_i[:]).then_inc(sel_done, 1)
            for k in range(NPART):
                pool.affine_select(out=sel[:], in_=sel[:], compare_op=ALU.not_equal, fill=1.0, base=-k * E,
                                   pattern=[[-1, E], [0, P]], channel_multiplier=1).then_inc(sel_done, 1)
                pool.wait_ge(sel_done, 7 + k)

            def rstd_of(b, k):
                n = 2 * b + k
                pool.wait_ge(stats_chain, 2 * NB * (n + 1))
                if not (isinstance(n, int) and n == 0):
                    wait_apart(pool, xn_ready, n, passed)
                pool.tensor_scalar(rstd[:], mv[:, :, 1], EPS, None, ALU.add).then_inc(rstd_chain, 1)
                pool.wait_ge(rstd_chain, 2 * n + 1)
                pool.tensor_tensor(rstd[:], rstd[:], neghalf[:], ALU.pow).then_inc(rstd_chain, 1)

            rstd_of(0, 0)
            rstd_of(0, 1)
            with pool.Fori(1, B) as b:
                rstd_of(b, 0)
                rstd_of(b, 1)

        @block.tensor
        def _(pe):
            pe.wait_ge(sel_done, SEL)

            def turn(dst, src):
                for n in range(NB):
                    last = pe.transpose(dst[:, n * P:(n + 1) * P], src(n), ident[:])
                last.then_inc(turned, 1)

            def prepare(slot, b, par):
                cols = lambda n: slice(n * P, (n + 1) * P)
                if slot == 0:
                    pe.wait_ge(xc_ready, b + 1)
                    wait(pe, score_chain, SCORE * b)
                    turn(PA, lambda n: xc[par][:, cols(n)])
                elif slot == 2:
                    pe.wait_ge(xn_ready, 2 * b + 1)
                    wait(pe, w_ready, b)
                    turn(PB, lambda n: xn[:, n, :])
                elif slot == 3:
                    pe.wait_ge(affine_done, 2 * b + 1)
                    turn(PA, lambda n: hT[par][:, cols(n)])
                elif slot == 5:
                    pe.wait_ge(xn_ready, 2 * b + 2)
                    turn(PB, lambda n: xn[:, n, :])
                elif slot == 6:
                    pe.wait_ge(affine_done, 2 * b + 2)
                    for n in range(NB):
                        last = pe.matmul(PA[:, n * E:(n + 1) * E], nT[par][:, cols(n)], router_w[:],
                                         start=True, stop=True)
                    last.then_inc(logits_filled, 1)
                elif slot == 8:
                    pe.wait_ge(score_chain, SCORE * (b + 1))
                    bank = PB.bitcast(BF16)
                    for n in range(NB):
                        last = pe.transpose(bank[:, cols(n)], wpart_wide[:, n, :], identb[:])
                    last.then_inc(w_turned, 1)

            def spread(b, par, k):
                if k == 1:
                    pe.wait_ge(w_ready, b + 1)
                n = E * b + k - 1
                wait(pe, xe_ready, n)
                pe.matmul(BC, sel[:, k - 1, :], wT[par][:], start=True, stop=True).then_inc(bc_filled, 1)

            def up(b, par, k):
                src = nT[par] if k == 0 else xe[k % 2]
                if k > 0:
                    pe.wait_ge(xe_ready, E * b + k)
                n = ITEMS * b + k
                for c in range(HC):
                    wait(pe, hid_ready, HC * n + c - 1 if isinstance(n, int) else HC * n + (c - 1))
                    wg = shg_w[:, c * P:(c + 1) * P] if k == 0 else gate_w[:, k - 1, c * P:(c + 1) * P]
                    wu = shu_w[:, c * P:(c + 1) * P] if k == 0 else up_w[:, k - 1, c * P:(c + 1) * P]
                    pe.matmul(G[c], wg, src[:], start=True, stop=True)
                    pe.matmul(U[c], wu, src[:], start=True, stop=True).then_inc(gu_filled, 1)

            def down(b, k):
                n = ITEMS * b + k
                if k == 0:
                    wait(pe, total_ready, b)
                for c in range(HC):
                    pe.wait_ge(hid_ready, HC * n + c + 1)
                    w = shd_w[:, c, :] if k == 0 else down_w[:, k - 1, c, :]
                    last = pe.matmul(OUT, w, hid[k % 2][:, c, :], start=(k == 0 and c == 0),
                                     stop=(k == ITEMS - 1 and c == HC - 1), skip_group_check=True)
                last.then_inc(down_done, 1)

            def sequence(b, par, nxt):
                spread(b, par, 1)
                for k in range(ITEMS):
                    up(b, par, k)
                    if k + 2 < ITEMS:
                        spread(b, par, k + 2)
                    if k > 0:
                        down(b, k - 1)
                    if nxt:
                        prepare(k, b + 1, 1 - par)
                down(b, ITEMS - 1)

            for slot in range(ITEMS):
                prepare(slot, 0, 0)
            sequence(0, 0, True)
            with pe.Fori(0, B // 2 - 1) as i:
                for q in range(2):
                    sequence(2 * i + 1 + q, 1 - q, True)
            sequence(B - 1, 1, False)

        @block.scalar
        def _(act):
            def prepare(slot, b, par):
                if slot == 0:
                    if not isinstance(b, int) or b >= 2:
                        act.wait_ge(x_done, b - 1)
                    act.activation(xc[par][:], xT[:, b, :], ACT.Copy).then_inc(xc_ready, 1)
                elif slot == 2:
                    act.wait_ge(turned, 4 * b + 2)
                    act.activation(hT[par][:], PB, ACT.Identity, bias=mod[:, FIRST + SHIFT, one(b)],
                                   scale=mod[:, FIRST + SCALE1, one(b)]).then_inc(affine_done, 1)
                elif slot == 5:
                    act.wait_ge(turned, 4 * b + 4)
                    act.activation(nT[par][:], PB, ACT.Identity, bias=col("ln_b"), scale=col("ln_w")).then_inc(affine_done, 1)
                elif slot == 6:
                    act.wait_ge(score_chain, SCORE * b + 1)
                    act.activation(th_top[:], top[:], ACT.Tanh, scale=0.5).then_inc(th_ready, 1)
                elif slot == 8:
                    act.wait_ge(w_turned, b + 1)
                    act.activation(wT[par][0:NPART * E, :], PB.bitcast(BF16)[0:NPART * E, 0:T],
                                   ACT.Copy).then_inc(w_ready, 1)

            def item(b, k):
                n = ITEMS * b + k
                for c in range(HC):
                    act.wait_ge(gu_filled, HC * n + c + 1)
                    wait(act, silu_ready, HC * n + c - 1 if isinstance(n, int) else HC * n + (c - 1))
                    act.activation(th[c][:], G[c], ACT.Tanh, scale=0.5).then_inc(tanh_ready, 1)

            def sequence(b, par, nxt):
                for k in range(ITEMS):
                    item(b, k)
                    if nxt:
                        prepare(k, b + 1, 1 - par)

            for slot in range(ITEMS):
                prepare(slot, 0, 0)
            sequence(0, 0, True)
            with act.Fori(0, B // 2 - 1) as i:
                for q in range(2):
                    sequence(2 * i + 1 + q, 1 - q, True)
            sequence(B - 1, 1, False)

        @block.vector
        def _(dve):
            def link(ins, b, step):
                ins.then_inc(score_chain, 1)
                dve.wait_ge(score_chain, SCORE * b + step)

            def norm_stats(b, k):
                n = 2 * b + k
                dve.wait_ge(turned, 4 * b + 2 * k + 1)
                for m in range(NB):
                    dve.bn_stats(stats[:, m, :], PA[:, m * P:(m + 1) * P]).then_inc(stats_chain, 1)
                dve.wait_ge(stats_chain, 2 * NB * n + NB)
                wait(dve, rstd_chain, 2 * n)
                wait_apart(dve, xn_ready, n, passed)
                for m in range(NB):
                    dve.bn_aggr(mv[:, m, :], stats[:, m, :]).then_inc(stats_chain, 1)

            def normalize(b, k):
                n = 2 * b + k
                dve.wait_ge(rstd_chain, 2 * n + 2)
                dve.wait_ge(stats_chain, 2 * NB * (n + 1))
                wait(dve, turned, 4 * b + 2 * k)
                for m in range(NB):
                    last = dve.tensor_scalar(xn[:, m, :], PA[:, m * P:(m + 1) * P], mv[:, m, 0:1], rstd[:, m:m + 1],
                                             ALU.subtract, ALU.mult)
                last.then_inc(xn_ready, 1)

            def prepare(slot, b, par):
                if slot in (0, 3):
                    norm_stats(b, slot // 3)
                elif slot in (1, 4):
                    normalize(b, slot // 3)
                elif slot == 6:
                    dve.wait_ge(logits_filled, b + 1)
                    wait(dve, w_turned, b)
                    logits = PA[:, 0:NB * E].rearrange("p (n e) -> p n e", n=NB)
                    wide = lambda x: x[:].unsqueeze(2).to_broadcast([P, NB, E])
                    link(dve.tensor_reduce(top[:], logits, AX_X, ALU.max), b, 1)
                    link(dve.tensor_tensor(equal[:], logits, wide(top), ALU.is_equal), b, 2)
                    link(dve.tensor_tensor(equal[:], equal[:], prio[:], ALU.mult), b, 3)
                    link(dve.tensor_reduce(topkey[:], equal[:], AX_X, ALU.max), b, 4)
                    link(dve.tensor_tensor(equal[:], equal[:], wide(topkey), ALU.is_equal), b, 5)
                    dve.wait_ge(th_ready, b + 1)
                    link(dve.tensor_scalar(score[:], th_top[:], 0.5, 0.5, ALU.mult, ALU.add), b, 6)
                    link(dve.tensor_tensor(wsc[:], equal[:], wide(score), ALU.mult), b, 7)
                    link(dve.tensor_copy(wpart[:, :, 0, :], wsc[:]), b, 8)
                    link(dve.tensor_tensor(wrest[:], wsc[:], wpart[:, :, 0, :], ALU.subtract), b, 9)
                    link(dve.tensor_copy(wpart[:, :, 1, :], wrest[:]), b, 10)
                    link(dve.tensor_tensor(wpart[:, :, 2, :], wrest[:], wpart[:, :, 1, :], ALU.subtract), b, 11)

            def mask_input(b, par, k):
                n = E * b + k - 1
                dve.wait_ge(bc_filled, n + 1)
                m = ITEMS * b + k - 1
                wait(dve, gu_filled, HC * m)
                dve.tensor_tensor(xe[k % 2][:], nT[par][:], BC, ALU.mult).then_inc(xe_ready, 1)

            def item(b, k):
                n = ITEMS * b + k
                for c in range(HC):
                    dve.wait_ge(tanh_ready, HC * n + c + 1)
                    dve.scalar_tensor_tensor(sil[c][:], th[c][:], 1.0, G[c], ALU.add, ALU.mult).then_inc(silu_ready, 1)
                    dve.wait_ge(silu_ready, HC * n + c + 1)
                    wait(dve, down_done, n if k == 0 else n - 1)
                    dve.scalar_tensor_tensor(hid[k % 2][:, c, :], sil[c][:], 0.5, U[c], ALU.mult,
                                             ALU.mult).then_inc(hid_ready, 1)

            def finish(b, par):
                dve.wait_ge(down_done, ITEMS * (b + 1))
                wait(dve, x_done, b)
                dve.tensor_tensor(total[:], hT[par][:], OUT, ALU.add).then_inc(total_ready, 1)
                dve.wait_ge(total_ready, b + 1)
                dve.scalar_tensor_tensor(xT[:, b, :], total[:], mod[:, FIRST + GATE, one(b)], xc[par][:],
                                         ALU.mult, ALU.add).then_inc(x_done, 1)

            def sequence(b, par, nxt):
                mask_input(b, par, 1)
                for k in range(ITEMS):
                    item(b, k)
                    if k + 2 < ITEMS:
                        mask_input(b, par, k + 2)
                    if nxt:
                        prepare(k, b + 1, 1 - par)
                finish(b, par)

            dve.wait_ge(sel_done, SEL)
            for slot in range(ITEMS):
                prepare(slot, 0, 0)
            sequence(0, 0, True)
            with dve.Fori(0, B // 2 - 1) as i:
                for q in range(2):
                    sequence(2 * i + 1 + q, 1 - q, True)
            sequence(B - 1, 1, False)


def mixing(nc, out, sb, sem, ps, xT, ident, neghalf, mod, col, Wmix, WoR, Win2, Wc, w1p, b1p):
    xc = sb("xc_t", [D, T])
    hp = sb("hp", [D, T + 1])
    xm = [sb(f"xm{p}", [D, T]) for p in range(2)]
    xn = [sb(f"xnt{k}", [P, NB, D]) for k in range(2)]
    stats = [sb(f"stats_t{k}", [P, NB, 6]) for k in range(2)]
    mv = [sb(f"mv_t{k}", [P, NB, 2]) for k in range(2)]
    rstd = [sb(f"rstd_t{k}", [P, NB]) for k in range(2)]
    ones = sb("ones_t", [D, T])
    tdB = sb("tdB", [D, T])
    mx = sb("mx", [D, T + 1])
    num = sb("num", [D, T + 1])
    den = sb("den", [D, T + 1])
    arg = sb("arg", [D, 4, T])
    ex = sb("ex", [D, 4, T])
    mo = sb("mo", [D, T])
    e2v = sb("e2v", [D, T])
    n1, n2 = sb("n1", [D, T]), sb("n2", [D, T])
    d1 = sb("d1", [D, T])
    numer, denom, recd = sb("numer", [D, T]), sb("denom", [D, T]), sb("recd", [D, T])
    thr = sb("thr", [D, T])
    ry, y = sb("ry", [D, T]), sb("y_t", [D, T])
    h2 = sb("h2", [D, T])
    s = sb("s_mlp", [P, T])
    RR = 4
    r = [sb(f"relu{k}", [P, T]) for k in range(RR)]
    mlp = sb("mlp", [D, T])
    xo = sb("xo", [D, T])
    y_out = [sb(f"y_out{p}", [P, NB, D]) for p in range(2)]

    PA, PB, K, V, R, S, O, O2 = (ps[:, k, :] for k in range(8))

    init_done, xc_ready = sem("t_init"), sem("t_xc")
    turned = [sem(f"t_turned{k}") for k in range(2)]
    stats_chain = [sem(f"t_stats{k}") for k in range(2)]
    rstd_chain = [sem(f"t_rstd{k}") for k in range(2)]
    xn_ready = [sem(f"t_xn{k}") for k in range(2)]
    h_ready = [sem(f"t_h{k}") for k in range(2)]
    kvr_filled, th_ready, scan_chain, ex_ready = sem("t_kvr"), sem("t_thr"), sem("t_chain"), sem("t_ex")
    pool_done, y_ready, o_filled, xm_ready = sem("t_pool"), sem("t_y"), sem("t_o"), sem("t_xm")
    s_filled, s_ready, relu_ready, relu_used = sem("t_s_filled"), sem("t_s"), sem("t_relu"), sem("t_relu_used")
    mlp_chain, xo_turned, yo_ready, stored = sem("t_mlp"), sem("t_xo_turned"), sem("t_yo"), sem("t_stored")
    passed = sem("t_passed")
    CH = 13

    def one(b):
        return slice(b, b + 1) if isinstance(b, int) else bass.ds(b, 1)

    def steps(eng, step):
        step(0, 0, True, False)
        step(1, 1, True, True)
        with eng.Fori(0, B // 2 - 1) as i:
            for q in range(2):
                step(2 * i + 2 + q, q, True, True)
        step(B, 0, False, True)

    with nc.Block() as block:
        @block.sync
        def _(sp):
            def store(b, par):
                wait(sp, stored, 16 * b) if isinstance(b, int) else wait_apart(sp, stored, 16 * b, passed)
                sp.wait_ge(yo_ready, b + 1)
                sp.dma_start(out[b].rearrange("(n p) f -> p n f", p=P), y_out[par][:]).then_inc(stored, 16)

            steps(sp, lambda b, par, mix, mlp: store(b - 1, 1 - par) if mlp else None)
            sp.wait_ge(stored, 16 * B)

        @block.gpsimd
        def _(pool):
            pool.memset(hp[:, 0:1], 0.0).then_inc(init_done, 1)
            pool.memset(mx[:, 0:1], TINY_MX).then_inc(init_done, 1)
            pool.memset(num[:, 0:1], 0.0).then_inc(init_done, 1)
            pool.memset(den[:, 0:1], 0.0).then_inc(init_done, 1)

            def rstd_of(k, b):
                pool.wait_ge(stats_chain[k], 2 * NB * (b + 1))
                wait_apart(pool, xn_ready[k], b, passed)
                pool.tensor_scalar(rstd[k][:], mv[k][:, :, 1], EPS, None, ALU.add).then_inc(rstd_chain[k], 1)
                pool.wait_ge(rstd_chain[k], 2 * b + 1)
                pool.tensor_tensor(rstd[k][:], rstd[k][:], neghalf[:], ALU.pow).then_inc(rstd_chain[k], 1)

            def step(b, par, mix, mlp):
                if mix:
                    rstd_of(0, b)
                if mlp:
                    rstd_of(1, b - 1)
                if mix:
                    pool.wait_ge(scan_chain, CH * b + 4)
                    pool.tensor_tensor(arg[:, 2, :], mx[:, 0:T], mo[:], ALU.subtract).then_inc(pool_done, 1)
                    pool.wait_ge(ex_ready, 2 * b + 2)
                    pool.wait_ge(scan_chain, CH * b + 7)
                    pool.tensor_tensor(n1[:], ex[:, 2, :], num[:, 0:T], ALU.mult).then_inc(pool_done, 1)
                    pool.wait_ge(scan_chain, CH * b + 8)
                    pool.tensor_tensor(d1[:], ex[:, 2, :], den[:, 0:T], ALU.mult).then_inc(pool_done, 1)

            steps(pool, step)

        @block.tensor
        def _(pe):
            def turn(bank, src, signal):
                for n in range(NB):
                    last = pe.transpose(bank[:, n * P:(n + 1) * P], src(n), ident[:])
                last.then_inc(signal, 1)

            def cols(n):
                return slice(n * P, (n + 1) * P)

            def step(b, par, mix, mlp):
                old = 1 - par
                if mix:
                    pe.wait_ge(xc_ready, b + 1)
                    wait(pe, h_ready[1], b - 1)
                    turn(PA, lambda n: xc[:, cols(n)], turned[0])
                    pe.wait_ge(xn_ready[0], b + 1)
                    turn(PB, lambda n: xn[0][:, n, :], turned[0])
                if mlp:
                    pe.wait_ge(xm_ready, b)
                    if mix:
                        pe.wait_ge(xn_ready[0], b + 1)
                    turn(PA, lambda n: xm[old][:, cols(n)], turned[1])
                if mix:
                    pe.wait_ge(h_ready[0], b + 1)
                    wait(pe, y_ready, b)
                    for k, bank in enumerate((K, V, R)):
                        pe.matmul(bank, Wmix[:, 2 * k, :], hp[:, 1:T + 1], start=True, stop=False)
                        pe.matmul(bank, Wmix[:, 2 * k + 1, :], hp[:, 0:T], start=False, stop=True).then_inc(kvr_filled, 1)
                if mlp:
                    pe.wait_ge(xn_ready[1], b)
                    turn(PB, lambda n: xn[1][:, n, :], turned[1])
                    pe.wait_ge(h_ready[1], b)
                    wait(pe, yo_ready, b - 1)
                    pe.matmul(S, Win2[:].rearrange("p q m -> p (q m)"), h2[:], start=True, stop=True).then_inc(s_filled, 1)
                    wait(pe, mlp_chain, 2 * (b - 1))
                    for p in range(HP):
                        pe.wait_ge(relu_ready, HP * (b - 1) + p + 1)
                        pe.matmul(O2, Wc[:, p, :], r[p % RR][:], start=(p == 0), stop=(p == HP - 1)).then_inc(relu_used, 1)
                if mix:
                    pe.wait_ge(y_ready, b + 1)
                    wait(pe, xm_ready, b)
                    pe.matmul(O, WoR[:], y[:], start=True, stop=True).then_inc(o_filled, 1)
                if mlp:
                    pe.wait_ge(mlp_chain, 2 * b)
                    pe.wait_ge(s_ready, b)
                    turn(S, lambda n: xo[:, cols(n)], xo_turned)

            pe.wait_ge(init_done, 6)
            steps(pe, step)

        @block.scalar
        def _(act):
            act.wait_ge(init_done, 6)

            def step(b, par, mix, mlp):
                if mix:
                    wait(act, xm_ready, b)
                    act.activation(xc[:], xT[:, b, :], ACT.Copy).then_inc(xc_ready, 1)
                    act.wait_ge(turned[0], 2 * b + 2)
                    wait(act, kvr_filled, 3 * b)
                    act.activation(hp[:, 1:T + 1], PB, ACT.Identity, bias=mod[:, SHIFT, one(b)],
                                   scale=mod[:, SCALE1, one(b)]).then_inc(h_ready[0], 1)
                if mix:
                    act.wait_ge(kvr_filled, 3 * b + 3)
                    wait(act, scan_chain, CH * b)
                    act.activation(thr[:], R, ACT.Tanh, scale=0.5).then_inc(th_ready, 1)
                if mlp:
                    act.wait_ge(turned[1], 2 * b)
                    wait(act, s_filled, b - 1)
                    act.activation(h2[:], PB, ACT.Identity, bias=mod[:, 3 + SHIFT, one(b - 1)],
                                   scale=mod[:, 3 + SCALE1, one(b - 1)]).then_inc(h_ready[1], 1)
                    act.wait_ge(s_filled, b)
                    act.activation(s[:], S, ACT.Identity, bias=col("bin")).then_inc(s_ready, 1)
                    act.wait_ge(s_ready, b)

                def relu(p):
                    n = HP * (b - 1) + p
                    if p < RR:
                        wait(act, relu_used, HP * (b - 1) - RR + p + 1)
                    else:
                        act.wait_ge(relu_used, HP * (b - 1) + (p - RR + 1))
                    act.activation(r[p % RR][:], s[:], ACT.Relu, bias=b1p[:, p:p + 1],
                                   scale=w1p[:, p:p + 1]).then_inc(relu_ready, 1)

                if mlp:
                    for p in range(RR):
                        relu(p)
                if mix:
                    act.wait_ge(scan_chain, CH * b + 3)
                    wait(act, scan_chain, CH * b)
                    act.activation(ex[:, 0:2, :], arg[:, 0:2, :], ACT.Exp).then_inc(ex_ready, 1)
                    act.wait_ge(pool_done, 3 * b + 1)
                    act.wait_ge(scan_chain, CH * b + 5)
                    act.activation(ex[:, 2:4, :], arg[:, 2:4, :], ACT.Exp).then_inc(ex_ready, 1)
                if mlp:
                    for p in range(RR, HP):
                        relu(p)
                    act.wait_ge(xo_turned, b)
                    if not isinstance(b, int) or b >= 3:
                        act.wait_ge(stored, 16 * (b - 2))
                    act.activation(y_out[1 - par][:].rearrange("p n f -> p (n f)"), S, ACT.Copy).then_inc(yo_ready, 1)

            steps(act, step)

        @block.vector
        def _(dve):
            dve.memset(ones[:], 1.0).then_inc(init_done, 1)
            dve.wait_ge(init_done, 5)
            dve.tensor_scalar(tdB[:], ones[:], col("ntd"), None, ALU.mult).then_inc(init_done, 1)
            dve.wait_ge(init_done, 6)

            def norm_stats(k, b):
                dve.wait_ge(turned[k], 2 * b + 1)
                for n in range(NB):
                    dve.bn_stats(stats[k][:, n, :], PA[:, n * P:(n + 1) * P]).then_inc(stats_chain[k], 1)
                dve.wait_ge(stats_chain[k], 2 * NB * b + NB)
                wait(dve, rstd_chain[k], 2 * b)
                wait_apart(dve, xn_ready[k], b, passed)
                for n in range(NB):
                    dve.bn_aggr(mv[k][:, n, :], stats[k][:, n, :]).then_inc(stats_chain[k], 1)

            def normalize(k, b):
                dve.wait_ge(rstd_chain[k], 2 * b + 2)
                dve.wait_ge(stats_chain[k], 2 * NB * (b + 1))
                wait(dve, turned[k], 2 * b)
                for n in range(NB):
                    last = dve.tensor_scalar(xn[k][:, n, :], PA[:, n * P:(n + 1) * P], mv[k][:, n, 0:1],
                                             rstd[k][:, n:n + 1], ALU.subtract, ALU.mult)
                last.then_inc(xn_ready[k], 1)

            def step(b, par, mix, mlp_too):
                def link(ins, n):
                    ins.then_inc(scan_chain, 1)

                def after(n):
                    dve.wait_ge(scan_chain, CH * b + n)

                if mix:
                    norm_stats(0, b)
                    normalize(0, b)
                if mlp_too:
                    norm_stats(1, b - 1)
                    normalize(1, b - 1)
                if mix:
                    before, now = slice(0, T), slice(1, T + 1)
                    dve.wait_ge(kvr_filled, 3 * b + 3)
                    wait(dve, pool_done, 3 * b)
                    wait(dve, ex_ready, 2 * b)
                    link(dve.tensor_tensor_scan(mx[:, now], tdB[:], K, TINY_MX, ALU.add, ALU.max), 1)
                    after(1)
                    link(dve.scalar_tensor_tensor(arg[:, 0, :], mx[:, before], col("ntd"), mx[:, now],
                                                  ALU.add, ALU.subtract), 2)
                    link(dve.tensor_tensor(arg[:, 1, :], K, mx[:, now], ALU.subtract), 3)
                    link(dve.scalar_tensor_tensor(mo[:], K, col("tf"), mx[:, before], ALU.add, ALU.max), 4)
                    after(4)
                    link(dve.scalar_tensor_tensor(arg[:, 3, :], K, col("tf"), mo[:], ALU.add, ALU.subtract), 5)
                    dve.wait_ge(ex_ready, 2 * b + 1)
                    link(dve.tensor_tensor(e2v[:], ex[:, 1, :], V, ALU.mult), 6)
                    after(6)
                    link(dve.tensor_tensor_scan(num[:, now], ex[:, 0, :], e2v[:], 0.0, ALU.mult, ALU.add), 7)
                    link(dve.tensor_tensor_scan(den[:, now], ex[:, 0, :], ex[:, 1, :], 0.0, ALU.mult, ALU.add), 8)
                    dve.wait_ge(ex_ready, 2 * b + 2)
                    link(dve.tensor_tensor(n2[:], ex[:, 3, :], V, ALU.mult), 9)
                if mlp_too:
                    dve.wait_ge(relu_used, HP * b)
                    dve.tensor_scalar(mlp[:], O2, col("cst"), mod[:, 3 + GATE, one(b - 1)], ALU.add,
                                      ALU.mult).then_inc(mlp_chain, 1)
                    dve.wait_ge(mlp_chain, 2 * (b - 1) + 1)
                    wait(dve, xo_turned, b - 1)
                    dve.tensor_tensor(xo[:], mlp[:], xm[1 - par][:], ALU.add).then_inc(mlp_chain, 1)
                if mix:
                    dve.wait_ge(pool_done, 3 * b + 3)
                    after(9)
                    link(dve.tensor_tensor(denom[:], d1[:], ex[:, 3, :], ALU.add), 10)
                    link(dve.tensor_tensor(numer[:], n1[:], n2[:], ALU.add), 11)
                    after(10)
                    link(dve.reciprocal(recd[:], denom[:]), 12)
                    after(11)
                    dve.wait_ge(th_ready, b + 1)
                    link(dve.scalar_tensor_tensor(ry[:], thr[:], 1.0, numer[:], ALU.add, ALU.mult), 13)
                    after(13)
                    wait(dve, o_filled, b)
                    dve.scalar_tensor_tensor(y[:], ry[:], 0.5, recd[:], ALU.mult, ALU.mult).then_inc(y_ready, 1)
                    dve.wait_ge(o_filled, b + 1)
                    dve.scalar_tensor_tensor(xm[par][:], O, mod[:, GATE, one(b)], xc[:], ALU.mult,
                                             ALU.add).then_inc(xm_ready, 1)

            steps(dve, step)


_INS = ["L0_attn_x", "L0_attn_Wq", "L0_attn_bq", "L0_attn_Wk", "L0_attn_bk", "L0_attn_Wv", "L0_attn_bv",
        "L0_attn_Wo", "L0_attn_bo", "L0_attn_Wq_lsr", "L0_attn_Wk_lsr", "L0_ffn_ln_w", "L0_ffn_ln_b",
        "L0_ffn_router_w", "L0_ffn_gate_w", "L0_ffn_up_w", "L0_ffn_down_w", "L0_ffn_sh_gate",
        "L0_ffn_sh_up", "L0_ffn_sh_down", "L0_c", "L0_wmod", "L1_attn_Wk", "L1_attn_Wv", "L1_attn_Wr",
        "L1_attn_Wo", "L1_attn_time_decay", "L1_attn_time_first", "L1_attn_time_mix_key",
        "L1_attn_time_mix_value", "L1_attn_time_mix_receptance", "L1_ffn_Win", "L1_ffn_bin_", "L1_ffn_W1",
        "L1_ffn_b1", "L1_ffn_W2", "L1_ffn_b2", "L1_ffn_Wout", "L1_ffn_bout", "L1_c", "L1_wmod"]


def kernel(**inputs):
    import numpy as _np
    import concourse.bacc as _bacc
    from concourse import mybir as _mybir
    from concourse.bass_utils import run_bass_kernel_spmd as _run

    nc = _bacc.Bacc("TRN2", target_bir_lowering=False, num_devices=1)
    arrays, args = {}, {}
    for name in _INS:
        x = _np.ascontiguousarray(inputs[name])
        arrays[f"in_{name}_dram"] = x
        args[name] = nc.dram_tensor(f"in_{name}_dram", x.shape, _mybir.dt.from_np(x.dtype), kind="ExternalInput").ap()
    y = nc.dram_tensor("out_dram", (B, T, D), F32, kind="ExternalOutput").ap()
    adaln_kernel(nc, args, y)
    r = _run(nc, [arrays], core_ids=[0])
    return r.results[0]["out_dram"]
```

```python
from contextlib import ExitStack

import concourse.bass as bass
from concourse import mybir

F32 = mybir.dt.float32
BF16 = mybir.dt.bfloat16
ALU = mybir.AluOpType
ACT = mybir.ActivationFunctionType
AX_X = mybir.AxisListType.X

P = 128
D = 128
B, T = 8, 512
NB = T // P
H, DH, RANK = 16, 8, 32
HG = 4
NG = H // HG
SLOTS = 9
NPART = 3
MAX_ROW = 96
E, HID = 8, 256
HC = HID // P
M, INNER = 64, 16
HP = INNER // 2
EPS = 1e-5
NEG = -1.0e30
SCALE = 1.0 / RANK ** 0.5
TINY_MX = -1.0e38
GATE_MIN = 0.25

SHIFT, SCALE1, GATE = 0, 1, 2


def wait(eng, sem, value):
    if not (isinstance(value, int) and value <= 0):
        eng.wait_ge(sem, value)


def wait_apart(eng, sem, value, passed):
    if isinstance(value, int):
        wait(eng, sem, value)
    else:
        eng.wait_ge(sem, value)
        eng.sem_inc(passed, 1)


def adaln_kernel(nc, a, out):
    with ExitStack() as ctx:
        build(nc, ctx, a, out)


def build(nc, ctx, a, out):
    def sb(name, shape, dt=F32, c=ctx):
        return c.enter_context(nc.sbuf_tensor(name, shape, dt))

    def sem(name):
        return ctx.enter_context(nc.semaphore(name))

    ps = ctx.enter_context(nc.psum_tensor("ps", [P, 8, 512], F32))

    xT = sb("xT", [D, B, T])
    ident = sb("ident", [P, P])
    identb = sb("identb", [P, P], BF16)
    neghalf = sb("neghalf", [P, NB])
    one_col = sb("one_col", [P, 1])
    mod = [sb(f"mod{l}", [D, 6, B]) for l in range(2)]
    NAMES = ["bq", "bk", "bv", "bo", "ln_w", "ln_b", "td", "tf", "mk", "mv", "mr", "bout",
             "bin", "b2", "bqP", "bkP", "bo2", "cst", "ntd"]
    vec = sb("vec", [P, len(NAMES)])

    def col(name):
        i = NAMES.index(name)
        return vec[:, i:i + 1]

    WqP = sb("WqP", [D, DH, H])
    WkP = sb("WkP", [D, DH, H])
    WvT = sb("WvT", [D, D])
    WoT = sb("WoT", [D, D])
    gab = sb("gab", [D, B])
    gu_w = sb("gu_w", [D, E, 2 * HID])
    down_w = sb("down_w", [P, E, HC, D])
    shg_w = sb("shg_w", [D, HID])
    shu_w = sb("shu_w", [D, HID])
    shd_w = sb("shd_w", [P, HC, D])
    router_w = sb("router_w", [D, E])
    Wmix = sb("Wmix", [D, 6, D])
    WoR = sb("WoR", [D, D])
    Win2 = sb("Win2", [D, 2, M])
    Wc = sb("Wc", [P, HP, D])
    w1p = sb("w1p", [P, HP])
    b1p = sb("b1p", [P, HP])

    setup(nc, a, sb, sem, ps, xT, ident, identb, neghalf, one_col, mod, col, WqP, WkP, WvT, WoT, gab,
          gu_w, down_w, shg_w, shu_w, shd_w, router_w, Wmix, WoR, Win2, Wc, w1p, b1p)
    with ExitStack() as c:
        attention(nc, a, lambda n, s, dt=F32: sb(n, s, dt, c), sem, ps, xT, ident, identb, neghalf,
                  mod[0], col, WqP, WkP, WvT, WoT, gab)
    with ExitStack() as c:
        moe(nc, lambda n, s, dt=F32: sb(n, s, dt, c), sem, ps, xT, ident, neghalf, mod[0], col,
            gu_w, down_w, shg_w, shu_w, shd_w, router_w)
    with ExitStack() as c:
        mixing(nc, out, lambda n, s, dt=F32: sb(n, s, dt, c), sem, ps, xT, ident, neghalf, mod[1],
               col, Wmix, WoR, Win2, Wc, w1p, b1p)


def setup(nc, a, sb0, sem, ps, xT, ident, identb, neghalf, one_col, mod, col, WqP, WkP, WvT, WoT, gab,
          gu_w, down_w, shg_w, shu_w, shd_w, router_w, Wmix, WoR, Win2, Wc, w1p, b1p):
    with ExitStack() as c:
        def sb(name, shape, dt=F32):
            return sb0(name, shape, dt, c)

        raw = sb("raw", [P, 4, D])
        identP = sb("identP", [P, DH, H])
        lsr = sb("lsr", [P, 2, RANK])
        lsrT = sb("lsrT", [RANK, 2, P])
        bdmask = sb("bdmask", [P, H, DH])
        BD = sb("BD", [P, DH, H])
        c_in = sb("c_in", [B, 2, D])
        cT = sb("cT", [D, 2, B])
        th = sb("th", [D, 2, B])
        scT = sb("scT", [D, 2, B])
        wmod = sb("wmod", [D, 2, 6 * D])
        gtmp = sb("gtmp", [D, 2, 2, B])
        gabs = sb("gabs", [D, 2, 2, B])
        mixw = sb("mixw", [D, 3, D])
        omm = sb("omm", [D, 3])
        Wout2 = sb("Wout2", [P, D])
        w2p = sb("w2p", [P, HP])
        inner = sb("inner", [P, 3, INNER])
        small_loaded, weights_loaded, moe_loaded = sem("small_loaded"), sem("weights_loaded"), sem("moe_loaded")
        consts_ready, turned, folded, copied = sem("consts_ready"), sem("turned"), sem("folded"), sem("copied")
        tanh_ready, td_ready = sem("tanh_ready"), sem("td_ready")

        def column(name):
            return a[name].rearrange("(p o) -> p o", o=1)

        smalls = [(col("bq"), column("L0_attn_bq")), (col("bk"), column("L0_attn_bk")),
                  (col("bv"), column("L0_attn_bv")), (col("bo"), column("L0_attn_bo")),
                  (col("ln_w"), column("L0_ffn_ln_w")), (col("ln_b"), column("L0_ffn_ln_b")),
                  (col("td"), column("L1_attn_time_decay")), (col("tf"), column("L1_attn_time_first")),
                  (col("mk"), column("L1_attn_time_mix_key")), (col("mv"), column("L1_attn_time_mix_value")),
                  (col("mr"), column("L1_attn_time_mix_receptance")), (col("bout"), column("L1_ffn_bout")),
                  (c_in[:, 0, :], a["L0_c"]), (c_in[:, 1, :], a["L1_c"]),
                  (lsr[:, 0, :], a["L0_attn_Wq_lsr"].rearrange("h d r -> (h d) r")),
                  (lsr[:, 1, :], a["L0_attn_Wk_lsr"].rearrange("h d r -> (h d) r"))]
        for q in range(2):
            half = slice(M * q, M * (q + 1))
            smalls += [(col("bin")[half, :], column("L1_ffn_bin_")), (col("b2")[half, :], column("L1_ffn_b2"))]
            for k, name in enumerate(("L1_ffn_W1", "L1_ffn_b1", "L1_ffn_W2")):
                smalls.append((inner[half, k, :], a[name]))
            smalls += [(Wout2[half, :], a["L1_ffn_Wout"]), (Win2[:, q, :], a["L1_ffn_Win"])]
        bigs = [(raw[:, 0, :], a["L0_attn_Wq"]), (raw[:, 1, :], a["L0_attn_Wk"]),
                (raw[:, 2, :], a["L0_attn_Wv"]), (raw[:, 3, :], a["L0_attn_Wo"]),
                (wmod[:, 0, :], a["L0_wmod"]), (wmod[:, 1, :], a["L1_wmod"]),
                (mixw[:, 0, :], a["L1_attn_Wk"]), (mixw[:, 1, :], a["L1_attn_Wv"]),
                (mixw[:, 2, :], a["L1_attn_Wr"]), (WoR[:, :], a["L1_attn_Wo"])]
        moes = [(gu_w[:, :, 0:HID], a["L0_ffn_gate_w"].rearrange("e p f -> p e f")),
                (gu_w[:, :, HID:], a["L0_ffn_up_w"].rearrange("e p f -> p e f")),
                (down_w[:, :, :, :], a["L0_ffn_down_w"].rearrange("e (c p) f -> p e c f", p=P)),
                (shg_w[:, :], a["L0_ffn_sh_gate"]), (shu_w[:, :], a["L0_ffn_sh_up"]),
                (shd_w[:, :, :], a["L0_ffn_sh_down"].rearrange("(c p) f -> p c f", p=P)),
                (router_w[:, :], a["L0_ffn_router_w"])]
        NSMALL, NBIG, NMOE = 16 * len(smalls), 16 * len(bigs), 16 * len(moes)

        with nc.Block() as block:
            @block.sync
            def _(sp):
                for dst, src in bigs:
                    sp.dma_start(dst, src).then_inc(weights_loaded, 16)
                for dst, src in moes:
                    sp.dma_start(dst, src).then_inc(moe_loaded, 16)
                sp.wait_ge(moe_loaded, NMOE)

            @block.gpsimd
            def _(pool):
                pool.memset(ident[:], 0.0).then_inc(consts_ready, 1)
                pool.memset(bdmask[:], 1.0).then_inc(consts_ready, 1)
                pool.memset(neghalf[:], -0.5).then_inc(consts_ready, 1)
                pool.memset(one_col[:], 1.0).then_inc(consts_ready, 1)
                pool.wait_ge(consts_ready, 4)
                pool.affine_select(out=ident[:], in_=ident[:], compare_op=ALU.not_equal, fill=1.0, base=0,
                                   pattern=[[-1, P]], channel_multiplier=1).then_inc(consts_ready, 1)
                pool.affine_select(out=bdmask[:], in_=bdmask[:], compare_op=ALU.is_ge, fill=0.0, base=0,
                                   pattern=[[-DH, H], [0, DH]], channel_multiplier=1).then_inc(consts_ready, 1)
                pool.wait_ge(consts_ready, 6)
                pool.affine_select(out=bdmask[:], in_=bdmask[:], compare_op=ALU.is_ge, fill=0.0, base=DH - 1,
                                   pattern=[[DH, H], [0, DH]], channel_multiplier=-1).then_inc(consts_ready, 1)
                pool.tensor_copy(identP[:].rearrange("p d h -> p h d"),
                                 ident[:].rearrange("p (h d) -> p h d", d=DH)).then_inc(consts_ready, 1)

            @block.tensor
            def _(pe):
                pe.wait_ge(consts_ready, 8)
                pe.wait_ge(small_loaded, NSMALL)
                for k in range(2):
                    pe.transpose(ps[0:RANK, 0, k * P:(k + 1) * P], lsr[:, k, :], ident[:])
                    pe.transpose(ps[:, 0, 256 + k * B:256 + (k + 1) * B], c_in[:, k, :], ident[0:B, 0:B])
                pe.matmul(ps[:, 0, 300:301], identP[:].rearrange("p d h -> p (d h)"), col("bk"),
                          start=True, stop=True)
                pe.matmul(ps[:, 0, 302:303], Wout2[0:M, :], col("b2")[0:M, :],
                          start=True, stop=True).then_inc(turned, 1)
                pe.wait_ge(weights_loaded, NBIG)
                for k in range(3):
                    last = pe.transpose(ps[:, 1, k * P:(k + 1) * P], raw[:, k + 1, :], ident[:])
                last.then_inc(turned, 1)
                pe.wait_ge(copied, 1)
                pe.matmul(ps[:, 2, 0:P], lsrT[:, 0, :], lsrT[:, 1, :], start=True, stop=True).then_inc(folded, 1)
                pe.wait_ge(copied, 2)
                pe.matmul(ps[:, 3, 0:1], WoT[:], col("bv"), start=True, stop=True).then_inc(folded, 1)
                pe.wait_ge(copied, 3)
                for l in range(2):
                    for j in range(6):
                        last = pe.matmul(ps[:, 4 + l, j * B:(j + 1) * B], wmod[:, l, j * D:(j + 1) * D],
                                         scT[:, l, :], start=True, stop=True)
                last.then_inc(folded, 1)
                pe.wait_ge(copied, 4)
                pe.matmul(ps[:, 6, 0:P], raw[:, 0, :], BD[:].rearrange("p d h -> p (d h)"), start=True, stop=True)
                pe.matmul(ps[:, 6, P:P + 1], BD[:].rearrange("p d h -> p (d h)"), col("bq"),
                          start=True, stop=True).then_inc(folded, 1)

            @block.scalar
            def _(act):
                for dst, src in smalls:
                    act.dma_start(dst, src).then_inc(small_loaded, 16)
                act.wait_ge(small_loaded, NSMALL)
                act.activation(col("ntd"), col("td"), ACT.Exp).then_inc(td_ready, 1)
                act.wait_ge(turned, 1)
                act.activation(th[:].rearrange("p l b -> p (l b)"), ps[:, 0, 256:256 + 2 * B], ACT.Tanh,
                               scale=0.5).then_inc(tanh_ready, 1)

            @block.vector
            def _(dve):
                dve.wait_ge(consts_ready, 8)
                dve.tensor_copy(identb[:], ident[:]).then_inc(td_ready, 1)
                dve.wait_ge(turned, 1)
                dve.wait_ge(tanh_ready, 1)
                dve.tensor_copy(lsrT[:].rearrange("p k n -> p (k n)"), ps[0:RANK, 0, 0:256]).then_inc(copied, 1)
                dve.scalar_tensor_tensor(scT[:].rearrange("p l b -> p (l b)"), th[:].rearrange("p l b -> p (l b)"),
                                         1.0, ps[:, 0, 256:256 + 2 * B], ALU.add, ALU.mult).then_inc(td_ready, 1)
                dve.tensor_copy(col("bkP"), ps[:, 0, 300:301])
                dve.tensor_tensor(col("cst"), col("bout"), ps[:, 0, 302:303], ALU.add)
                dve.wait_ge(turned, 2)
                dve.tensor_copy(WkP[:].rearrange("p d h -> p h d"),
                                ps[:, 1, 0:P].rearrange("p (h d) -> p h d", d=DH))
                dve.tensor_copy(WvT[:], ps[:, 1, P:2 * P])
                dve.tensor_copy(WoT[:], ps[:, 1, 2 * P:3 * P]).then_inc(copied, 1)
                dve.wait_ge(td_ready, 3)
                dve.tensor_scalar(scT[:], scT[:], 0.5, None, ALU.mult).then_inc(copied, 1)
                dve.wait_ge(folded, 1)
                dve.scalar_tensor_tensor(BD[:].rearrange("p d h -> p h d"),
                                         ps[:, 2, 0:P].rearrange("p (h d) -> p h d", d=DH), SCALE, bdmask[:],
                                         ALU.mult, ALU.mult).then_inc(copied, 1)
                dve.tensor_scalar(col("ntd"), col("ntd"), -1.0, None, ALU.mult)
                for k, m in enumerate(("mk", "mv", "mr")):
                    dve.tensor_scalar(omm[:, k:k + 1], col(m), -1.0, 1.0, ALU.mult, ALU.add).then_inc(td_ready, 1)
                for k, dst in enumerate((w1p, b1p, w2p)):
                    for q in range(2):
                        half = slice(M * q, M * (q + 1))
                        dve.tensor_copy(dst[half, :], inner[half, k, :].rearrange("m (p q) -> m q p", q=2)[:, q, :]).then_inc(td_ready, 1)
                dve.wait_ge(td_ready, 12)
                for k, m in enumerate(("mk", "mv", "mr")):
                    dve.tensor_scalar(Wmix[:, 2 * k, :], mixw[:, k, :], col(m), None, ALU.mult)
                    dve.tensor_scalar(Wmix[:, 2 * k + 1, :], mixw[:, k, :], omm[:, k:k + 1], None, ALU.mult)
                for p in range(HP):
                    dve.tensor_scalar(Wc[:, p, :], Wout2[:], w2p[:, p:p + 1], None, ALU.mult)
                dve.wait_ge(folded, 2)
                dve.tensor_tensor(col("bo2"), col("bo"), ps[:, 3, 0:1], ALU.add).then_inc(td_ready, 1)
                dve.wait_ge(folded, 3)
                for l in range(2):
                    dve.tensor_copy(mod[l][:].rearrange("p j b -> p (j b)"), ps[:, 4 + l, 0:6 * B]).then_inc(td_ready, 1)
                dve.wait_ge(td_ready, 15)
                for l in range(2):
                    for s in range(2):
                        g = mod[l][:, 3 * s + GATE, :]
                        dve.tensor_scalar(mod[l][:, 3 * s + SCALE1, :], mod[l][:, 3 * s + SCALE1, :], 1.0, None, ALU.add)
                        dve.tensor_scalar(gtmp[:, l, s, :], g, 0.0, 2.0, ALU.is_ge, ALU.mult)
                        dve.tensor_scalar(gabs[:, l, s, :], g, -1.0, None, ALU.mult).then_inc(td_ready, 1)
                dve.wait_ge(td_ready, 19)
                for l in range(2):
                    for s in range(2):
                        dve.tensor_tensor(gabs[:, l, s, :], gabs[:, l, s, :], mod[l][:, 3 * s + GATE, :],
                                          ALU.max).then_inc(td_ready, 1)
                dve.wait_ge(td_ready, 23)
                dve.tensor_scalar(gabs[:], gabs[:], GATE_MIN, None, ALU.max).then_inc(td_ready, 1)
                dve.wait_ge(td_ready, 24)
                for l in range(2):
                    for s in range(2):
                        dve.scalar_tensor_tensor(mod[l][:, 3 * s + GATE, :], gtmp[:, l, s, :], -1.0,
                                                 gabs[:, l, s, :], ALU.add, ALU.mult).then_inc(td_ready, 1)
                dve.wait_ge(td_ready, 28)
                dve.tensor_scalar(gab[:], mod[0][:, GATE, :], col("bo2"), None, ALU.mult)
                dve.wait_ge(folded, 4)
                dve.tensor_copy(WqP[:].rearrange("p d h -> p (d h)"), ps[:, 6, 0:P])
                dve.tensor_copy(col("bqP"), ps[:, 6, P:P + 1]).then_inc(td_ready, 1)


def attention(nc, a, sb, sem, ps, xT, ident, identb, neghalf, mod, col, WqP, WkP, WvT, WoT, gab):
    x_in = [sb(f"x_in{p}", [P, NB, D]) for p in range(2)]
    xn = sb("xn", [P, NB, D])
    hT = sb("hT", [D, T])
    mv = sb("mv_a", [P, NB, 2])
    stats = sb("stats_a", [P, NB, 6])
    rstd = sb("rstd_a", [P, NB])
    full = sb("full", [P, 2, T])
    rest = sb("rest", [P, 2, T])
    part = sb("part", [P, 2, NPART, T], BF16)
    Qs = [sb(f"Qs{p}", [P, H, T], BF16) for p in range(2)]
    Ks = [sb(f"Ks{p}", [P, H, T], BF16) for p in range(2)]
    V = [sb(f"V{p}", [P, NB, D]) for p in range(2)]
    Vg = sb("Vg", [P, NB, HG, 32])
    mask4 = sb("mask4", [P, HG, P], BF16)
    maskT = sb("maskT", [P, 2, P], BF16)
    mask_f = sb("mask_f", [P, P])
    nmax = [sb(f"nmax{p}", [P, NB, H]) for p in range(2)]
    nrest = sb("nrest", [P, NB, H])
    npart_wide = sb("npart", [P, NB, P], BF16)
    npart = npart_wide[:, :, 0:NPART * H].rearrange("p n (k h) -> p n k h", k=NPART)
    nmT = sb("nmT", [NPART * H, T], BF16)
    zero48 = sb("zero48", [NPART * H, T], BF16)
    PR = sb("PR", [P, HG, 1280])
    yT = sb("yT", [P, NG, T])
    rec = sb("rec", [P, NG, NB, HG])
    yn = sb("yn", [P, NB, H, DH])
    ynT = sb("ynT", [D, T])
    SEG = {0: (0, 512), 1: (512, 384), 3: (896, 128), 2: (1024, 256)}

    A = [ps[:, 0:2, :], ps[:, 2:4, :]]
    X2 = [ps[:, 4, :], ps[:, 5, :]]
    Y, C = ps[:, 6, :], ps[:, 7, :]

    x_loaded, qk_moved, nm_moved = sem("x_loaded"), sem("qk_moved"), sem("nm_moved")
    init_done, mask_done = sem("init_done"), sem("mask_done")
    stats_chain, pool_chain, xn_ready = sem("stats_chain"), sem("pool_chain"), sem("xn_ready")
    xt_filled, xt_copied, ht_filled, ht_ready = sem("xt_filled"), sem("xt_copied"), sem("ht_filled"), sem("ht_ready")
    qk_filled, v_filled, v_copied = sem("qk_filled"), sem("v_filled"), sem("v_copied")
    full_ready, rest_ready, part1_ready, split_done = sem("full_ready"), sem("rest_ready"), sem("part1_ready"), sem("split_done")
    s1_filled, max_taken, s2_filled, exp_done = sem("s1_filled"), sem("max_taken"), sem("s2_filled"), sem("exp_done")
    vg_ready, pv_done, y_copied = sem("vg_ready"), sem("pv_done"), sem("y_copied")
    nm_chain, nm_filled, nm_copied = sem("nm_chain"), sem("nm_filled"), sem("nm_copied")
    yt_filled, rec_ready, yn_ready = sem("yt_filled"), sem("rec_ready"), sem("yn_ready")
    ynt_filled, ynt_ready, o_filled, x_done = sem("ynt_filled"), sem("ynt_ready"), sem("o_filled"), sem("x_done")

    INIT = 10
    RING = 2
    passed = sem("a_passed")
    QK_DMAS = 16 * (2 * SLOTS + 1)

    ORDER = [2, 2, 1, 2, 2, 1, 2, 2, 1, 2, 2, 1, 2, 2, 1, 1]
    UNITS1 = [(0, range(0, 4), 4), (1, range(0, 4), 2), (2, range(0, 2), 1), (2, range(2, 4), 1),
              (3, range(0, 2), 1), (3, range(2, 4), 1)]
    UNITS2 = []
    for h0 in (0, 2):
        for h in (h0, h0 + 1):
            UNITS2 += [[(h, 0, 0)], [(h, 1, 0), (h, 3, 384)]]
        UNITS2.append([(h0, 2, 0), (h0 + 1, 2, 256)])
    N1, N2 = len(UNITS1), len(UNITS2)

    def s1_banks(u):
        ib, heads, per = UNITS1[u]
        n = (ib + 1) * P
        banks = A[u % 2][:, 0:len(heads) // per, :]
        return banks[:, :, 0:n * per].rearrange("p k (h n) -> p k h n", h=per)

    with nc.Block() as block:
        @block.sync
        def _(sp):
            def load_x(b, par):
                if not isinstance(b, int) or b >= 2:
                    wait_apart(sp, xt_filled, b - 1, passed)
                    wait_apart(sp, xn_ready, b - 1, passed)
                wait(sp, x_loaded, 16 * b)
                sp.dma_start(x_in[par][:], a["L0_attn_x"][b].rearrange("(n p) f -> p n f", p=P)).then_inc(x_loaded, 16)

            def move_qk(b, par):
                wait_apart(sp, split_done, 2 * b + 2, passed)
                if not isinstance(b, int) or b >= 2:
                    wait_apart(sp, pv_done, NG * (b - 1), passed)
                else:
                    sp.wait_ge(init_done, INIT)
                wait(sp, qk_moved, QK_DMAS * b)
                for s in range(SLOTS):
                    rows = slice(DH * s, DH * (s + 1))
                    sp.dma_start(Qs[par][rows, :, :], part[:, 0, s // NPART, :]).then_inc(qk_moved, 16)
                    sp.dma_start(Ks[par][rows, :, :], part[:, 1, s % NPART, :]).then_inc(qk_moved, 16)
                sp.dma_start(Qs[par][MAX_ROW:MAX_ROW + NPART, :, :], zero48[:]).then_inc(qk_moved, 16)

            def move_nm(b, par):
                sp.wait_ge(nm_copied, b + 1)
                sp.dma_start(Qs[par][MAX_ROW:MAX_ROW + NPART, :, :], nmT[:]).then_inc(nm_moved, 16)

            load_x(0, 0)
            load_x(1, 1)
            move_qk(0, 0)
            move_qk(1, 1)
            move_nm(0, 0)
            with sp.Fori(0, B // 2 - 1) as i:
                for par in range(2):
                    b = 2 * i + par
                    load_x(b + 2, par)
                    move_nm(b + 1, 1 - par)
                    move_qk(b + 2, par)
            move_nm(B - 1, 1)

        @block.gpsimd
        def _(pool):
            pool.memset(mask_f[:], 0.0).then_inc(mask_done, 1)
            pool.wait_ge(mask_done, 1)
            pool.affine_select(out=mask_f[:], in_=mask_f[:], compare_op=ALU.is_ge, fill=NEG, base=0,
                               pattern=[[-1, P]], channel_multiplier=1).then_inc(mask_done, 1)
            pool.wait_ge(mask_done, 2)
            for h in range(HG):
                pool.tensor_copy(mask4[:, h, :], mask_f[:]).then_inc(mask_done, 1)
            pool.memset(xn[:, 0, :], 0.0).then_inc(mask_done, 1)
            pool.wait_ge(mask_done, 7)
            pool.affine_select(out=xn[:, 0, :], in_=xn[:, 0, :], compare_op=ALU.is_ge, fill=NEG, base=0,
                               pattern=[[1, P]], channel_multiplier=-1).then_inc(mask_done, 1)
            pool.wait_ge(mask_done, 8)
            for h in range(2):
                pool.tensor_copy(maskT[:, h, :], xn[:, 0, :]).then_inc(mask_done, 1)

            def rstd_of(b):
                wait_apart(pool, stats_chain, 2 * NB * (b + 1), passed)
                pool.tensor_scalar(rstd[:], mv[:, :, 1], EPS, None, ALU.add).then_inc(pool_chain, 1)
                pool.wait_ge(pool_chain, 2 * b + 1)
                pool.tensor_tensor(rstd[:], rstd[:], neghalf[:], ALU.pow).then_inc(pool_chain, 1)

            rstd_of(0)
            rstd_of(1)
            with pool.Fori(0, B // 2 - 1) as i:
                for par in range(2):
                    rstd_of(2 * i + par + 2)

        @block.tensor
        def _(pe):
            def project(b, par, first=False):
                pe.wait_ge(x_loaded, 16 * (b + 1))
                if not first:
                    pe.wait_ge(exp_done, NG * N2 * (b - 1) + RING)
                for n in range(NB):
                    last = pe.transpose(X2[1][:, n * P:(n + 1) * P], x_in[par][:, n, :], ident[:])
                last.then_inc(xt_filled, 1)
                pe.wait_ge(xn_ready, b + 1)
                for n in range(NB):
                    last = pe.transpose(A[0][:, 0, n * P:(n + 1) * P], xn[:, n, :], ident[:])
                last.then_inc(ht_filled, 1)

            def project2(b, par, first=False):
                pe.wait_ge(ht_ready, b + 1)
                pe.matmul(A[0][:, 1, :], WqP[:].rearrange("p d h -> p (d h)"), hT[:], start=True, stop=True)
                pe.matmul(A[1][:, 0, :], WkP[:].rearrange("p d h -> p (d h)"), hT[:],
                          start=True, stop=True).then_inc(qk_filled, 1)
                if not first:
                    pe.wait_ge(nm_copied, b)
                elif b > 0:
                    pe.wait_ge(v_copied, b)
                for n in range(NB):
                    last = pe.matmul(X2[0][:, n * P:(n + 1) * P], hT[:, n * P:(n + 1) * P], WvT[:],
                                     start=True, stop=True)
                last.then_inc(v_filled, 1)

            def unit1(b, g, par, u):
                ib, heads, per = UNITS1[u]
                n = (ib + 1) * P
                t = NG * b + g
                pe.wait_ge(max_taken, N1 * t + (u + 1))
                banks = s1_banks(u)
                for k in range(banks.shape[1]):
                    for j in range(per):
                        h = g * HG + heads[k * per + j]
                        pe.matmul(banks[:, k, j, :], Qs[par][:, h, ib * P:(ib + 1) * P], Ks[par][:, h, 0:n],
                                  start=(j == 0), stop=False, skip_group_check=True)
                    last = pe.matmul(banks[:, k, :, n - P:n], identb[:], mask4[:, 0:per, :],
                                     start=False, stop=True, skip_group_check=True)
                last.then_inc(s1_filled, 1)

            def unit2(b, g, par, u):
                t = NG * b + g
                pe.wait_ge(exp_done, N2 * t + (u + 1))
                bank = X2[u % 2]
                for k, (hh, jb, at) in enumerate(UNITS2[u]):
                    h = g * HG + hh
                    last = pe.matmul(bank[:, at:at + T - jb * P], Ks[par][:, h, jb * P:(jb + 1) * P],
                                     Qs[par][:, h, jb * P:T], start=(k == 0), stop=False, skip_group_check=True)
                ats = [at for _, _, at in UNITS2[u]]
                if len(ats) == 1:
                    last = pe.matmul(bank[:, 0:P], identb[:], maskT[:, 0, :], start=False, stop=True,
                                     skip_group_check=True)
                elif ats[1] == 256:
                    last = pe.matmul(bank.rearrange("p (k n) -> p k n", k=2)[:, :, 0:P], identb[:], maskT[:],
                                     start=False, stop=True, skip_group_check=True)
                else:
                    last = pe.matmul(bank.rearrange("p (k n) -> p k n", k=4)[:, 0:4:3, :], identb[:], maskT[:],
                                     start=False, stop=True, skip_group_check=True)
                last.then_inc(s2_filled, 1)

            def pv(b, g):
                t = NG * b + g
                pe.wait_ge(vg_ready, t + 1)
                pe.wait_ge(exp_done, N2 * (t + 1) + RING)
                pe.wait_ge(y_copied, t + 1)
                pe.wait_ge(x_done, b + 1)
                for jb in range(NB):
                    at, n = SEG[jb]
                    for hh in range(HG):
                        last = pe.matmul(Y[32 * hh:32 * hh + 32, jb * P:T], Vg[:, jb, hh, :], PR[:, hh, at:at + n],
                                         start=(jb == 0), stop=(jb == NB - 1), skip_group_check=True)
                last.then_inc(pv_done, 1)

            def groups(b, par, with1, with2):
                if with2:
                    wait_apart(pe, nm_moved, 16 * (b + 1), passed)
                if with1:
                    wait_apart(pe, qk_moved, QK_DMAS * (b + 2), passed)
                with pe.Fori(0, NG) as g:
                    u1 = u2 = 0
                    for kind in ORDER:
                        if kind == 1:
                            if with1:
                                unit1(b + 1, g, 1 - par, u1)
                            u1 += 1
                        else:
                            if with2:
                                unit2(b, g, par, u2)
                            u2 += 1
                    if with2:
                        pv(b, g)

            def turn_maxima(b, par):
                pe.wait_ge(nm_chain, 4 * (b + 1))
                if not isinstance(b, int) or b > 0:
                    pe.wait_ge(exp_done, NG * N2 * b + RING)
                bank = X2[0].bitcast(BF16)
                for n in range(NB):
                    last = pe.transpose(bank[:, n * P:(n + 1) * P], npart_wide[:, n, :], identb[:])
                last.then_inc(nm_filled, 1)

            def turn_y(b):
                pe.wait_ge(y_copied, NG * (b + 1) + 1)
                last_one = isinstance(b, int) and b == B - 1
                pe.wait_ge(max_taken, NG * N1 * (B if last_one else b + 2) + RING)
                for g in range(NG):
                    for n in range(NB):
                        last = pe.transpose(ps[:, g, n * P:(n + 1) * P], yT[:, g, n * P:(n + 1) * P], ident[:])
                last.then_inc(yt_filled, 1)

            def output(b):
                pe.wait_ge(yn_ready, NB * (b + 1))
                for n in range(NB):
                    last = pe.transpose(C[:, n * P:(n + 1) * P], yn[:, n, :, :].rearrange("p h d -> p (h d)"), ident[:])
                last.then_inc(ynt_filled, 1)

            def output2(b):
                pe.wait_ge(ynt_ready, b + 1)
                pe.matmul(Y, WoT[:], ynT[:], start=True, stop=True).then_inc(o_filled, 1)

            pe.wait_ge(mask_done, 10)
            pe.wait_ge(init_done, INIT)
            project(0, 0, True)
            project2(0, 0, True)
            pe.wait_ge(xt_copied, 1)
            pe.wait_ge(full_ready, 4)
            project(1, 1, True)
            project2(1, 1, True)
            pe.wait_ge(full_ready, 8)
            pe.wait_ge(v_copied, 2)
            pe.wait_ge(xt_copied, 2)
            groups(-1, 1, True, False)
            turn_maxima(0, 0)

            def sequence(b, par, nxt, nxt2):
                groups(b, par, nxt, True)
                if nxt:
                    turn_maxima(b + 1, 1 - par)
                turn_y(b)
                output(b)
                if nxt2:
                    project(b + 2, par)
                output2(b)
                if nxt2:
                    project2(b + 2, par)
                    pe.wait_ge(full_ready, 4 * (b + 3))
                    pe.wait_ge(v_copied, b + 3)
                    pe.wait_ge(xt_copied, b + 3)

            with pe.Fori(0, B // 2 - 1) as i:
                for par in range(2):
                    sequence(2 * i + par, par, True, True)
            sequence(B - 2, 0, True, False)
            pe.wait_ge(nm_copied, B)
            sequence(B - 1, 1, False, False)


        @block.scalar
        def _(act):
            act.sem_inc(exp_done, RING)
            act.sem_inc(y_copied, 1)

            def one(b):
                return slice(b, b + 1) if isinstance(b, int) else bass.ds(b, 1)

            def copy_x(b):
                act.wait_ge(xt_filled, b + 1)
                act.activation(xT[:, b, :], X2[1], ACT.Identity, bias=gab[:, one(b)]).then_inc(xt_copied, 1)

            def copy_h(b):
                act.wait_ge(ht_filled, b + 1)
                wait(act, v_filled, b)
                act.activation(hT[:], A[0][:, 0, :], ACT.Identity, bias=mod[:, SHIFT, one(b)],
                               scale=mod[:, SCALE1, one(b)]).then_inc(ht_ready, 1)

            def split(b):
                act.wait_ge(qk_filled, b + 1)
                wait(act, qk_moved, QK_DMAS * b)
                for k, (bank, bias) in enumerate(((A[0][:, 1, :], "bqP"), (A[1][:, 0, :], "bkP"))):
                    act.activation(full[:, k, :], bank, ACT.Identity, bias=col(bias)).then_inc(full_ready, 1)
                    act.activation(part[:, k, 0, :], bank, ACT.Identity, bias=col(bias)).then_inc(full_ready, 1)
                for k in range(2):
                    act.wait_ge(rest_ready, 2 * b + k + 1)
                    act.activation(part[:, k, 1, :], rest[:, k, :], ACT.Copy).then_inc(part1_ready, 1)

            def groups(b, par):
                with act.Fori(0, NG) as g:
                    t = NG * b + g
                    act.activation(Vg[:, :, :, 0:DH],
                                   V[par][:, :, bass.ds(g * (HG * DH), HG * DH)].rearrange("p n (h d) -> p n h d", h=HG),
                                   ACT.Copy).then_inc(vg_ready, 1)
                    for u in range(N2):
                        act.wait_ge(s2_filled, N2 * t + u + 1)
                        bank, todo = X2[u % 2], UNITS2[u]
                        h, jb, _ = todo[0]
                        if jb == 2:
                            dst = PR[:, h:h + 2, SEG[2][0]:1280]
                            src = bank.rearrange("p (k n) -> p k n", k=2)
                        else:
                            dst, src = PR[:, h, SEG[jb][0]:SEG[jb][0] + 512], bank
                        act.activation(dst, src, ACT.Exp).then_inc(exp_done, 1)
                    act.wait_ge(pv_done, t + 1)
                    act.activation(yT[:, g, :], Y, ACT.Copy).then_inc(y_copied, 1)

            def copy_maxima(b):
                act.wait_ge(nm_filled, b + 1)
                wait(act, nm_moved, 16 * b)
                act.activation(nmT[:], X2[0].bitcast(BF16)[0:NPART * H, 0:T], ACT.Copy).then_inc(nm_copied, 1)

            def copy_y(b):
                act.wait_ge(ynt_filled, b + 1)
                act.activation(ynT[:], C, ACT.Copy).then_inc(ynt_ready, 1)

            act.wait_ge(init_done, INIT)
            for b in range(2):
                copy_x(b)
                copy_h(b)
                split(b)
                act.wait_ge(v_copied, b + 1)
            copy_maxima(0)

            def sequence(b, par, nxt, nxt2):
                act.wait_ge(v_copied, b + 1)
                groups(b, par)
                if nxt:
                    copy_maxima(b + 1)
                copy_y(b)
                if nxt2:
                    copy_x(b + 2)
                    copy_h(b + 2)
                    split(b + 2)

            with act.Fori(0, B // 2 - 1) as i:
                for par in range(2):
                    sequence(2 * i + par, par, True, True)
            sequence(B - 2, 0, True, False)
            sequence(B - 1, 1, False, False)

        @block.vector
        def _(dve):
            dve.sem_inc(max_taken, RING)
            dve.sem_inc(x_done, 1)
            for p in range(2):
                dve.memset(Qs[p][:].rearrange("p h t -> p (h t)").bitcast(mybir.dt.uint32), 0).then_inc(init_done, 1)
                dve.memset(Ks[p][:].rearrange("p h t -> p (h t)").bitcast(mybir.dt.uint32), 0).then_inc(init_done, 1)
            dve.memset(zero48[:], 0.0).then_inc(init_done, 1)
            dve.memset(Vg[:], 0.0).then_inc(init_done, 1)
            dve.memset(npart_wide[:], 0.0).then_inc(init_done, 1)
            dve.wait_ge(init_done, 7)
            for p in range(2):
                dve.memset(Ks[p][MAX_ROW:MAX_ROW + NPART, :, :], 1.0).then_inc(init_done, 1)
            dve.memset(Vg[:, :, :, DH:DH + 1], 1.0).then_inc(init_done, 1)

            def norm_stats(b, par):
                dve.wait_ge(x_loaded, 16 * (b + 1))
                for n in range(NB):
                    dve.bn_stats(stats[:, n, :], x_in[par][:, n, :]).then_inc(stats_chain, 1)
                dve.wait_ge(stats_chain, 2 * NB * b + NB)
                wait(dve, pool_chain, 2 * b)
                wait_apart(dve, xn_ready, b, passed)
                for n in range(NB):
                    dve.bn_aggr(mv[:, n, :], stats[:, n, :]).then_inc(stats_chain, 1)

            def normalize(b, par):
                dve.wait_ge(pool_chain, 2 * b + 2)
                dve.wait_ge(stats_chain, 2 * NB * (b + 1))
                wait(dve, ht_filled, b)
                for n in range(NB):
                    last = dve.tensor_scalar(xn[:, n, :], x_in[par][:, n, :], mv[:, n, 0:1], rstd[:, n:n + 1],
                                             ALU.subtract, ALU.mult)
                last.then_inc(xn_ready, 1)

            def split(b, par):
                for k in range(2):
                    dve.wait_ge(full_ready, 4 * b + 2 * k + 2)
                    wait(dve, split_done, 2 * b)
                    dve.tensor_tensor(rest[:, k, :], full[:, k, :], part[:, k, 0, :], ALU.subtract).then_inc(rest_ready, 1)
                dve.wait_ge(v_filled, b + 1)
                if not isinstance(b, int) or b >= 2:
                    dve.wait_ge(vg_ready, NG * (b - 1))
                dve.tensor_copy(V[par][:].rearrange("p n f -> p (n f)"), X2[0]).then_inc(v_copied, 1)
                for k in range(2):
                    dve.wait_ge(part1_ready, 2 * b + k + 1)
                    dve.tensor_tensor(part[:, k, 2, :], rest[:, k, :], part[:, k, 1, :], ALU.subtract).then_inc(split_done, 1)

            def maxima(b, par):
                with dve.Fori(0, NG) as g:
                    for u, (ib, heads, per) in enumerate(UNITS1):
                        t = NG * b + g
                        dve.wait_ge(s1_filled, N1 * t + u + 1)
                        banks = s1_banks(u)
                        dst = nmax[par][:, ib, bass.ds(g * HG + heads[0], len(heads))]
                        if per > 1:
                            dst = dst.rearrange("p (k h) -> p k h", h=per)
                            if banks.shape[1] == 1:
                                dst, banks = dst[:, 0, :], banks[:, 0, :, :]
                        else:
                            banks = banks[:, :, 0, :]
                        dve.tensor_reduce(dst, banks, AX_X, ALU.max, negate=True).then_inc(max_taken, 1)

            def split_maxima(b, par):
                dve.wait_ge(max_taken, NG * N1 * (b + 1) + RING)
                wait(dve, nm_filled, b)
                dve.tensor_copy(npart[:, :, 0, :], nmax[par][:]).then_inc(nm_chain, 1)
                dve.wait_ge(nm_chain, 4 * b + 1)
                dve.tensor_tensor(nrest[:], nmax[par][:], npart[:, :, 0, :], ALU.subtract).then_inc(nm_chain, 1)
                dve.wait_ge(nm_chain, 4 * b + 2)
                dve.tensor_copy(npart[:, :, 1, :], nrest[:]).then_inc(nm_chain, 1)
                dve.wait_ge(nm_chain, 4 * b + 3)
                dve.tensor_tensor(npart[:, :, 2, :], nrest[:], npart[:, :, 1, :], ALU.subtract).then_inc(nm_chain, 1)

            def divide(b):
                dve.wait_ge(yt_filled, b + 1)
                turned = ps[:, 0:NG, :].rearrange("p g (n h r) -> p g n h r", n=NB, h=HG)
                wait(dve, yn_ready, NB * b)
                for g in range(NG):
                    dve.reciprocal(rec[:, g, :, :], turned[:, g, :, :, DH]).then_inc(rec_ready, 1)
                dve.wait_ge(rec_ready, NG * (b + 1))
                wait(dve, ynt_filled, b)
                for n in range(NB):
                    dve.tensor_tensor(yn[:, n, :, :].rearrange("p (g h) d -> p g h d", g=NG), turned[:, :, n, :, 0:DH],
                                      rec[:, :, n, :].unsqueeze(3).to_broadcast([P, NG, HG, DH]),
                                      ALU.mult).then_inc(yn_ready, 1)

            def add_output(b):
                dve.wait_ge(o_filled, b + 1)
                one = slice(b, b + 1) if isinstance(b, int) else bass.ds(b, 1)
                dve.scalar_tensor_tensor(xT[:, b, :], Y, mod[:, GATE, one], xT[:, b, :],
                                         ALU.mult, ALU.add).then_inc(x_done, 1)

            for b in range(2):
                norm_stats(b, b)
                normalize(b, b)
                split(b, b)
            maxima(0, 0)
            split_maxima(0, 0)

            def sequence(b, par, nxt, nxt2):
                if nxt:
                    maxima(b + 1, 1 - par)
                    split_maxima(b + 1, 1 - par)
                if nxt2:
                    norm_stats(b + 2, par)
                divide(b)
                if nxt2:
                    normalize(b + 2, par)
                add_output(b)
                if nxt2:
                    split(b + 2, par)

            with dve.Fori(0, B // 2 - 1) as i:
                for par in range(2):
                    sequence(2 * i + par, par, True, True)
            sequence(B - 2, 0, True, False)
            sequence(B - 1, 1, False, False)


def moe(nc, sb, sem, ps, xT, ident, neghalf, mod, col, gu_w, down_w, shg_w, shu_w, shd_w, router_w):
    FIRST = 3
    BLOCKS = B * NB
    GROUP = 8
    TILES = GROUP * (-(-(BLOCKS + E - 1) // GROUP))
    ROW = D + 4
    ZT = 10

    sorted_in = nc.dram_tensor("sorted_in", (TILES * P, ROW), F32, kind="Internal").ap()
    sorted_out = nc.dram_tensor("sorted_out", (TILES * P, D), F32, kind="Internal").ap()

    xc = [sb(f"xc{p}", [D, T]) for p in range(2)]
    hT = [sb(f"hTm{p}", [D, T]) for p in range(2)]
    nT = [sb(f"nTm{p}", [D, T]) for p in range(2)]
    xn = [sb(f"xnm{k}", [P, NB, D]) for k in range(2)]
    stats = [sb(f"stats_m{k}", [P, NB, 6]) for k in range(2)]
    mv = [sb(f"mv_m{k}", [P, NB, 2]) for k in range(2)]
    rstd = [sb(f"rstd_m{k}", [P, NB]) for k in range(2)]
    hall = sb("hall", [D, B, T])
    nall = sb("nall", [D, B, T])
    rows = sb("rows", [P, BLOCKS, ROW])
    zeros = sb("zeros_m", [P, ZT, ROW])
    count_i = sb("count_i", [P, BLOCKS, E], mybir.dt.int32)
    prio = sb("prio", [P, BLOCKS, E])
    steps_P = sb("steps_P", [P, E, BLOCKS])
    tile_no = sb("tile_no", [P, TILES, E - 1])
    before = sb("before", [P, P])
    ones = sb("ones_m", [P, P])
    top, topkey, th_top = sb("top", [P, BLOCKS]), sb("topkey", [P, BLOCKS]), sb("th_top", [P, BLOCKS])
    key = sb("key", [P, BLOCKS, E])
    here = sb("here", [P, BLOCKS, E])
    totals = sb("totals", [P, E, BLOCKS])
    none = sb("none_m", [P, E * BLOCKS])
    sums = sb("sums", [P, E * BLOCKS + 1])
    count = sb("count", [P, E])
    over = sb("over", [P, E, BLOCKS])
    etiles = sb("etiles", [P, E])
    first = sb("first", [P, E + 1])
    shift = sb("shift", [P, E])
    place = sb("place", [P, BLOCKS, E])
    pos = sb("pos", [P, BLOCKS])
    pos_i = sb("pos_i", [P, BLOCKS], mybir.dt.int32)
    later = sb("later", [P, TILES, E - 1])
    expert = sb("expert", [P, TILES])
    expert_i = sb("expert_i", [P, TILES], mybir.dt.int32)
    th = [sb(f"thm{c}", [P, T]) for c in range(HC)]
    sil = [sb(f"sil{c}", [P, T]) for c in range(HC)]
    hid = [sb(f"hid{p}", [P, HC, T]) for p in range(2)]
    tin = [sb(f"tin{k}", [P, ROW]) for k in range(GROUP)]
    tn = [sb(f"tn{p}", [D, P]) for p in range(2)]
    tth = [sb(f"tth{p}", [P, HID]) for p in range(2)]
    tsil = [sb(f"tsil{p}", [P, HID]) for p in range(2)]
    thid = [sb(f"thid{p}", [P, HID]) for p in range(2)]
    thT = [sb(f"thT{p}", [P, HC, P]) for p in range(2)]
    tout = [sb(f"tout{p}", [P, 2, D]) for p in range(2)]
    back = [sb(f"back{p}", [P, NB, D]) for p in range(2)]
    total = sb("total", [D, T])

    PA, PB, PC, PD = (ps[:, k, :] for k in range(4))
    LOG = ps[:, 4, 0:BLOCKS * E].rearrange("p (n e) -> p n e", e=E)
    RANKS, TOTALS = ps[:, 5, 0:BLOCKS * E], ps[:, 6, 0:BLOCKS * E]
    G, U, OUT = [ps[:, 0, :], ps[:, 1, :]], [ps[:, 2, :], ps[:, 3, :]], ps[:, 7, :]
    TIN, TGU = [ps[:, 5, 0:P], ps[:, 6, 0:P]], [ps[:, 0, :], ps[:, 1, :]]
    THT, TY = [ps[:, 2, 0:HID], ps[:, 3, 0:HID]], [ps[:, 4, 0:D], ps[:, 7, 0:D]]

    consts, zero_ready, zeroed = sem("m_consts"), sem("m_zero_ready"), sem("m_zeroed")
    init_dve = sem("m_init_dve")
    xc_ready, h_ready, h_kept, n_ready = sem("m_xc_ready"), sem("m_h_ready"), sem("m_h_kept"), sem("m_n_ready")
    n_kept, rows_kept, logits_filled = sem("m_n_kept"), sem("m_rows_kept"), sem("m_logits")
    tokens_filled = [sem(f"m_tokens{k}") for k in range(2)]
    turned = [sem(f"m_turned{k}") for k in range(2)]
    stats_chain = [sem(f"m_stats{k}") for k in range(2)]
    rstd_chain = [sem(f"m_rstd{k}") for k in range(2)]
    xn_ready = [sem(f"m_xn{k}") for k in range(2)]
    route, th_ready, counted, scattered = sem("m_route"), sem("m_th_top"), sem("m_counted"), sem("m_scattered")
    gu_filled, tanh_ready, silu_ready, hid_ready = sem("m_gu"), sem("m_tanh"), sem("m_silu"), sem("m_hid")
    down_done, shared_added = sem("m_down"), sem("m_shared_added")
    t_loaded = [sem(f"m_t_loaded{k}") for k in range(GROUP)]
    t_stored = [sem(f"m_t_stored{p}") for p in range(2)]
    t_in, t_n, t_gu, t_th, t_sil, t_hid = (sem(f"m_t_{k}") for k in ("in", "n", "gu", "th", "sil", "hid"))
    t_turned, t_hT, t_down, t_out = (sem(f"m_t_{k}") for k in ("turned", "hT", "down", "out"))
    fetched = [sem(f"m_fetched{p}") for p in range(2)]
    back_turned, total_ready, x_done = sem("m_back_turned"), sem("m_total"), sem("m_x_done")
    passed = sem("m_passed")
    CONSTS = 11
    TOP_READY, HERE_READY, ROWS_READY, EXPERTS_READY = 1, 5, 19, 22

    def one(b):
        return slice(b, b + 1) if isinstance(b, int) else bass.ds(b, 1)

    def blocks(b):
        return slice(NB * b, NB * (b + 1)) if isinstance(b, int) else bass.ds(NB * b, NB)

    def late(b, n):
        return not isinstance(b, int) or b >= n

    def norm_steps(eng, step):
        step(-1, 1, True, False)
        step(0, 0, True, True)
        step(1, 1, True, True)
        with eng.Fori(1, B // 2 - 1) as i:
            for q in range(2):
                step(2 * i + q, q, True, True)
        step(B - 2, 0, True, True)
        step(B - 1, 1, False, True)

    def shared_steps(eng, step):
        step(0, 0, True, False)
        step(1, 1, True, True)
        with eng.Fori(1, B // 2) as i:
            for q in range(2):
                step(2 * i + q, q, True, True)
        step(B, 0, False, True)

    def tile_steps(eng, step):
        for k in range(GROUP):
            step(k, k, 0)
        with eng.Fori(1, TILES // GROUP - 1) as i:
            for k in range(GROUP):
                step(GROUP * i + k, k, i)
        for k in range(GROUP):
            step(TILES - GROUP + k, k, TILES // GROUP - 1)

    with nc.Block() as block:
        @block.sync
        def _(sp):
            sp.wait_ge(zero_ready, 1)
            for z in range(TILES // ZT):
                sp.dma_start(sorted_in[z * ZT * P:(z + 1) * ZT * P, :].rearrange("(p n) f -> p n f", p=P),
                             zeros[:]).then_inc(zeroed, 16)

            def store(t, k):
                half = (k // 2) % 2
                wait_apart(sp, t_out, t + 2, passed)
                if isinstance(t, int):
                    dst = sorted_out[t * P:(t + 2) * P, :]
                else:
                    dst = sorted_out[bass.ds(t * P, 2 * P), :]
                sp.dma_start(dst.rearrange("(n p) f -> p n f", p=P), tout[half][:]).then_inc(t_stored[half], 16)

            def step(t, k):
                if late(t, GROUP):
                    wait_apart(sp, t_hid, t - GROUP + 1, passed)
                src = sorted_in[t * P:(t + 1) * P, :] if isinstance(t, int) else sorted_in[bass.ds(t * P, P), :]
                sp.dma_start(tin[k][:], src).then_inc(t_loaded[k], 16)
                if k % 2 and late(t, GROUP + 1):
                    store(t - GROUP - 1, k - 1)

            sp.wait_ge(scattered, 16 * BLOCKS)
            for t in range(GROUP):
                step(t, t)
            with sp.Fori(1, TILES // GROUP) as i:
                for k in range(GROUP):
                    step(GROUP * i + k, k)
            for t in range(TILES - GROUP, TILES, 2):
                store(t, t % GROUP)
            for half in range(2):
                sp.wait_ge(t_stored[half], 16 * (TILES // 4))

        @block.gpsimd
        def _(pool):
            pool.memset(zeros[:], 0.0).then_inc(zero_ready, 1)
            pool.memset(ones[:], 1.0).then_inc(consts, 1)
            pool.memset(before[:], 1.0).then_inc(consts, 1)
            pool.memset(none[:], 0.0).then_inc(consts, 1)
            pool.iota(count_i[:], pattern=[[0, BLOCKS], [-1, E]], base=E, channel_multiplier=0).then_inc(consts, 1)
            pool.wait_ge(consts, 4)
            pool.affine_select(out=before[:], in_=before[:], compare_op=ALU.is_ge, fill=0.0, base=-1,
                               pattern=[[1, P]], channel_multiplier=-1).then_inc(consts, 1)

            def rstd_of(k, b):
                pool.wait_ge(stats_chain[k], 2 * NB * (b + 1))
                if late(b, 1):
                    wait_apart(pool, xn_ready[k], b, passed)
                pool.tensor_scalar(rstd[k][:], mv[k][:, :, 1], EPS, None, ALU.add).then_inc(rstd_chain[k], 1)
                pool.wait_ge(rstd_chain[k], 2 * b + 1)
                pool.tensor_tensor(rstd[k][:], rstd[k][:], neghalf[:], ALU.pow).then_inc(rstd_chain[k], 1)

            def step(s, par, do_first, do_second):
                if do_first:
                    rstd_of(0, s + 1)
                if do_second:
                    rstd_of(1, s)
                    wait_apart(pool, xn_ready[1], s + 1, passed)
                    pool.tensor_copy(rows[:, blocks(s), 0:D], xn[1][:]).then_inc(rows_kept, 1)
                    wait_apart(pool, n_ready, s + 1, passed)
                    pool.tensor_copy(nall[:, s, :], nT[par][:]).then_inc(n_kept, 1)

            rstd_of(0, 0)
            pool.tensor_copy(prio[:], count_i[:]).then_inc(consts, 1)
            pool.wait_ge(consts, 6)
            pool.iota(count_i[:].rearrange("p n e -> p (n e)"), pattern=[[0, E], [P, BLOCKS]], base=0,
                      channel_multiplier=0).then_inc(consts, 1)
            pool.wait_ge(consts, 7)
            pool.tensor_copy(steps_P[:].rearrange("p e n -> p (e n)"), count_i[:].rearrange("p n e -> p (n e)")).then_inc(consts, 1)
            pool.wait_ge(consts, 8)
            count_t = later[:].bitcast(mybir.dt.int32)
            pool.iota(count_t, pattern=[[1, TILES], [0, E - 1]], base=0, channel_multiplier=0).then_inc(consts, 1)
            pool.wait_ge(consts, 9)
            pool.tensor_copy(tile_no[:], count_t).then_inc(consts, 1)
            pool.memset(rows[:, :, D + 2:ROW], 0.0).then_inc(consts, 1)
            norm_steps(pool, lambda s, par, f, g: step(s, par, f, g) if not (isinstance(s, int) and s < 0) else None)

            pool.wait_ge(zeroed, 16 * (TILES // ZT))
            pool.wait_ge(route, ROWS_READY)
            for n in range(BLOCKS):
                pool.indirect_dma_start(sorted_in, bass.IndirectOffsetOnAxis(pos_i[:, n:n + 1], 0),
                                        rows[:, n, :], None).then_inc(scattered, 16)
            for half in range(2):
                pool.wait_ge(t_stored[half], 16 * (TILES // 4))
            for b in range(B):
                if b >= 2:
                    pool.wait_ge(back_turned, b - 1)
                for n in range(NB):
                    pool.indirect_dma_start(back[b % 2][:, n, :], None, sorted_out,
                                            bass.IndirectOffsetOnAxis(pos_i[:, NB * b + n:NB * b + n + 1], 0)
                                            ).then_inc(fetched[b % 2], 16)

        @block.tensor
        def _(pe):
            cols = lambda n: slice(n * P, (n + 1) * P)

            def turn(bank, src, signal):
                for n in range(NB):
                    last = pe.transpose(bank[:, cols(n)], src(n), ident[:])
                last.then_inc(signal, 1)

            def step(s, par, do_first, do_second):
                new = 1 - par
                if do_first:
                    pe.wait_ge(xc_ready, s + 2)
                    wait(pe, xn_ready[0], s + 1)
                    turn(PA, lambda n: xc[new][:, cols(n)], tokens_filled[0])
                if do_second:
                    pe.wait_ge(h_ready, s + 1)
                    wait(pe, xn_ready[1], s)
                    turn(PC, lambda n: hT[par][:, cols(n)], tokens_filled[1])
                if do_first:
                    pe.wait_ge(xn_ready[0], s + 2)
                    wait(pe, h_ready, s + 1)
                    turn(PB, lambda n: xn[0][:, n, :], turned[0])
                if do_second:
                    pe.wait_ge(xn_ready[1], s + 1)
                    wait(pe, n_ready, s)
                    turn(PD, lambda n: xn[1][:, n, :], turned[1])
                    pe.wait_ge(n_ready, s + 1)
                    for n in range(NB):
                        last = pe.matmul(LOG[:, one(NB * s + n), :].rearrange("p o e -> p (o e)"),
                                         nT[par][:, cols(n)], router_w[:], start=True, stop=True,
                                         skip_group_check=True)
                    last.then_inc(logits_filled, 1)

            norm_steps(pe, step)

            pe.wait_ge(route, HERE_READY)
            pe.wait_ge(consts, CONSTS)
            flat = here[:].rearrange("p n e -> p (n e)")
            pe.matmul(TOTALS, ones[:], flat, start=True, stop=True).then_inc(counted, 1)
            pe.matmul(RANKS, before[:], flat, start=True, stop=True).then_inc(counted, 1)

            pe.wait_ge(n_kept, B)
            pe.wait_ge(xn_ready[1], B)

            def shared(b, par, do_up, do_down):
                for c in range(HC):
                    if do_up:
                        if late(b, 1):
                            pe.wait_ge(hid_ready, HC * (b - 1) + c + 1)
                        pe.matmul(G[c], shg_w[:, cols(c)], nall[:, b, :], start=True, stop=True)
                        pe.matmul(U[c], shu_w[:, cols(c)], nall[:, b, :], start=True, stop=True).then_inc(gu_filled, 1)
                if do_down:
                    if late(b, 2):
                        pe.wait_ge(shared_added, b - 1)
                    for c in range(HC):
                        pe.wait_ge(hid_ready, HC * (b - 1) + c + 1)
                        last = pe.matmul(OUT, shd_w[:, c, :], hid[1 - par][:, c, :], start=(c == 0), stop=(c == HC - 1))
                    last.then_inc(down_done, 1)

            shared_steps(pe, shared)

            def turn_in(t, k):
                two = k % 2
                if isinstance(t, int):
                    pe.wait_ge(t_loaded[k], 16 * (t // GROUP + 1))
                if late(t, 2):
                    pe.wait_ge(t_n, t - 1)
                pe.transpose(TIN[two], tin[k][:, 0:D], ident[:]).then_inc(t_in, 1)

            def up(t, k, e):
                pe.wait_ge(t_n, t + 1)
                if late(t, 2):
                    pe.wait_ge(t_hid, t - 1)
                w = gu_w[:, one(e), :].rearrange("p o f -> p (o f)")
                pe.matmul(TGU[k % 2], tn[k % 2][:], w, start=True, stop=True).then_inc(t_gu, 1)

            def turn_hidden(t, k):
                two = k % 2
                pe.wait_ge(t_hid, t + 1)
                if late(t, 2):
                    pe.wait_ge(t_hT, t - 1)
                for c in range(HC):
                    last = pe.transpose(THT[two][:, cols(c)], thid[two][:, cols(c)], ident[:])
                last.then_inc(t_turned, 1)

            def down(t, k, e):
                two = k % 2
                pe.wait_ge(t_hT, t + 1)
                if late(t, 2):
                    pe.wait_ge(t_out, t - 1)
                for c in range(HC):
                    w = down_w[:, one(e), c, :].rearrange("p o f -> p (o f)")
                    last = pe.matmul(TY[two], thT[two][:, c, :], w, start=(c == 0), stop=(c == HC - 1))
                last.then_inc(t_down, 1)

            expert_regs = [pe.alloc_register(f"expert{j}") for j in range(GROUP + 2)]

            def load_experts(t0, n):
                pe.reg_load(expert_regs[:n], expert_i[0:1, t0:t0 + n] if isinstance(t0, int)
                            else expert_i[0:1, bass.ds(t0, n)])
                return [pe.snap(r, min_val=0, max_val=E - 1) for r in expert_regs[:n]]

            pe.wait_ge(route, EXPERTS_READY)
            pe.wait_ge(shared_added, B)
            turn_in(0, 0)
            turn_in(1, 1)
            up(0, 0, load_experts(0, 1)[0])

            def group(i, first_group, last_group):
                t = GROUP * i
                lo = 0 if first_group else -1
                experts = load_experts(t + lo, GROUP + (0 if last_group else 1) - lo)
                for k in range(GROUP):
                    if not (last_group and k >= GROUP - 2):
                        n = (k + 2) % GROUP
                        if not isinstance(t, int):
                            pe.wait_ge(t_loaded[n], 16 * (i + 1 + (k + 2) // GROUP))
                        turn_in(t + k + 2, n)
                    if not (last_group and k == GROUP - 1):
                        up(t + k + 1, (k + 1) % GROUP, experts[k + 1 - lo])
                    turn_hidden(t + k, k)
                    if not (first_group and k == 0):
                        down(t + k - 1, (k - 1) % GROUP, experts[k - 1 - lo])
                if last_group:
                    down(t + GROUP - 1, GROUP - 1, experts[GROUP - 1 - lo])

            group(0, True, False)
            with pe.Fori(1, TILES // GROUP - 1) as i:
                group(i, False, False)
            group(TILES // GROUP - 1, False, True)

            def join(b, par, i):
                pe.wait_ge(fetched[par], 16 * NB * (i + 1))
                if late(b, 1):
                    pe.wait_ge(total_ready, b)
                turn(PA, lambda n: back[par][:, n, :], back_turned)

            join(0, 0, 0)
            join(1, 1, 0)
            with pe.Fori(1, B // 2) as i:
                for q in range(2):
                    join(2 * i + q, q, i)

        @block.scalar
        def _(act):
            def copy_x(b, par):
                if late(b, 2):
                    act.wait_ge(tokens_filled[0], b - 1)
                act.activation(xc[par][:], xT[:, b, :], ACT.Copy).then_inc(xc_ready, 1)

            def step(s, par, do_first, do_second):
                new = 1 - par
                if do_first:
                    if late(s, 1):
                        act.wait_ge(tokens_filled[1], s)
                    act.wait_ge(turned[0], s + 2)
                    if late(s, 1):
                        act.wait_ge(h_kept, s)
                    act.activation(hT[new][:], PB, ACT.Identity, bias=mod[:, FIRST + SHIFT, one(s + 1)],
                                   scale=mod[:, FIRST + SCALE1, one(s + 1)]).then_inc(h_ready, 1)
                if do_second:
                    if late(s, 2):
                        act.wait_ge(logits_filled, s - 1)
                        act.wait_ge(n_kept, s - 1)
                    act.wait_ge(turned[1], s + 1)
                    act.activation(nT[par][:], PD, ACT.Identity, bias=col("ln_b"), scale=col("ln_w")).then_inc(n_ready, 1)
                if do_first:
                    act.wait_ge(h_ready, s + 2)
                    act.activation(hall[:, s + 1, :], hT[new][:], ACT.Copy).then_inc(h_kept, 1)
                    if not isinstance(s, int) or 0 <= s < B - 2:
                        copy_x(s + 2, par)

            copy_x(0, 0)
            copy_x(1, 1)
            norm_steps(act, step)

            act.wait_ge(route, TOP_READY)
            act.activation(th_top[:], top[:], ACT.Tanh, scale=0.5).then_inc(th_ready, 1)

            def shared(b, par, do_up, do_down):
                for c in range(HC if do_up else 0):
                    act.wait_ge(gu_filled, HC * b + c + 1)
                    if late(b, 1):
                        act.wait_ge(silu_ready, HC * (b - 1) + c + 1)
                    act.activation(th[c][:], G[c], ACT.Tanh, scale=0.5).then_inc(tanh_ready, 1)

            shared_steps(act, shared)

            def n_of(t, k):
                two = k % 2
                act.wait_ge(t_in, t + 1)
                if late(t, 2):
                    act.wait_ge(t_gu, t - 1)
                act.activation(tn[two][:], TIN[two], ACT.Identity, bias=col("ln_b"), scale=col("ln_w")).then_inc(t_n, 1)

            def tanh_of(t, k):
                two = k % 2
                act.wait_ge(t_gu, t + 1)
                if late(t, 2):
                    act.wait_ge(t_sil, t - 1)
                act.activation(tth[two][:], TGU[two][:, 0:HID], ACT.Tanh, scale=tin[k][:, D:D + 1]).then_inc(t_th, 1)

            def hidden_of(t, k):
                two = k % 2
                act.wait_ge(t_turned, t + 1)
                if late(t, 2):
                    act.wait_ge(t_down, t - 1)
                act.activation(thT[two][:].rearrange("p c n -> p (c n)"), THT[two], ACT.Copy).then_inc(t_hT, 1)

            def tile(t, k, i):
                if not (isinstance(t, int) and t + 2 >= TILES):
                    n_of(t + 2, (k + 2) % GROUP)
                if not (isinstance(t, int) and t + 1 >= TILES):
                    tanh_of(t + 1, (k + 1) % GROUP)
                hidden_of(t, k)

            n_of(0, 0)
            n_of(1, 1)
            tanh_of(0, 0)
            tile_steps(act, tile)

        @block.vector
        def _(dve):
            done = [0]

            def link(ins):
                ins.then_inc(route, 1)
                done[0] += 1
                dve.wait_ge(route, done[0])

            def norm_stats(k, b):
                dve.wait_ge(tokens_filled[k], b + 1)
                bank = (PA, PC)[k]
                for m in range(NB):
                    dve.bn_stats(stats[k][:, m, :], bank[:, m * P:(m + 1) * P]).then_inc(stats_chain[k], 1)
                dve.wait_ge(stats_chain[k], 2 * NB * b + NB)
                wait(dve, rstd_chain[k], 2 * b)
                wait_apart(dve, xn_ready[k], b, passed)
                for m in range(NB):
                    dve.bn_aggr(mv[k][:, m, :], stats[k][:, m, :]).then_inc(stats_chain[k], 1)

            def normalize(k, b):
                bank = (PA, PC)[k]
                dve.wait_ge(rstd_chain[k], 2 * b + 2)
                dve.wait_ge(stats_chain[k], 2 * NB * (b + 1))
                wait(dve, turned[k], b)
                if k == 1:
                    wait(dve, rows_kept, b)
                for m in range(NB):
                    last = dve.tensor_scalar(xn[k][:, m, :], bank[:, m * P:(m + 1) * P], mv[k][:, m, 0:1],
                                             rstd[k][:, m:m + 1], ALU.subtract, ALU.mult)
                last.then_inc(xn_ready[k], 1)

            def step(s, par, do_first, do_second):
                if do_first:
                    norm_stats(0, s + 1)
                if do_second:
                    norm_stats(1, s)
                if do_first:
                    normalize(0, s + 1)
                if do_second:
                    normalize(1, s)

            norm_steps(dve, step)

            wide = lambda x: x[:].unsqueeze(2).to_broadcast([P, BLOCKS, E])
            dve.memset(sums[:, 0:1], 0.0).then_inc(init_dve, 1)
            dve.memset(first[:, 0:1], 0.0).then_inc(init_dve, 1)
            dve.wait_ge(logits_filled, B)
            dve.wait_ge(consts, CONSTS)
            link(dve.tensor_reduce(top[:], LOG, AX_X, ALU.max))
            link(dve.tensor_tensor(key[:], LOG, wide(top), ALU.is_equal))
            link(dve.tensor_tensor(key[:], key[:], prio[:], ALU.mult))
            link(dve.tensor_reduce(topkey[:], key[:], AX_X, ALU.max))
            link(dve.tensor_tensor(here[:], key[:], wide(topkey), ALU.is_equal))
            dve.wait_ge(th_ready, 1)
            dve.wait_ge(rows_kept, B)
            link(dve.tensor_scalar(rows[:, :, D], th_top[:], 0.25, 0.25, ALU.mult, ALU.add))
            link(dve.scalar_tensor_tensor(rows[:, :, D + 1], rows[:, :, D], 2.0, rows[:, :, D], ALU.mult, ALU.mult))
            dve.wait_ge(counted, 1)
            link(dve.tensor_copy(totals[:].rearrange("p e n -> p n e"), TOTALS.rearrange("p (n e) -> p n e", e=E)))
            dve.wait_ge(init_dve, 2)
            link(dve.tensor_tensor_scan(sums[:, 1:], totals[:].rearrange("p e n -> p (e n)"), none[:], 0.0,
                                        ALU.add, ALU.add))
            starts = sums[:, 0:E * BLOCKS].rearrange("p (e n) -> p e n", e=E)
            ends = sums[:, 1:].rearrange("p (e n) -> p e n", e=E)
            link(dve.tensor_tensor(count[:], ends[:, :, BLOCKS - 1], starts[:, :, 0], ALU.subtract))
            link(dve.tensor_tensor(over[:], count[:].unsqueeze(2).to_broadcast([P, E, BLOCKS]), steps_P[:], ALU.is_gt))
            link(dve.tensor_reduce(etiles[:], over[:], AX_X, ALU.add))
            link(dve.tensor_tensor_scan(first[:, 1:], etiles[:], none[:, 0:E], 0.0, ALU.add, ALU.add))
            link(dve.scalar_tensor_tensor(shift[:], first[:, 0:E], float(P), starts[:, :, 0], ALU.mult, ALU.subtract))
            dve.wait_ge(counted, 2)
            link(dve.tensor_tensor(place[:], RANKS.rearrange("p (n e) -> p n e", e=E),
                                   starts.rearrange("p e n -> p n e"), ALU.add))
            link(dve.tensor_tensor(place[:], place[:], shift[:].unsqueeze(1).to_broadcast([P, BLOCKS, E]), ALU.add))
            link(dve.tensor_tensor(place[:], place[:], here[:], ALU.mult))
            link(dve.tensor_reduce(pos[:], place[:], AX_X, ALU.add))
            link(dve.tensor_copy(pos_i[:], pos[:]))
            link(dve.tensor_tensor(later[:], tile_no[:], first[:, 1:E].unsqueeze(1).to_broadcast([P, TILES, E - 1]),
                                   ALU.is_ge))
            link(dve.tensor_reduce(expert[:], later[:], AX_X, ALU.add))
            link(dve.tensor_copy(expert_i[:], expert[:]))

            def shared(b, par, do_up, do_down):
                for c in range(HC if do_up else 0):
                    dve.wait_ge(tanh_ready, HC * b + c + 1)
                    dve.scalar_tensor_tensor(sil[c][:], th[c][:], 1.0, G[c], ALU.add, ALU.mult).then_inc(silu_ready, 1)
                    dve.wait_ge(silu_ready, HC * b + c + 1)
                    if late(b, 2):
                        dve.wait_ge(down_done, b - 1)
                    dve.scalar_tensor_tensor(hid[par][:, c, :], sil[c][:], 0.5, U[c], ALU.mult,
                                             ALU.mult).then_inc(hid_ready, 1)
                if do_down:
                    dve.wait_ge(down_done, b)
                    dve.tensor_tensor(hall[:, b - 1, :], hall[:, b - 1, :], OUT, ALU.add).then_inc(shared_added, 1)

            dve.wait_ge(h_kept, B)
            shared_steps(dve, shared)

            def hidden(t, k):
                two = k % 2
                dve.wait_ge(t_th, t + 1)
                dve.scalar_tensor_tensor(tsil[two][:], tth[two][:], 1.0, TGU[two][:, 0:HID], ALU.add,
                                         ALU.mult).then_inc(t_sil, 1)
                dve.wait_ge(t_sil, t + 1)
                if late(t, 2):
                    dve.wait_ge(t_turned, t - 1)
                dve.scalar_tensor_tensor(thid[two][:], tsil[two][:], tin[k][:, D + 1:D + 2], TGU[two][:, HID:],
                                         ALU.mult, ALU.mult).then_inc(t_hid, 1)

            def output(t, k, i):
                half, two = (k // 2) % 2, k % 2
                dve.wait_ge(t_down, t + 1)
                if two == 0 and late(t, 4):
                    dve.wait_ge(t_stored[half], 16 * (GROUP // 4 * i + k // 4))
                dve.tensor_copy(tout[half][:, two, :], TY[two]).then_inc(t_out, 1)

            def tile(t, k, i):
                if not (isinstance(t, int) and t + 1 >= TILES):
                    hidden(t + 1, (k + 1) % GROUP)
                if late(t, 1):
                    output(t - 1, (k - 1) % GROUP, i)

            hidden(0, 0)
            tile_steps(dve, tile)
            output(TILES - 1, GROUP - 1, TILES // GROUP - 1)

            def join(b):
                dve.wait_ge(back_turned, b + 1)
                if late(b, 1):
                    dve.wait_ge(x_done, b)
                dve.tensor_tensor(total[:], hall[:, b, :], PA, ALU.add).then_inc(total_ready, 1)
                dve.wait_ge(total_ready, b + 1)
                dve.scalar_tensor_tensor(xT[:, b, :], total[:], mod[:, FIRST + GATE, one(b)], xT[:, b, :],
                                         ALU.mult, ALU.add).then_inc(x_done, 1)

            join(0)
            with dve.Fori(1, B) as b:
                join(b)


def mixing(nc, out, sb, sem, ps, xT, ident, neghalf, mod, col, Wmix, WoR, Win2, Wc, w1p, b1p):
    xc = sb("xc_t", [D, T])
    hp = sb("hp", [D, T + 1])
    xm = [sb(f"xm{p}", [D, T]) for p in range(2)]
    xn = [sb(f"xnt{k}", [P, NB, D]) for k in range(2)]
    stats = [sb(f"stats_t{k}", [P, NB, 6]) for k in range(2)]
    mv = [sb(f"mv_t{k}", [P, NB, 2]) for k in range(2)]
    rstd = [sb(f"rstd_t{k}", [P, NB]) for k in range(2)]
    ones = sb("ones_t", [D, T])
    tdB = sb("tdB", [D, T])
    mx = sb("mx", [D, T + 1])
    num = sb("num", [D, T + 1])
    den = sb("den", [D, T + 1])
    arg = sb("arg", [D, 4, T])
    ex = sb("ex", [D, 4, T])
    mo = sb("mo", [D, T])
    e2v = sb("e2v", [D, T])
    n1, n2 = sb("n1", [D, T]), sb("n2", [D, T])
    d1 = sb("d1", [D, T])
    numer, denom, recd = sb("numer", [D, T]), sb("denom", [D, T]), sb("recd", [D, T])
    thr = sb("thr", [D, T])
    ry, y = sb("ry", [D, T]), sb("y_t", [D, T])
    h2 = sb("h2", [D, T])
    s = sb("s_mlp", [P, T])
    RR = 4
    r = [sb(f"relu{k}", [P, T]) for k in range(RR)]
    mlp = sb("mlp", [D, T])
    xo = sb("xo", [D, T])
    y_out = [sb(f"y_out{p}", [P, NB, D]) for p in range(2)]

    PA, PB, K, V, R, S, O, O2 = (ps[:, k, :] for k in range(8))

    init_done, xc_ready = sem("t_init"), sem("t_xc")
    turned = [sem(f"t_turned{k}") for k in range(2)]
    stats_chain = [sem(f"t_stats{k}") for k in range(2)]
    rstd_chain = [sem(f"t_rstd{k}") for k in range(2)]
    xn_ready = [sem(f"t_xn{k}") for k in range(2)]
    h_ready = [sem(f"t_h{k}") for k in range(2)]
    kvr_filled, th_ready, scan_chain, ex_ready = sem("t_kvr"), sem("t_thr"), sem("t_chain"), sem("t_ex")
    pool_done, y_ready, o_filled, xm_ready = sem("t_pool"), sem("t_y"), sem("t_o"), sem("t_xm")
    s_filled, s_ready, relu_ready, relu_used = sem("t_s_filled"), sem("t_s"), sem("t_relu"), sem("t_relu_used")
    mlp_chain, xo_turned, yo_ready, stored = sem("t_mlp"), sem("t_xo_turned"), sem("t_yo"), sem("t_stored")
    passed = sem("t_passed")
    CH = 13

    def one(b):
        return slice(b, b + 1) if isinstance(b, int) else bass.ds(b, 1)

    def steps(eng, step):
        step(0, 0, True, False)
        step(1, 1, True, True)
        with eng.Fori(0, B // 2 - 1) as i:
            for q in range(2):
                step(2 * i + 2 + q, q, True, True)
        step(B, 0, False, True)

    with nc.Block() as block:
        @block.sync
        def _(sp):
            def store(b, par):
                wait(sp, stored, 16 * b) if isinstance(b, int) else wait_apart(sp, stored, 16 * b, passed)
                sp.wait_ge(yo_ready, b + 1)
                sp.dma_start(out[b].rearrange("(n p) f -> p n f", p=P), y_out[par][:]).then_inc(stored, 16)

            steps(sp, lambda b, par, mix, mlp: store(b - 1, 1 - par) if mlp else None)
            sp.wait_ge(stored, 16 * B)

        @block.gpsimd
        def _(pool):
            pool.memset(hp[:, 0:1], 0.0).then_inc(init_done, 1)
            pool.memset(mx[:, 0:1], TINY_MX).then_inc(init_done, 1)
            pool.memset(num[:, 0:1], 0.0).then_inc(init_done, 1)
            pool.memset(den[:, 0:1], 0.0).then_inc(init_done, 1)

            def rstd_of(k, b):
                pool.wait_ge(stats_chain[k], 2 * NB * (b + 1))
                wait_apart(pool, xn_ready[k], b, passed)
                pool.tensor_scalar(rstd[k][:], mv[k][:, :, 1], EPS, None, ALU.add).then_inc(rstd_chain[k], 1)
                pool.wait_ge(rstd_chain[k], 2 * b + 1)
                pool.tensor_tensor(rstd[k][:], rstd[k][:], neghalf[:], ALU.pow).then_inc(rstd_chain[k], 1)

            def step(b, par, mix, mlp):
                if mix:
                    rstd_of(0, b)
                if mlp:
                    rstd_of(1, b - 1)
                if mix:
                    pool.wait_ge(scan_chain, CH * b + 4)
                    pool.tensor_tensor(arg[:, 2, :], mx[:, 0:T], mo[:], ALU.subtract).then_inc(pool_done, 1)
                    pool.wait_ge(ex_ready, 2 * b + 2)
                    pool.wait_ge(scan_chain, CH * b + 7)
                    pool.tensor_tensor(n1[:], ex[:, 2, :], num[:, 0:T], ALU.mult).then_inc(pool_done, 1)
                    pool.wait_ge(scan_chain, CH * b + 8)
                    pool.tensor_tensor(d1[:], ex[:, 2, :], den[:, 0:T], ALU.mult).then_inc(pool_done, 1)

            steps(pool, step)

        @block.tensor
        def _(pe):
            def turn(bank, src, signal):
                for n in range(NB):
                    last = pe.transpose(bank[:, n * P:(n + 1) * P], src(n), ident[:])
                last.then_inc(signal, 1)

            def cols(n):
                return slice(n * P, (n + 1) * P)

            def step(b, par, mix, mlp):
                old = 1 - par
                if mix:
                    pe.wait_ge(xc_ready, b + 1)
                    wait(pe, h_ready[1], b - 1)
                    turn(PA, lambda n: xc[:, cols(n)], turned[0])
                    pe.wait_ge(xn_ready[0], b + 1)
                    turn(PB, lambda n: xn[0][:, n, :], turned[0])
                if mlp:
                    pe.wait_ge(xm_ready, b)
                    if mix:
                        pe.wait_ge(xn_ready[0], b + 1)
                    turn(PA, lambda n: xm[old][:, cols(n)], turned[1])
                if mix:
                    pe.wait_ge(h_ready[0], b + 1)
                    wait(pe, y_ready, b)
                    for k, bank in enumerate((K, V, R)):
                        pe.matmul(bank, Wmix[:, 2 * k, :], hp[:, 1:T + 1], start=True, stop=False)
                        pe.matmul(bank, Wmix[:, 2 * k + 1, :], hp[:, 0:T], start=False, stop=True).then_inc(kvr_filled, 1)
                if mlp:
                    pe.wait_ge(xn_ready[1], b)
                    turn(PB, lambda n: xn[1][:, n, :], turned[1])
                    pe.wait_ge(h_ready[1], b)
                    wait(pe, yo_ready, b - 1)
                    pe.matmul(S, Win2[:].rearrange("p q m -> p (q m)"), h2[:], start=True, stop=True).then_inc(s_filled, 1)
                    wait(pe, mlp_chain, 2 * (b - 1))
                    for p in range(HP):
                        pe.wait_ge(relu_ready, HP * (b - 1) + p + 1)
                        pe.matmul(O2, Wc[:, p, :], r[p % RR][:], start=(p == 0), stop=(p == HP - 1)).then_inc(relu_used, 1)
                if mix:
                    pe.wait_ge(y_ready, b + 1)
                    wait(pe, xm_ready, b)
                    pe.matmul(O, WoR[:], y[:], start=True, stop=True).then_inc(o_filled, 1)
                if mlp:
                    pe.wait_ge(mlp_chain, 2 * b)
                    pe.wait_ge(s_ready, b)
                    turn(S, lambda n: xo[:, cols(n)], xo_turned)

            pe.wait_ge(init_done, 6)
            steps(pe, step)

        @block.scalar
        def _(act):
            act.wait_ge(init_done, 6)

            def step(b, par, mix, mlp):
                if mix:
                    wait(act, xm_ready, b)
                    act.activation(xc[:], xT[:, b, :], ACT.Copy).then_inc(xc_ready, 1)
                    act.wait_ge(turned[0], 2 * b + 2)
                    wait(act, kvr_filled, 3 * b)
                    act.activation(hp[:, 1:T + 1], PB, ACT.Identity, bias=mod[:, SHIFT, one(b)],
                                   scale=mod[:, SCALE1, one(b)]).then_inc(h_ready[0], 1)
                if mix:
                    act.wait_ge(kvr_filled, 3 * b + 3)
                    wait(act, scan_chain, CH * b)
                    act.activation(thr[:], R, ACT.Tanh, scale=0.5).then_inc(th_ready, 1)
                if mlp:
                    act.wait_ge(turned[1], 2 * b)
                    wait(act, s_filled, b - 1)
                    act.activation(h2[:], PB, ACT.Identity, bias=mod[:, 3 + SHIFT, one(b - 1)],
                                   scale=mod[:, 3 + SCALE1, one(b - 1)]).then_inc(h_ready[1], 1)
                    act.wait_ge(s_filled, b)
                    act.activation(s[:], S, ACT.Identity, bias=col("bin")).then_inc(s_ready, 1)
                    act.wait_ge(s_ready, b)

                def relu(p):
                    n = HP * (b - 1) + p
                    if p < RR:
                        wait(act, relu_used, HP * (b - 1) - RR + p + 1)
                    else:
                        act.wait_ge(relu_used, HP * (b - 1) + (p - RR + 1))
                    act.activation(r[p % RR][:], s[:], ACT.Relu, bias=b1p[:, p:p + 1],
                                   scale=w1p[:, p:p + 1]).then_inc(relu_ready, 1)

                if mlp:
                    for p in range(RR):
                        relu(p)
                if mix:
                    act.wait_ge(scan_chain, CH * b + 3)
                    wait(act, scan_chain, CH * b)
                    act.activation(ex[:, 0:2, :], arg[:, 0:2, :], ACT.Exp).then_inc(ex_ready, 1)
                    act.wait_ge(pool_done, 3 * b + 1)
                    act.wait_ge(scan_chain, CH * b + 5)
                    act.activation(ex[:, 2:4, :], arg[:, 2:4, :], ACT.Exp).then_inc(ex_ready, 1)
                if mlp:
                    for p in range(RR, HP):
                        relu(p)
                    act.wait_ge(xo_turned, b)
                    if not isinstance(b, int) or b >= 3:
                        act.wait_ge(stored, 16 * (b - 2))
                    act.activation(y_out[1 - par][:].rearrange("p n f -> p (n f)"), S, ACT.Copy).then_inc(yo_ready, 1)

            steps(act, step)

        @block.vector
        def _(dve):
            dve.memset(ones[:], 1.0).then_inc(init_done, 1)
            dve.wait_ge(init_done, 5)
            dve.tensor_scalar(tdB[:], ones[:], col("ntd"), None, ALU.mult).then_inc(init_done, 1)
            dve.wait_ge(init_done, 6)

            def norm_stats(k, b):
                dve.wait_ge(turned[k], 2 * b + 1)
                for n in range(NB):
                    dve.bn_stats(stats[k][:, n, :], PA[:, n * P:(n + 1) * P]).then_inc(stats_chain[k], 1)
                dve.wait_ge(stats_chain[k], 2 * NB * b + NB)
                wait(dve, rstd_chain[k], 2 * b)
                wait_apart(dve, xn_ready[k], b, passed)
                for n in range(NB):
                    dve.bn_aggr(mv[k][:, n, :], stats[k][:, n, :]).then_inc(stats_chain[k], 1)

            def normalize(k, b):
                dve.wait_ge(rstd_chain[k], 2 * b + 2)
                dve.wait_ge(stats_chain[k], 2 * NB * (b + 1))
                wait(dve, turned[k], 2 * b)
                for n in range(NB):
                    last = dve.tensor_scalar(xn[k][:, n, :], PA[:, n * P:(n + 1) * P], mv[k][:, n, 0:1],
                                             rstd[k][:, n:n + 1], ALU.subtract, ALU.mult)
                last.then_inc(xn_ready[k], 1)

            def step(b, par, mix, mlp_too):
                def link(ins, n):
                    ins.then_inc(scan_chain, 1)

                def after(n):
                    dve.wait_ge(scan_chain, CH * b + n)

                if mix:
                    norm_stats(0, b)
                    normalize(0, b)
                if mlp_too:
                    norm_stats(1, b - 1)
                    normalize(1, b - 1)
                if mix:
                    before, now = slice(0, T), slice(1, T + 1)
                    dve.wait_ge(kvr_filled, 3 * b + 3)
                    wait(dve, pool_done, 3 * b)
                    wait(dve, ex_ready, 2 * b)
                    link(dve.tensor_tensor_scan(mx[:, now], tdB[:], K, TINY_MX, ALU.add, ALU.max), 1)
                    after(1)
                    link(dve.scalar_tensor_tensor(arg[:, 0, :], mx[:, before], col("ntd"), mx[:, now],
                                                  ALU.add, ALU.subtract), 2)
                    link(dve.tensor_tensor(arg[:, 1, :], K, mx[:, now], ALU.subtract), 3)
                    link(dve.scalar_tensor_tensor(mo[:], K, col("tf"), mx[:, before], ALU.add, ALU.max), 4)
                    after(4)
                    link(dve.scalar_tensor_tensor(arg[:, 3, :], K, col("tf"), mo[:], ALU.add, ALU.subtract), 5)
                    dve.wait_ge(ex_ready, 2 * b + 1)
                    link(dve.tensor_tensor(e2v[:], ex[:, 1, :], V, ALU.mult), 6)
                    after(6)
                    link(dve.tensor_tensor_scan(num[:, now], ex[:, 0, :], e2v[:], 0.0, ALU.mult, ALU.add), 7)
                    link(dve.tensor_tensor_scan(den[:, now], ex[:, 0, :], ex[:, 1, :], 0.0, ALU.mult, ALU.add), 8)
                    dve.wait_ge(ex_ready, 2 * b + 2)
                    link(dve.tensor_tensor(n2[:], ex[:, 3, :], V, ALU.mult), 9)
                if mlp_too:
                    dve.wait_ge(relu_used, HP * b)
                    dve.tensor_scalar(mlp[:], O2, col("cst"), mod[:, 3 + GATE, one(b - 1)], ALU.add,
                                      ALU.mult).then_inc(mlp_chain, 1)
                    dve.wait_ge(mlp_chain, 2 * (b - 1) + 1)
                    wait(dve, xo_turned, b - 1)
                    dve.tensor_tensor(xo[:], mlp[:], xm[1 - par][:], ALU.add).then_inc(mlp_chain, 1)
                if mix:
                    dve.wait_ge(pool_done, 3 * b + 3)
                    after(9)
                    link(dve.tensor_tensor(denom[:], d1[:], ex[:, 3, :], ALU.add), 10)
                    link(dve.tensor_tensor(numer[:], n1[:], n2[:], ALU.add), 11)
                    after(10)
                    link(dve.reciprocal(recd[:], denom[:]), 12)
                    after(11)
                    dve.wait_ge(th_ready, b + 1)
                    link(dve.scalar_tensor_tensor(ry[:], thr[:], 1.0, numer[:], ALU.add, ALU.mult), 13)
                    after(13)
                    wait(dve, o_filled, b)
                    dve.scalar_tensor_tensor(y[:], ry[:], 0.5, recd[:], ALU.mult, ALU.mult).then_inc(y_ready, 1)
                    dve.wait_ge(o_filled, b + 1)
                    dve.scalar_tensor_tensor(xm[par][:], O, mod[:, GATE, one(b)], xc[:], ALU.mult,
                                             ALU.add).then_inc(xm_ready, 1)

            steps(dve, step)


_INS = ["L0_attn_x", "L0_attn_Wq", "L0_attn_bq", "L0_attn_Wk", "L0_attn_bk", "L0_attn_Wv", "L0_attn_bv",
        "L0_attn_Wo", "L0_attn_bo", "L0_attn_Wq_lsr", "L0_attn_Wk_lsr", "L0_ffn_ln_w", "L0_ffn_ln_b",
        "L0_ffn_router_w", "L0_ffn_gate_w", "L0_ffn_up_w", "L0_ffn_down_w", "L0_ffn_sh_gate",
        "L0_ffn_sh_up", "L0_ffn_sh_down", "L0_c", "L0_wmod", "L1_attn_Wk", "L1_attn_Wv", "L1_attn_Wr",
        "L1_attn_Wo", "L1_attn_time_decay", "L1_attn_time_first", "L1_attn_time_mix_key",
        "L1_attn_time_mix_value", "L1_attn_time_mix_receptance", "L1_ffn_Win", "L1_ffn_bin_", "L1_ffn_W1",
        "L1_ffn_b1", "L1_ffn_W2", "L1_ffn_b2", "L1_ffn_Wout", "L1_ffn_bout", "L1_c", "L1_wmod"]


def kernel(**inputs):
    import numpy as _np
    import concourse.bacc as _bacc
    from concourse import mybir as _mybir
    from concourse.bass_utils import run_bass_kernel_spmd as _run

    nc = _bacc.Bacc("TRN2", target_bir_lowering=False, num_devices=1)
    arrays, args = {}, {}
    for name in _INS:
        x = _np.ascontiguousarray(inputs[name])
        arrays[f"in_{name}_dram"] = x
        args[name] = nc.dram_tensor(f"in_{name}_dram", x.shape, _mybir.dt.from_np(x.dtype), kind="ExternalInput").ap()
    y = nc.dram_tensor("out_dram", (B, T, D), F32, kind="ExternalOutput").ap()
    adaln_kernel(nc, args, y)
    r = _run(nc, [arrays], core_ids=[0])
    return r.results[0]["out_dram"]
```

```python
from contextlib import ExitStack

import concourse.bass as bass
from concourse import mybir

F32 = mybir.dt.float32
BF16 = mybir.dt.bfloat16
ALU = mybir.AluOpType
ACT = mybir.ActivationFunctionType
AX_X = mybir.AxisListType.X

P = 128
D = 128
B, T = 8, 512
NB = T // P
H, DH, RANK = 16, 8, 32
HG = 4
NG = H // HG
NPART = 3
MAX_ROW = 96
E, HID = 8, 256
HC = HID // P
M, INNER = 64, 16
HP = INNER // 2
EPS = 1e-5
NEG = -1.0e30
SCALE = 1.0 / RANK ** 0.5
TINY_MX = -1.0e38
GATE_MIN = 0.25
TWO_BF16_ONES = 0x3F803F80
BLOCKS = B * NB
GROUP = 8
TILES = GROUP * (-(-(BLOCKS + E - 1) // GROUP))

SHIFT, SCALE1, GATE = 0, 1, 2


def wait(eng, sem, value):
    if not (isinstance(value, int) and value <= 0):
        eng.wait_ge(sem, value)


def wait_apart(eng, sem, value, passed):
    if isinstance(value, int):
        wait(eng, sem, value)
    else:
        eng.wait_ge(sem, value)
        eng.sem_inc(passed, 1)


def adaln_kernel(nc, a, out):
    with ExitStack() as ctx:
        build(nc, ctx, a, out)


def build(nc, ctx, a, out):
    def sb(name, shape, dt=F32, c=ctx):
        return c.enter_context(nc.sbuf_tensor(name, shape, dt))

    def sem(name):
        return ctx.enter_context(nc.semaphore(name))

    ps = ctx.enter_context(nc.psum_tensor("ps", [P, 8, 512], F32))

    xT = sb("xT", [D, B, T])
    ident = sb("ident", [P, P])
    identb = sb("identb", [P, P], BF16)
    neghalf = sb("neghalf", [P, NB])
    mod = [sb(f"mod{l}", [D, 6, B]) for l in range(2)]
    NAMES = ["bq", "bk", "bv", "bo", "ln_w", "ln_b", "td", "tf", "mk", "mv", "mr", "bout",
             "bin", "b2", "bqP", "bkP", "bo2", "cst", "ntd"]
    vec = sb("vec", [P, len(NAMES)])

    def col(name):
        i = NAMES.index(name)
        return vec[:, i:i + 1]

    WqP = sb("WqP", [D, DH, H])
    WkP = sb("WkP", [D, DH, H])
    WvT = sb("WvT", [D, D])
    WoT = sb("WoT", [D, D])
    gab = sb("gab", [D, B])
    gcst = sb("gcst", [D, B])
    shg_w = sb("shg_w", [D, HID])
    shu_w = sb("shu_w", [D, HID])
    shd_w = sb("shd_w", [P, HC, D])
    router_w = sb("router_w", [D, E])
    Wmix = sb("Wmix", [D, 6, D])
    WoR = sb("WoR", [D, D])
    Win2 = sb("Win2", [D, 2, M])
    Wc = sb("Wc", [P, HP, D])
    w1p = sb("w1p", [P, HP])
    b1p = sb("b1p", [P, HP])

    stacks = ctx.enter_context(ExitStack())
    Qs = [sb(f"Qs{p}", [P, H, T], BF16, stacks) for p in range(2)]
    Ks = [sb(f"Ks{p}", [P, H, T], BF16, stacks) for p in range(2)]
    x_in = [sb(f"x_in{p}", [P, NB, D], F32, stacks) for p in range(2)]
    x_loaded = sem("x_loaded")
    setup(nc, a, Qs, Ks, x_in, x_loaded, sb, sem, ps, xT, ident, identb, neghalf, mod, col, WqP, WkP, WvT, WoT, gab, gcst,
          shg_w, shu_w, shd_w, router_w, Wmix, WoR, Win2, Wc, w1p, b1p)
    with ExitStack() as c:
        attention(nc, a, lambda n, s, dt=F32: sb(n, s, dt, c), sem, ps, xT, ident, identb, neghalf,
                  mod[0], col, WqP, WkP, WvT, WoT, gab, Qs, Ks, x_in, x_loaded)
    stacks.close()
    pos_i = sb("pos_i", [P, BLOCKS], mybir.dt.int32)
    sorted_out = nc.dram_tensor("sorted_out", (TILES * P, D), F32, kind="Internal").ap()
    with ExitStack() as c:
        moe(nc, lambda n, s, dt=F32: sb(n, s, dt, c), sem, ps, xT, ident, neghalf, mod[0], col, a,
            shg_w, shu_w, shd_w, router_w, pos_i, sorted_out)
    with ExitStack() as c:
        mixing(nc, out, lambda n, s, dt=F32: sb(n, s, dt, c), sem, ps, xT, ident, neghalf, mod[0],
               mod[1], col, Wmix, WoR, Win2, Wc, w1p, b1p, gcst, pos_i, sorted_out)


def setup(nc, a, Qs, Ks, x_in, x_loaded, sb0, sem, ps, xT, ident, identb, neghalf, mod, col, WqP, WkP, WvT, WoT, gab, gcst,
          shg_w, shu_w, shd_w, router_w, Wmix, WoR, Win2, Wc, w1p, b1p):
    with ExitStack() as c:
        def sb(name, shape, dt=F32):
            return sb0(name, shape, dt, c)

        raw = sb("raw", [P, 4, D])
        identP = sb("identP", [P, DH, H])
        lsr = sb("lsr", [P, 2, RANK])
        lsrT = sb("lsrT", [RANK, 2, P])
        bdmask = sb("bdmask", [P, H, DH])
        BD = sb("BD", [P, DH, H])
        c_in = sb("c_in", [B, 2, D])
        cT = sb("cT", [D, 2, B])
        th = sb("th", [D, 2, B])
        scT = sb("scT", [D, 2, B])
        wmod = sb("wmod", [D, 2, 6 * D])
        gtmp = sb("gtmp", [D, 2, 2, B])
        gabs = sb("gabs", [D, 2, 2, B])
        mixw = sb("mixw", [D, 3, D])
        omm = sb("omm", [D, 3])
        Wout2 = sb("Wout2", [P, D])
        w2p = sb("w2p", [P, HP])
        inner = sb("inner", [P, 3, INNER])
        units_loaded = sem("units_loaded")
        small_loaded, weights_loaded, moe_loaded = sem("small_loaded"), sem("weights_loaded"), sem("moe_loaded")
        stacks_zero = [sem(f"stacks_zero{p}") for p in range(2)]
        consts_ready, turned, folded, copied = sem("consts_ready"), sem("turned"), sem("folded"), sem("copied")
        tanh_ready, td_ready = sem("tanh_ready"), sem("td_ready")

        def column(name):
            return a[name].rearrange("(p o) -> p o", o=1)

        smalls = [(col("bq"), column("L0_attn_bq")), (col("bk"), column("L0_attn_bk")),
                  (col("bv"), column("L0_attn_bv")), (col("bo"), column("L0_attn_bo")),
                  (col("ln_w"), column("L0_ffn_ln_w")), (col("ln_b"), column("L0_ffn_ln_b")),
                  (col("td"), column("L1_attn_time_decay")), (col("tf"), column("L1_attn_time_first")),
                  (col("mk"), column("L1_attn_time_mix_key")), (col("mv"), column("L1_attn_time_mix_value")),
                  (col("mr"), column("L1_attn_time_mix_receptance")), (col("bout"), column("L1_ffn_bout")),
                  (c_in[:, 0, :], a["L0_c"]), (c_in[:, 1, :], a["L1_c"]),
                  (lsr[:, 0, :], a["L0_attn_Wq_lsr"].rearrange("h d r -> (h d) r")),
                  (lsr[:, 1, :], a["L0_attn_Wk_lsr"].rearrange("h d r -> (h d) r"))]
        unit_smalls = []
        for q in range(2):
            half = slice(M * q, M * (q + 1))
            unit_smalls += [(col("bin")[half, :], column("L1_ffn_bin_")), (col("b2")[half, :], column("L1_ffn_b2"))]
            for k, name in enumerate(("L1_ffn_W1", "L1_ffn_b1", "L1_ffn_W2")):
                unit_smalls.append((inner[half, k, :], a[name]))
            unit_smalls += [(Wout2[half, :], a["L1_ffn_Wout"]), (Win2[:, q, :], a["L1_ffn_Win"])]
        bigs = [(raw[:, 0, :], a["L0_attn_Wq"]), (raw[:, 1, :], a["L0_attn_Wk"]),
                (raw[:, 2, :], a["L0_attn_Wv"]), (raw[:, 3, :], a["L0_attn_Wo"]),
                (wmod[:, 0, :], a["L0_wmod"]), (wmod[:, 1, :], a["L1_wmod"]),
                (mixw[:, 0, :], a["L1_attn_Wk"]), (mixw[:, 1, :], a["L1_attn_Wv"]),
                (mixw[:, 2, :], a["L1_attn_Wr"]), (WoR[:, :], a["L1_attn_Wo"])]
        moes = [(shg_w[:, :], a["L0_ffn_sh_gate"]), (shu_w[:, :], a["L0_ffn_sh_up"]),
                (shd_w[:, :, :], a["L0_ffn_sh_down"].rearrange("(c p) f -> p c f", p=P)),
                (router_w[:, :], a["L0_ffn_router_w"])]
        NSMALL, NBIG, NMOE = 16 * len(smalls), 16 * len(bigs), 16 * len(moes)

        def clear(eng, p):
            for stack in (Qs[p], Ks[p]):
                eng.memset(stack[:].rearrange("p h t -> p (h t)").bitcast(mybir.dt.uint32), 0).then_inc(stacks_zero[p], 1)
            eng.wait_ge(stacks_zero[p], 2)
            eng.memset(Ks[p][MAX_ROW:MAX_ROW + NPART, :, :].rearrange("p h t -> p (h t)").bitcast(mybir.dt.uint32),
                       TWO_BF16_ONES).then_inc(stacks_zero[p], 1)

        with nc.Block() as block:
            @block.sync
            def _(sp):
                for dst, src in bigs:
                    sp.dma_start(dst, src).then_inc(weights_loaded, 16)
                for dst, src in moes:
                    sp.dma_start(dst, src).then_inc(moe_loaded, 16)
                for b in range(2):
                    sp.dma_start(x_in[b][:], a["L0_attn_x"][b].rearrange("(n p) f -> p n f", p=P)).then_inc(x_loaded, 16)
                    sp.wait_ge(x_loaded, 16 * (b + 1))
                sp.wait_ge(moe_loaded, NMOE)

            @block.gpsimd
            def _(pool):
                pool.memset(ident[:], 0.0).then_inc(consts_ready, 1)
                pool.memset(bdmask[:], 1.0).then_inc(consts_ready, 1)
                pool.memset(neghalf[:], -0.5).then_inc(consts_ready, 1)
                pool.wait_ge(consts_ready, 3)
                pool.affine_select(out=ident[:], in_=ident[:], compare_op=ALU.not_equal, fill=1.0, base=0,
                                   pattern=[[-1, P]], channel_multiplier=1).then_inc(consts_ready, 1)
                pool.affine_select(out=bdmask[:], in_=bdmask[:], compare_op=ALU.is_ge, fill=0.0, base=0,
                                   pattern=[[-DH, H], [0, DH]], channel_multiplier=1).then_inc(consts_ready, 1)
                pool.wait_ge(consts_ready, 5)
                pool.affine_select(out=bdmask[:], in_=bdmask[:], compare_op=ALU.is_ge, fill=0.0, base=DH - 1,
                                   pattern=[[DH, H], [0, DH]], channel_multiplier=-1).then_inc(consts_ready, 1)
                pool.tensor_copy(identP[:].rearrange("p d h -> p h d"),
                                 ident[:].rearrange("p (h d) -> p h d", d=DH)).then_inc(consts_ready, 1)
                for dst, src in unit_smalls:
                    pool.dma_start(dst, src).then_inc(units_loaded, 16)
                clear(pool, 1)

            @block.tensor
            def _(pe):
                pe.wait_ge(consts_ready, 7)
                pe.wait_ge(small_loaded, NSMALL)
                for k in range(2):
                    pe.transpose(ps[0:RANK, 0, k * P:(k + 1) * P], lsr[:, k, :], ident[:])
                    pe.transpose(ps[:, 0, 256 + k * B:256 + (k + 1) * B], c_in[:, k, :], ident[0:B, 0:B])
                pe.matmul(ps[:, 0, 300:301], identP[:].rearrange("p d h -> p (d h)"), col("bk"),
                          start=True, stop=True).then_inc(turned, 1)
                pe.wait_ge(weights_loaded, NBIG)
                for k in range(3):
                    last = pe.transpose(ps[:, 1, k * P:(k + 1) * P], raw[:, k + 1, :], ident[:])
                last.then_inc(turned, 1)
                pe.wait_ge(copied, 1)
                pe.matmul(ps[:, 2, 0:P], lsrT[:, 0, :], lsrT[:, 1, :], start=True, stop=True).then_inc(folded, 1)
                pe.wait_ge(copied, 2)
                pe.matmul(ps[:, 3, 0:1], WoT[:], col("bv"), start=True, stop=True)
                pe.wait_ge(units_loaded, 16 * len(unit_smalls))
                pe.matmul(ps[:, 3, 2:3], Wout2[0:M, :], col("b2")[0:M, :],
                          start=True, stop=True).then_inc(folded, 1)
                pe.wait_ge(copied, 3)
                for l in range(2):
                    for j in range(6):
                        last = pe.matmul(ps[:, 4 + l, j * B:(j + 1) * B], wmod[:, l, j * D:(j + 1) * D],
                                         scT[:, l, :], start=True, stop=True)
                last.then_inc(folded, 1)
                pe.wait_ge(copied, 4)
                pe.matmul(ps[:, 6, 0:P], raw[:, 0, :], BD[:].rearrange("p d h -> p (d h)"), start=True, stop=True)
                pe.matmul(ps[:, 6, P:P + 1], BD[:].rearrange("p d h -> p (d h)"), col("bq"),
                          start=True, stop=True).then_inc(folded, 1)

            @block.scalar
            def _(act):
                for dst, src in smalls:
                    act.dma_start(dst, src).then_inc(small_loaded, 16)
                act.wait_ge(small_loaded, NSMALL)
                act.activation(col("ntd"), col("td"), ACT.Exp).then_inc(td_ready, 1)
                act.wait_ge(turned, 1)
                act.activation(th[:].rearrange("p l b -> p (l b)"), ps[:, 0, 256:256 + 2 * B], ACT.Tanh,
                               scale=0.5).then_inc(tanh_ready, 1)

            @block.vector
            def _(dve):
                clear(dve, 0)
                dve.wait_ge(consts_ready, 7)
                dve.tensor_copy(identb[:], ident[:]).then_inc(td_ready, 1)
                dve.wait_ge(turned, 1)
                dve.wait_ge(tanh_ready, 1)
                dve.tensor_copy(lsrT[:].rearrange("p k n -> p (k n)"), ps[0:RANK, 0, 0:256]).then_inc(copied, 1)
                dve.scalar_tensor_tensor(scT[:].rearrange("p l b -> p (l b)"), th[:].rearrange("p l b -> p (l b)"),
                                         1.0, ps[:, 0, 256:256 + 2 * B], ALU.add, ALU.mult).then_inc(td_ready, 1)
                dve.tensor_copy(col("bkP"), ps[:, 0, 300:301])
                dve.wait_ge(turned, 2)
                dve.tensor_copy(WkP[:].rearrange("p d h -> p h d"),
                                ps[:, 1, 0:P].rearrange("p (h d) -> p h d", d=DH))
                dve.tensor_copy(WvT[:], ps[:, 1, P:2 * P])
                dve.tensor_copy(WoT[:], ps[:, 1, 2 * P:3 * P]).then_inc(copied, 1)
                dve.wait_ge(td_ready, 3)
                dve.tensor_scalar(scT[:], scT[:], 0.5, None, ALU.mult).then_inc(copied, 1)
                dve.wait_ge(folded, 1)
                dve.scalar_tensor_tensor(BD[:].rearrange("p d h -> p h d"),
                                         ps[:, 2, 0:P].rearrange("p (h d) -> p h d", d=DH), SCALE, bdmask[:],
                                         ALU.mult, ALU.mult).then_inc(copied, 1)
                dve.tensor_scalar(col("ntd"), col("ntd"), -1.0, None, ALU.mult)
                for k, m in enumerate(("mk", "mv", "mr")):
                    dve.tensor_scalar(omm[:, k:k + 1], col(m), -1.0, 1.0, ALU.mult, ALU.add).then_inc(td_ready, 1)
                dve.wait_ge(units_loaded, 16 * len(unit_smalls))
                for k, dst in enumerate((w1p, b1p, w2p)):
                    for q in range(2):
                        half = slice(M * q, M * (q + 1))
                        dve.tensor_copy(dst[half, :], inner[half, k, :].rearrange("m (p q) -> m q p", q=2)[:, q, :]).then_inc(td_ready, 1)
                dve.wait_ge(td_ready, 12)
                for k, m in enumerate(("mk", "mv", "mr")):
                    dve.tensor_scalar(Wmix[:, 2 * k, :], mixw[:, k, :], col(m), None, ALU.mult)
                    dve.tensor_scalar(Wmix[:, 2 * k + 1, :], mixw[:, k, :], omm[:, k:k + 1], None, ALU.mult)
                for p in range(HP):
                    dve.tensor_scalar(Wc[:, p, :], Wout2[:], w2p[:, p:p + 1], None, ALU.mult)
                dve.wait_ge(folded, 2)
                dve.tensor_tensor(col("cst"), col("bout"), ps[:, 3, 2:3], ALU.add)
                dve.tensor_tensor(col("bo2"), col("bo"), ps[:, 3, 0:1], ALU.add).then_inc(td_ready, 1)
                dve.wait_ge(folded, 3)
                for l in range(2):
                    dve.tensor_copy(mod[l][:].rearrange("p j b -> p (j b)"), ps[:, 4 + l, 0:6 * B]).then_inc(td_ready, 1)
                dve.wait_ge(td_ready, 15)
                for l in range(2):
                    for s in range(2):
                        g = mod[l][:, 3 * s + GATE, :]
                        dve.tensor_scalar(mod[l][:, 3 * s + SCALE1, :], mod[l][:, 3 * s + SCALE1, :], 1.0, None, ALU.add)
                        dve.tensor_scalar(gtmp[:, l, s, :], g, 0.0, 2.0, ALU.is_ge, ALU.mult)
                        dve.tensor_scalar(gabs[:, l, s, :], g, -1.0, None, ALU.mult).then_inc(td_ready, 1)
                dve.wait_ge(td_ready, 19)
                for l in range(2):
                    for s in range(2):
                        dve.tensor_tensor(gabs[:, l, s, :], gabs[:, l, s, :], mod[l][:, 3 * s + GATE, :],
                                          ALU.max).then_inc(td_ready, 1)
                dve.wait_ge(td_ready, 23)
                dve.tensor_scalar(gabs[:], gabs[:], GATE_MIN, None, ALU.max).then_inc(td_ready, 1)
                dve.wait_ge(td_ready, 24)
                for l in range(2):
                    for s in range(2):
                        dve.scalar_tensor_tensor(mod[l][:, 3 * s + GATE, :], gtmp[:, l, s, :], -1.0,
                                                 gabs[:, l, s, :], ALU.add, ALU.mult).then_inc(td_ready, 1)
                dve.wait_ge(td_ready, 28)
                dve.tensor_scalar(gab[:], mod[0][:, GATE, :], col("bo2"), None, ALU.mult)
                dve.tensor_scalar(gcst[:], mod[1][:, 3 + GATE, :], col("cst"), None, ALU.mult)
                dve.wait_ge(folded, 4)
                dve.tensor_copy(WqP[:].rearrange("p d h -> p (d h)"), ps[:, 6, 0:P])
                dve.tensor_copy(col("bqP"), ps[:, 6, P:P + 1]).then_inc(td_ready, 1)


def attention(nc, a, sb, sem, ps, xT, ident, identb, neghalf, mod, col, WqP, WkP, WvT, WoT, gab, Qs, Ks,
              x_in, x_loaded):
    xn = sb("xn", [P, NB, D])
    hT = sb("hT", [D, T])
    mv = sb("mv_a", [P, NB, 2])
    stats = sb("stats_a", [P, NB, 6])
    rstd = sb("rstd_a", [P, NB])
    full = sb("full", [P, T])
    rest = sb("rest", [P, T])
    part = sb("part", [P, 2, NPART, T], BF16)
    V = [sb(f"V{p}", [P, NB, D]) for p in range(2)]
    Vg = [sb(f"Vg{p}", [P, NB, HG, 32]) for p in range(2)]
    mask4 = sb("mask4", [P, HG, P], BF16)
    maskT = sb("maskT", [P, 2, P], BF16)
    mask_f = sb("mask_f", [P, P])
    nmax = [sb(f"nmax{p}", [P, NB, HG]) for p in range(2)]
    nrest = sb("nrest", [P, NB, HG])
    npart_wide = sb("npart", [P, NB, P], BF16)
    npart = npart_wide[:, :, 0:NPART * HG].rearrange("p n (k h) -> p n k h", k=NPART)
    nmT = [sb(f"nmT{p}", [NPART * HG, T], BF16) for p in range(2)]
    zeros = sb("zeros_a", [NPART * HG, T], BF16)
    PR = [sb(f"PR{p}", [P, HG, 1280]) for p in range(2)]
    yT = [sb(f"yT{p}", [P, T]) for p in range(2)]
    rec = sb("rec", [P, NB, HG])
    yn = [sb(f"yn{p}", [P, NB, H, DH]) for p in range(2)]
    ynT = sb("ynT", [D, T])
    SEG = {0: (0, 512), 1: (512, 384), 3: (896, 128), 2: (1024, 256)}
    parts_out = [nc.dram_tensor(f"qk_parts{p}", (2, NPART, P, T), BF16, kind="Internal").ap() for p in range(2)]

    A = [ps[:, 0:2, :], ps[:, 2:4, :]]
    X2 = [ps[:, 4, :], ps[:, 5, :]]
    WIDE = X2 + [ps[:, k, :] for k in range(4)]
    Y, C = ps[:, 6, :], ps[:, 7, :]

    parts_stored = sem("parts_stored")
    qk_loaded, nm_moved = sem("qk_loaded"), sem("nm_moved")
    init_done, mask_done = sem("init_done"), sem("mask_done")
    stats_chain, pool_chain, xn_ready = sem("stats_chain"), sem("pool_chain"), sem("xn_ready")
    xt_filled, xt_copied, ht_filled, ht_ready = sem("xt_filled"), sem("xt_copied"), sem("ht_filled"), sem("ht_ready")
    qk_filled, v_filled, v_copied = sem("qk_filled"), sem("v_filled"), sem("v_copied")
    full_ready, rest_ready, part1_ready, split_done = sem("full_ready"), sem("rest_ready"), sem("part1_ready"), sem("split_done")
    s1_filled, max_taken, s2_filled, exp_done = sem("s1_filled"), sem("max_taken"), sem("s2_filled"), sem("exp_done")
    vg_ready, pv_done, y_copied = sem("vg_ready"), sem("pv_done"), sem("y_copied")
    nm_chain, nm_filled, nm_copied = sem("nm_chain"), sem("nm_filled"), sem("nm_copied")
    yt_filled, rec_ready, yn_ready = sem("yt_filled"), sem("rec_ready"), sem("yn_ready")
    ynt_filled, ynt_ready, o_filled, x_done = sem("ynt_filled"), sem("ynt_ready"), sem("o_filled"), sem("x_done")
    passed = sem("a_passed")

    INIT = 6
    RING = 2
    LOADS = 16 * (2 * NPART + 1)

    ORDER = "22P122S122S122S122S11"
    UNITS1 = [(0, range(0, 4), 4), (1, range(0, 4), 2), (2, range(0, 2), 1), (2, range(2, 4), 1),
              (3, range(0, 2), 1), (3, range(2, 4), 1)]
    UNITS2 = []
    for h0 in (0, 2):
        for h in (h0, h0 + 1):
            UNITS2 += [[(h, 0, 0)], [(h, 1, 0), (h, 3, 384)]]
        UNITS2.append([(h0, 2, 0), (h0 + 1, 2, 256)])
    N1, N2 = len(UNITS1), len(UNITS2)

    def x_bank(b, g, u):
        if isinstance(b, int) and b == B - 1:
            return WIDE[(N2 * g + u) % len(WIDE)]
        return X2[u % 2]

    def s1_banks(u):
        ib, heads, per = UNITS1[u]
        n = (ib + 1) * P
        banks = A[u % 2][:, 0:len(heads) // per, :]
        return banks[:, :, 0:n * per].rearrange("p k (h n) -> p k h n", h=per)

    def one(b):
        return slice(b, b + 1) if isinstance(b, int) else bass.ds(b, 1)

    def within(b, lo, hi=B - 1):
        return not isinstance(b, int) or lo <= b <= hi

    def all_groups(eng, group):
        for b in (-1, 0, 1):
            for g in range(NG):
                group(b, g, b % 2)
        with eng.Fori(1, B // 2 - 1) as i:
            for par in range(2):
                for g in range(NG):
                    group(2 * i + par, g, par)
        for b in (B - 2, B - 1):
            for g in range(NG):
                group(b, g, b % 2)

    with nc.Block() as block:
        @block.sync
        def _(sp):
            def load_x(b, par):
                wait_apart(sp, xt_filled, b - 1, passed)
                wait_apart(sp, xn_ready, b - 1, passed)
                wait_apart(sp, x_loaded, 16 * b, passed)
                src = a["L0_attn_x"][b] if isinstance(b, int) else a["L0_attn_x"][bass.ds(b, 1)].rearrange("o t f -> (o t) f")
                sp.dma_start(x_in[par][:], src.rearrange("(n p) f -> p n f", p=P)).then_inc(x_loaded, 16)

            def store_part(k, par):
                sp.dma_start(parts_out[par][k].rearrange("s r t -> r s t"), part[:, k, :, :]).then_inc(parts_stored, 16)

            def store_parts(b, par):
                wait_apart(sp, split_done, 2 * b + 2, passed)
                if within(b, 2):
                    wait_apart(sp, qk_loaded, LOADS * NG * (b - 1), passed)
                for k in range(2):
                    store_part(k, par)

            def load_slots(k, g, par):
                heads = slice(g * HG, (g + 1) * HG)
                flat = parts_out[par][k].rearrange("s (d h) t -> s d (h t)", h=H)[:, :, g * HG * T:(g + 1) * HG * T]
                for i in range(NPART):
                    rows = slice(NPART * DH * i, NPART * DH * (i + 1))
                    src = flat if k else flat[i].unsqueeze(0).to_broadcast([NPART, DH, HG * T])
                    sp.dma_start((Qs, Ks)[k][par][rows, heads, :].rearrange("r h t -> r (h t)"), src).then_inc(qk_loaded, 16)

            def load_zeros(g, par):
                sp.dma_start(Qs[par][MAX_ROW:MAX_ROW + NPART, g * HG:(g + 1) * HG, :], zeros[:]).then_inc(qk_loaded, 16)

            def load_qk(b, g, par):
                t = NG * b + g
                if within(b, 2):
                    wait_apart(sp, s2_filled, N2 * (t - 2 * NG + 1), passed)
                wait_apart(sp, parts_stored, 32 * (b + 1), passed)
                wait_apart(sp, qk_loaded, LOADS * t, passed)
                for k in range(2):
                    load_slots(k, g, par)
                load_zeros(g, par)

            def move_nm(b, g, par):
                t = NG * b + g
                wait_apart(sp, nm_copied, t + 1, passed)
                wait_apart(sp, nm_moved, 16 * t, passed)
                sp.dma_start(Qs[par][MAX_ROW:MAX_ROW + NPART, g * HG:(g + 1) * HG, :], nmT[g % 2][:]).then_inc(nm_moved, 16)

            def group(b, g, par):
                ahead = lambda n: (b + (g + n) // NG, (g + n) % NG, (par + (g + n) // NG) % 2)
                if g == 0 and within(b + 2, 2):
                    load_x(b + 2, par)
                if g == 3 and within(b + 2, 0):
                    store_parts(b + 2, par)
                if within(ahead(3)[0], 0):
                    move_nm(*ahead(3))
                if within(ahead(5)[0], 0):
                    load_qk(*ahead(5))

            sp.wait_ge(init_done, INIT)
            load_zeros(0, 0)
            for k in range(2):
                sp.wait_ge(split_done, k + 1)
                store_part(k, 0)
                sp.wait_ge(parts_stored, 16 * (k + 1))
                load_slots(k, 0, 0)
            all_groups(sp, group)

        @block.gpsimd
        def _(pool):
            def rstd_of(b):
                wait_apart(pool, stats_chain, 2 * NB * (b + 1), passed)
                pool.tensor_scalar(rstd[:], mv[:, :, 1], EPS, None, ALU.add).then_inc(pool_chain, 1)
                pool.wait_ge(pool_chain, 2 * b + 1)
                pool.tensor_tensor(rstd[:], rstd[:], neghalf[:], ALU.pow).then_inc(pool_chain, 1)

            rstd_of(0)
            pool.memset(mask_f[:], 0.0).then_inc(mask_done, 1)
            pool.wait_ge(mask_done, 1)
            pool.affine_select(out=mask_f[:], in_=mask_f[:], compare_op=ALU.is_ge, fill=NEG, base=0,
                               pattern=[[-1, P]], channel_multiplier=1).then_inc(mask_done, 1)
            pool.wait_ge(mask_done, 2)
            for h in range(HG):
                pool.tensor_copy(mask4[:, h, :], mask_f[:]).then_inc(mask_done, 1)
            pool.wait_ge(mask_done, 6)
            pool.memset(mask_f[:], 0.0).then_inc(mask_done, 1)
            pool.wait_ge(mask_done, 7)
            pool.affine_select(out=mask_f[:], in_=mask_f[:], compare_op=ALU.is_ge, fill=NEG, base=0,
                               pattern=[[1, P]], channel_multiplier=-1).then_inc(mask_done, 1)
            pool.wait_ge(mask_done, 8)
            for h in range(2):
                pool.tensor_copy(maskT[:, h, :], mask_f[:]).then_inc(mask_done, 1)

            with pool.Fori(1, B) as b:
                rstd_of(b)

        @block.tensor
        def _(pe):
            def unit1(b, g, par, u):
                ib, heads, per = UNITS1[u]
                n = (ib + 1) * P
                t = NG * b + g
                if u == 0:
                    wait_apart(pe, qk_loaded, LOADS * (t + 1), passed)
                pe.wait_ge(max_taken, N1 * t + (u + 1))
                banks = s1_banks(u)
                for k in range(banks.shape[1]):
                    for j in range(per):
                        h = g * HG + heads[k * per + j]
                        pe.matmul(banks[:, k, j, :], Qs[par][:, h, ib * P:(ib + 1) * P], Ks[par][:, h, 0:n],
                                  start=(j == 0), stop=False, skip_group_check=True)
                    last = pe.matmul(banks[:, k, :, n - P:n], identb[:], mask4[:, 0:per, :],
                                     start=False, stop=True, skip_group_check=True)
                last.then_inc(s1_filled, 1)

            def unit2(b, g, par, u):
                t = NG * b + g
                if u == 0:
                    wait_apart(pe, nm_moved, 16 * (t + 1), passed)
                in_ring = N2 * g + u if isinstance(b, int) and b == B - 1 else 0
                if in_ring < 2:
                    pe.wait_ge(exp_done, N2 * t + (u + 1))
                elif in_ring < len(WIDE):
                    pe.wait_ge(max_taken, RING + N1 * NG * B)
                else:
                    pe.wait_ge(exp_done, N2 * t + (u + 1) - (len(WIDE) - 2))
                bank = x_bank(b, g, u)
                for k, (hh, jb, at) in enumerate(UNITS2[u]):
                    h = g * HG + hh
                    pe.matmul(bank[:, at:at + T - jb * P], Ks[par][:, h, jb * P:(jb + 1) * P],
                              Qs[par][:, h, jb * P:T], start=(k == 0), stop=False, skip_group_check=True)
                ats = [at for _, _, at in UNITS2[u]]
                if len(ats) == 1:
                    last = pe.matmul(bank[:, 0:P], identb[:], maskT[:, 0, :], start=False, stop=True,
                                     skip_group_check=True)
                elif ats[1] == 256:
                    last = pe.matmul(bank.rearrange("p (k n) -> p k n", k=2)[:, :, 0:P], identb[:], maskT[:],
                                     start=False, stop=True, skip_group_check=True)
                else:
                    last = pe.matmul(bank.rearrange("p (k n) -> p k n", k=4)[:, 0:4:3, :], identb[:], maskT[:],
                                     start=False, stop=True, skip_group_check=True)
                last.then_inc(s2_filled, 1)

            def pv(t, odd):
                pe.wait_ge(vg_ready, t + 1)
                pe.wait_ge(exp_done, N2 * (t + 1) + RING)
                if not isinstance(t, int) or t > 0:
                    pe.wait_ge(y_copied, t)
                for jb in range(NB):
                    at, n = SEG[jb]
                    for hh in range(HG):
                        last = pe.matmul(Y[32 * hh:32 * hh + 32, jb * P:T], Vg[odd][:, jb, hh, :], PR[odd][:, hh, at:at + n],
                                         start=(jb == 0), stop=(jb == NB - 1), skip_group_check=True)
                last.then_inc(pv_done, 1)

            reader = [None]

            def take_c(next_reader, value):
                if reader[0]:
                    pe.wait_ge(*reader[0])
                reader[0] = (next_reader, value)

            def turn(src, signal, bank=C, eye=ident):
                for n in range(NB):
                    last = pe.transpose(bank[:, n * P:(n + 1) * P], src(n), eye[:])
                last.then_inc(signal, 1)

            def turn_maxima(t):
                pe.wait_ge(nm_chain, 4 * (t + 1))
                take_c(nm_copied, t + 1)
                turn(lambda n: npart_wide[:, n, :], nm_filled, C.bitcast(BF16), identb)

            def turn_y(t, odd):
                pe.wait_ge(y_copied, t + 1)
                take_c(yn_ready, t + 1)
                turn(lambda n: yT[odd][:, n * P:(n + 1) * P], yt_filled)

            def turn_x(b, par):
                pe.wait_ge(x_loaded, 16 * (b + 1))
                take_c(xt_copied, b + 1)
                turn(lambda n: x_in[par][:, n, :], xt_filled)

            def turn_xn(b):
                pe.wait_ge(xn_ready, b + 1)
                take_c(ht_ready, b + 1)
                turn(lambda n: xn[:, n, :], ht_filled)

            def project(b, k):
                pe.wait_ge(ht_ready, b + 1)
                take_c(full_ready, 4 * b + 2 * k + 2)
                pe.matmul(C, (WqP, WkP)[k][:].rearrange("p d h -> p (d h)"), hT[:], start=True, stop=True).then_inc(qk_filled, 1)

            def project_v(b):
                take_c(v_copied, b + 1)
                for n in range(NB):
                    last = pe.matmul(C[:, n * P:(n + 1) * P], hT[:, n * P:(n + 1) * P], WvT[:], start=True, stop=True)
                last.then_inc(v_filled, 1)

            def turn_yn(b, par):
                pe.wait_ge(yn_ready, NG * (b + 1))
                take_c(ynt_ready, b + 1)
                turn(lambda n: yn[par][:, n, :, :].rearrange("p h d -> p (h d)"), ynt_filled)

            def output(b):
                take_c(x_done, b + 1)
                pe.matmul(C, WoT[:], ynT[:], start=True, stop=True).then_inc(o_filled, 1)

            def slot(b, g, par, n):
                if n == 0:
                    if within(b + (g + 3) // NG, 0):
                        turn_maxima(NG * b + (g + 3))
                elif n == 2:
                    if within(b if g else b - 1, 0):
                        turn_y(NG * b + (g - 1), (g - 1) % 2)
                elif g == 0 and within(b + 2, 0):
                    turn_x(b + 2, par) if n == 1 else turn_xn(b + 2)
                elif g == 1 and within(b + 2, 0):
                    project(b + 2, n // 3)
                elif g == 2 and within(b - 1, 0):
                    turn_yn(b - 1, 1 - par) if n == 1 else output(b - 1)
                elif g == 3 and n == 1 and within(b + 2, 0):
                    project_v(b + 2)

            def group(b, g, par):
                if not isinstance(b, int) and g == 0:
                    reader[0] = (yn_ready, NG * b - 1)
                u1 = u2 = slots = 0
                for kind in ORDER:
                    if kind == "1":
                        if within(b + 1, 0):
                            unit1(b + 1, g, 1 - par, u1)
                        u1 += 1
                    elif kind == "2":
                        if within(b, 0):
                            unit2(b, g, par, u2)
                        u2 += 1
                    elif kind == "P":
                        if within(b if g else b - 1, 0):
                            pv(NG * b + (g - 1), (g - 1) % 2)
                    else:
                        slot(b, g, par, slots)
                        slots += 1

            turn_x(0, 0)
            turn_xn(0)
            project(0, 0)
            project(0, 1)
            project_v(0)
            pe.wait_ge(mask_done, 10)
            pe.wait_ge(init_done, INIT)
            all_groups(pe, group)
            last_t = NG * B - 1
            pv(last_t, last_t % 2)
            turn_y(last_t, last_t % 2)
            turn_yn(B - 1, (B - 1) % 2)
            pe.wait_ge(ynt_ready, B)
            output(B - 1)

        @block.scalar
        def _(act):
            act.sem_inc(exp_done, RING)

            def copy_x(b):
                act.wait_ge(xt_filled, b + 1)
                act.activation(xT[:, b, :], C, ACT.Identity, bias=gab[:, one(b)]).then_inc(xt_copied, 1)

            def copy_h(b):
                act.wait_ge(ht_filled, b + 1)
                if within(b, 1):
                    act.wait_ge(v_filled, b)
                act.activation(hT[:], C, ACT.Identity, bias=mod[:, SHIFT, one(b)],
                               scale=mod[:, SCALE1, one(b)]).then_inc(ht_ready, 1)

            def first_part(b, k):
                act.wait_ge(qk_filled, 2 * b + k + 1)
                bias = col(("bqP", "bkP")[k])
                if within(b, 1) or k:
                    act.wait_ge(rest_ready, 2 * b + k)
                if within(b, 1):
                    act.wait_ge(parts_stored, 32 * b)
                act.activation(full[:], C, ACT.Identity, bias=bias).then_inc(full_ready, 1)
                act.activation(part[:, k, 0, :], C, ACT.Identity, bias=bias).then_inc(full_ready, 1)

            def second_part(b, k):
                act.wait_ge(rest_ready, 2 * b + k + 1)
                act.activation(part[:, k, 1, :], rest[:], ACT.Copy).then_inc(part1_ready, 1)

            def copy_maxima(t, odd):
                act.wait_ge(nm_filled, t + 1)
                if not isinstance(t, int) or t >= 2:
                    act.wait_ge(nm_moved, 16 * (t - 1))
                act.activation(nmT[odd][:], C.bitcast(BF16)[0:NPART * HG, 0:T], ACT.Copy).then_inc(nm_copied, 1)

            def copy_y(t, odd):
                act.wait_ge(pv_done, t + 1)
                if not isinstance(t, int) or t >= 2:
                    act.wait_ge(yt_filled, t - 1)
                act.activation(yT[odd][:], Y, ACT.Copy).then_inc(y_copied, 1)

            def copy_yn(b):
                act.wait_ge(ynt_filled, b + 1)
                if within(b, 1):
                    act.wait_ge(o_filled, b)
                act.activation(ynT[:], C, ACT.Copy).then_inc(ynt_ready, 1)

            def group(b, g, par):
                t = NG * b + g
                odd = g % 2
                if within(b, 0):
                    act.wait_ge(v_copied, b + 1)
                    if not isinstance(t, int) or t >= 2:
                        act.wait_ge(pv_done, t - 1)
                    act.activation(Vg[odd][:, :, :, 0:DH],
                                   V[par][:, :, g * HG * DH:(g + 1) * HG * DH].rearrange("p n (h d) -> p n h d", h=HG),
                                   ACT.Copy).then_inc(vg_ready, 1)
                for u in range(N2):
                    if within(b, 0):
                        act.wait_ge(s2_filled, N2 * t + u + 1)
                        bank, todo = x_bank(b, g, u), UNITS2[u]
                        h, jb, _ = todo[0]
                        if jb == 2:
                            dst = PR[odd][:, h:h + 2, SEG[2][0]:1280]
                            src = bank.rearrange("p (k n) -> p k n", k=2)
                        else:
                            dst, src = PR[odd][:, h, SEG[jb][0]:SEG[jb][0] + 512], bank
                        act.activation(dst, src, ACT.Exp).then_inc(exp_done, 1)
                    if u == 1 and within(b if g else b - 1, 0):
                        copy_y(NG * b + (g - 1), 1 - odd)
                    if u == 3:
                        if within(b + (g + 3) // NG, 0):
                            copy_maxima(NG * b + (g + 3), 1 - odd)
                        if g == 2 and within(b + 2, 0):
                            second_part(b + 2, 1)
                    if u == 5:
                        if g == 0 and within(b + 2, 0):
                            copy_x(b + 2)
                        if g == 1 and within(b + 2, 0):
                            first_part(b + 2, 0)
                        if g == 2 and within(b - 1, 0):
                            copy_yn(b - 1)
                    if u == 9:
                        if g == 0 and within(b + 2, 0):
                            copy_h(b + 2)
                        if g == 1 and within(b + 2, 0):
                            second_part(b + 2, 0)
                            first_part(b + 2, 1)

            copy_x(0)
            copy_h(0)
            first_part(0, 0)
            second_part(0, 0)
            first_part(0, 1)
            second_part(0, 1)
            act.wait_ge(init_done, INIT)
            all_groups(act, group)
            last_t = NG * B - 1
            copy_y(last_t, last_t % 2)
            copy_yn(B - 1)

        @block.vector
        def _(dve):
            dve.sem_inc(max_taken, RING)

            def norm_stats(b, par):
                dve.wait_ge(x_loaded, 16 * (b + 1))
                for n in range(NB):
                    dve.bn_stats(stats[:, n, :], x_in[par][:, n, :]).then_inc(stats_chain, 1)
                dve.wait_ge(stats_chain, 2 * NB * b + NB)
                wait(dve, pool_chain, 2 * b)
                wait_apart(dve, xn_ready, b, passed)
                for n in range(NB):
                    dve.bn_aggr(mv[:, n, :], stats[:, n, :]).then_inc(stats_chain, 1)

            def normalize(b, par):
                dve.wait_ge(pool_chain, 2 * b + 2)
                dve.wait_ge(stats_chain, 2 * NB * (b + 1))
                wait(dve, ht_filled, b)
                for n in range(NB):
                    last = dve.tensor_scalar(xn[:, n, :], x_in[par][:, n, :], mv[:, n, 0:1], rstd[:, n:n + 1],
                                             ALU.subtract, ALU.mult)
                last.then_inc(xn_ready, 1)

            def remainder(b, k):
                dve.wait_ge(full_ready, 4 * b + 2 * k + 2)
                wait(dve, split_done, 2 * b + k)
                dve.tensor_tensor(rest[:], full[:], part[:, k, 0, :], ALU.subtract).then_inc(rest_ready, 1)

            def third_part(b, k):
                dve.wait_ge(part1_ready, 2 * b + k + 1)
                dve.tensor_tensor(part[:, k, 2, :], rest[:], part[:, k, 1, :], ALU.subtract).then_inc(split_done, 1)

            def copy_v(b, par):
                dve.wait_ge(v_filled, b + 1)
                if within(b, 2):
                    dve.wait_ge(vg_ready, NG * (b - 1))
                dve.tensor_copy(V[par][:].rearrange("p n f -> p (n f)"), C).then_inc(v_copied, 1)

            def unit1(b, g, u):
                ib, heads, per = UNITS1[u]
                t = NG * b + g
                dve.wait_ge(s1_filled, N1 * t + u + 1)
                banks = s1_banks(u)
                dst = nmax[g % 2][:, ib, heads[0]:heads[-1] + 1]
                if per > 1:
                    dst = dst.rearrange("p (k h) -> p k h", h=per)
                    if banks.shape[1] == 1:
                        dst, banks = dst[:, 0, :], banks[:, 0, :, :]
                else:
                    banks = banks[:, :, 0, :]
                dve.tensor_reduce(dst, banks, AX_X, ALU.max, negate=True).then_inc(max_taken, 1)

            def split_maxima(t, odd):
                dve.wait_ge(max_taken, N1 * (t + 1) + RING)
                wait(dve, nm_filled, t)
                dve.tensor_copy(npart[:, :, 0, :], nmax[odd][:]).then_inc(nm_chain, 1)
                dve.wait_ge(nm_chain, 4 * t + 1)
                dve.tensor_tensor(nrest[:], nmax[odd][:], npart[:, :, 0, :], ALU.subtract).then_inc(nm_chain, 1)
                dve.wait_ge(nm_chain, 4 * t + 2)
                dve.tensor_copy(npart[:, :, 1, :], nrest[:]).then_inc(nm_chain, 1)
                dve.wait_ge(nm_chain, 4 * t + 3)
                dve.tensor_tensor(npart[:, :, 2, :], nrest[:], npart[:, :, 1, :], ALU.subtract).then_inc(nm_chain, 1)

            def divide(b, g, par):
                t = NG * b + g
                dve.wait_ge(yt_filled, t + 1)
                turned = C.rearrange("p (n h r) -> p n h r", n=NB, h=HG)
                wait(dve, yn_ready, t)
                dve.reciprocal(rec[:], turned[:, :, :, DH]).then_inc(rec_ready, 1)
                dve.wait_ge(rec_ready, t + 1)
                if g == 0 and within(b, 2):
                    dve.wait_ge(ynt_filled, b - 1)
                dve.tensor_tensor(yn[par][:, :, g * HG:(g + 1) * HG, :], turned[:, :, :, 0:DH],
                                  rec[:].unsqueeze(3).to_broadcast([P, NB, HG, DH]), ALU.mult).then_inc(yn_ready, 1)

            def add_output(b):
                dve.wait_ge(o_filled, b + 1)
                dve.scalar_tensor_tensor(xT[:, b, :], C, mod[:, GATE, one(b)], xT[:, b, :],
                                         ALU.mult, ALU.add).then_inc(x_done, 1)

            def group(b, g, par):
                pj = within(b + 2, 0)
                if within(b + (g + 3) // NG, 0):
                    split_maxima(NG * b + (g + 3), (g + 3) % 2)
                for u in range(N1):
                    if within(b + 1, 0):
                        unit1(b + 1, g, u)
                    if u == 0 and g == 0 and pj:
                        norm_stats(b + 2, par)
                    if u == 1:
                        if g == 0 and pj:
                            normalize(b + 2, par)
                        if g == 2 and pj:
                            third_part(b + 2, 1)
                        if g == 3 and pj:
                            copy_v(b + 2, par)
                    if u == 2:
                        if g == 1 and pj:
                            remainder(b + 2, 0)
                        if within(b if g else b - 1, 0):
                            divide(b if g else b - 1, (g - 1) % NG, par if g else 1 - par)
                    if u == 3 and g == 2 and within(b - 1, 0):
                        add_output(b - 1)
                    if u == 5 and g == 1 and pj:
                        third_part(b + 2, 0)
                        remainder(b + 2, 1)

            norm_stats(0, 0)
            for p in range(2):
                dve.memset(Vg[p][:], 0.0).then_inc(init_done, 1)
            normalize(0, 0)
            dve.memset(zeros[:], 0.0).then_inc(init_done, 1)
            dve.memset(npart_wide[:], 0.0).then_inc(init_done, 1)
            dve.wait_ge(init_done, 4)
            for p in range(2):
                dve.memset(Vg[p][:, :, :, DH:DH + 1], 1.0).then_inc(init_done, 1)
            for k in range(2):
                remainder(0, k)
                third_part(0, k)
            copy_v(0, 0)
            all_groups(dve, group)
            divide(B - 1, NG - 1, (B - 1) % 2)
            add_output(B - 1)


def moe(nc, sb, sem, ps, xT, ident, neghalf, mod, col, a, shg_w, shu_w, shd_w, router_w,
        pos_i, sorted_out):
    FIRST = 3
    ROW = D + 4
    ZT = 10

    sorted_in = nc.dram_tensor("sorted_in", (TILES * P, ROW), F32, kind="Internal").ap()

    gu_w = sb("gu_w", [D, E, 2 * HID])
    down_w = sb("down_w", [P, E, HC, D])
    xc = [sb(f"xc{p}", [D, T]) for p in range(2)]
    hT = [sb(f"hTm{p}", [D, T]) for p in range(2)]
    nT = [sb(f"nTm{p}", [D, T]) for p in range(2)]
    xn = [sb(f"xnm{k}", [P, NB, D]) for k in range(2)]
    stats = [sb(f"stats_m{k}", [P, NB, 6]) for k in range(2)]
    mv = [sb(f"mv_m{k}", [P, NB, 2]) for k in range(2)]
    rstd = [sb(f"rstd_m{k}", [P, NB]) for k in range(2)]
    hall = sb("hall", [D, B, T])
    nall = sb("nall", [D, B, T])
    rows = sb("rows", [P, BLOCKS, ROW])
    zeros = sb("zeros_m", [P, ZT, ROW])
    count_i = sb("count_i", [P, BLOCKS, E], mybir.dt.int32)
    prio = sb("prio", [P, BLOCKS, E])
    steps_P = sb("steps_P", [P, E, BLOCKS])
    tile_no = sb("tile_no", [P, TILES, E - 1])
    before = sb("before", [P, P])
    ones = sb("ones_m", [P, P])
    top, topkey, th_top = sb("top", [P, BLOCKS]), sb("topkey", [P, BLOCKS]), sb("th_top", [P, BLOCKS])
    key = sb("key", [P, BLOCKS, E])
    here = sb("here", [P, BLOCKS, E])
    totals = sb("totals", [P, E, BLOCKS])
    none = sb("none_m", [P, E * BLOCKS])
    sums = sb("sums", [P, E * BLOCKS + 1])
    count = sb("count", [P, E])
    over = sb("over", [P, E, BLOCKS])
    etiles = sb("etiles", [P, E])
    first = sb("first", [P, E + 1])
    shift = sb("shift", [P, E])
    place = sb("place", [P, BLOCKS, E])
    pos = sb("pos", [P, BLOCKS])
    later = sb("later", [P, TILES, E - 1])
    expert = sb("expert", [P, TILES])
    expert_i = sb("expert_i", [P, TILES], mybir.dt.int32)
    th = [sb(f"thm{c}", [P, T]) for c in range(HC)]
    sil = [sb(f"sil{c}", [P, T]) for c in range(HC)]
    hid = [sb(f"hid{p}", [P, HC, T]) for p in range(2)]
    tin = [sb(f"tin{k}", [P, ROW]) for k in range(GROUP)]
    tn = [sb(f"tn{p}", [D, P]) for p in range(2)]
    tth = [sb(f"tth{p}", [P, HID]) for p in range(2)]
    tsil = [sb(f"tsil{p}", [P, HID]) for p in range(2)]
    thid = [sb(f"thid{p}", [P, HID]) for p in range(2)]
    thT = [sb(f"thT{p}", [P, HC, P]) for p in range(2)]
    tout = [sb(f"tout{p}", [P, 2, D]) for p in range(2)]

    PA, PB, PC, PD = (ps[:, k, :] for k in range(4))
    LOG = ps[:, 4, 0:BLOCKS * E].rearrange("p (n e) -> p n e", e=E)
    RANKS, TOTALS = ps[:, 5, 0:BLOCKS * E], ps[:, 6, 0:BLOCKS * E]
    G, U, OUT = [ps[:, 0, :], ps[:, 1, :]], [ps[:, 2, :], ps[:, 3, :]], ps[:, 7, :]
    TIN, TGU = [ps[:, 5, 0:P], ps[:, 6, 0:P]], [ps[:, 0, :], ps[:, 1, :]]
    THT, TY = [ps[:, 2, 0:HID], ps[:, 3, 0:HID]], [ps[:, 4, 0:D], ps[:, 7, 0:D]]

    weights_loaded = sem("m_weights")
    consts, zero_ready, zeroed = sem("m_consts"), sem("m_zero_ready"), sem("m_zeroed")
    init_dve = sem("m_init_dve")
    xc_ready, h_ready, h_kept, n_ready = sem("m_xc_ready"), sem("m_h_ready"), sem("m_h_kept"), sem("m_n_ready")
    n_kept, rows_kept, logits_filled = sem("m_n_kept"), sem("m_rows_kept"), sem("m_logits")
    tokens_filled = [sem(f"m_tokens{k}") for k in range(2)]
    turned = [sem(f"m_turned{k}") for k in range(2)]
    stats_chain = [sem(f"m_stats{k}") for k in range(2)]
    rstd_chain = [sem(f"m_rstd{k}") for k in range(2)]
    xn_ready = [sem(f"m_xn{k}") for k in range(2)]
    route, th_ready, counted, scattered = sem("m_route"), sem("m_th_top"), sem("m_counted"), sem("m_scattered")
    gu_filled, tanh_ready, silu_ready, hid_ready = sem("m_gu"), sem("m_tanh"), sem("m_silu"), sem("m_hid")
    down_done, shared_added, x_added = sem("m_down"), sem("m_shared_added"), sem("m_x_added")
    t_loaded = [sem(f"m_t_loaded{k}") for k in range(GROUP)]
    t_stored = [sem(f"m_t_stored{p}") for p in range(2)]
    t_in, t_n, t_gu, t_th, t_sil, t_hid = (sem(f"m_t_{k}") for k in ("in", "n", "gu", "th", "sil", "hid"))
    t_turned, t_hT, t_down, t_out = (sem(f"m_t_{k}") for k in ("turned", "hT", "down", "out"))
    passed = sem("m_passed")
    CONSTS = 11
    TOP_READY, HERE_READY, ROWS_READY, EXPERTS_READY = 1, 5, 19, 22

    def one(b):
        return slice(b, b + 1) if isinstance(b, int) else bass.ds(b, 1)

    def blocks(b):
        return slice(NB * b, NB * (b + 1)) if isinstance(b, int) else bass.ds(NB * b, NB)

    def late(b, n):
        return not isinstance(b, int) or b >= n

    def norm_steps(eng, step):
        step(-1, 1, True, False)
        step(0, 0, True, True)
        step(1, 1, True, True)
        with eng.Fori(1, B // 2 - 1) as i:
            for q in range(2):
                step(2 * i + q, q, True, True)
        step(B - 2, 0, True, True)
        step(B - 1, 1, False, True)

    def shared_steps(eng, step):
        step(0, 0, True, False)
        step(1, 1, True, True)
        with eng.Fori(1, B // 2) as i:
            for q in range(2):
                step(2 * i + q, q, True, True)
        step(B, 0, False, True)

    def tile_steps(eng, step):
        for k in range(GROUP):
            step(k, k, 0)
        with eng.Fori(1, TILES // GROUP - 1) as i:
            for k in range(GROUP):
                step(GROUP * i + k, k, i)
        for k in range(GROUP):
            step(TILES - GROUP + k, k, TILES // GROUP - 1)

    with nc.Block() as block:
        @block.sync
        def _(sp):
            for dst, src in ((gu_w[:, :, 0:HID], a["L0_ffn_gate_w"].rearrange("e p f -> p e f")),
                             (gu_w[:, :, HID:], a["L0_ffn_up_w"].rearrange("e p f -> p e f")),
                             (down_w[:, :, :, :], a["L0_ffn_down_w"].rearrange("e (c p) f -> p e c f", p=P))):
                sp.dma_start(dst, src).then_inc(weights_loaded, 16)
            sp.wait_ge(zero_ready, 1)
            for z in range(TILES // ZT):
                sp.dma_start(sorted_in[z * ZT * P:(z + 1) * ZT * P, :].rearrange("(p n) f -> p n f", p=P),
                             zeros[:]).then_inc(zeroed, 16)

            def store(t, k):
                half = (k // 2) % 2
                wait_apart(sp, t_out, t + 2, passed)
                if isinstance(t, int):
                    dst = sorted_out[t * P:(t + 2) * P, :]
                else:
                    dst = sorted_out[bass.ds(t * P, 2 * P), :]
                sp.dma_start(dst.rearrange("(n p) f -> p n f", p=P), tout[half][:]).then_inc(t_stored[half], 16)

            def step(t, k):
                if late(t, GROUP):
                    wait_apart(sp, t_hid, t - GROUP + 1, passed)
                src = sorted_in[t * P:(t + 1) * P, :] if isinstance(t, int) else sorted_in[bass.ds(t * P, P), :]
                sp.dma_start(tin[k][:], src).then_inc(t_loaded[k], 16)
                if k % 2 and late(t, GROUP + 1):
                    store(t - GROUP - 1, k - 1)

            sp.wait_ge(scattered, 16 * BLOCKS)
            for t in range(GROUP):
                step(t, t)
            with sp.Fori(1, TILES // GROUP) as i:
                for k in range(GROUP):
                    step(GROUP * i + k, k)
            for t in range(TILES - GROUP, TILES, 2):
                store(t, t % GROUP)
            for half in range(2):
                sp.wait_ge(t_stored[half], 16 * (TILES // 4))

        @block.gpsimd
        def _(pool):
            pool.memset(zeros[:], 0.0).then_inc(zero_ready, 1)
            pool.memset(ones[:], 1.0).then_inc(consts, 1)
            pool.memset(before[:], 1.0).then_inc(consts, 1)
            pool.memset(none[:], 0.0).then_inc(consts, 1)
            pool.iota(count_i[:], pattern=[[0, BLOCKS], [-1, E]], base=E, channel_multiplier=0).then_inc(consts, 1)
            pool.wait_ge(consts, 4)
            pool.affine_select(out=before[:], in_=before[:], compare_op=ALU.is_ge, fill=0.0, base=-1,
                               pattern=[[1, P]], channel_multiplier=-1).then_inc(consts, 1)

            def rstd_of(k, b):
                pool.wait_ge(stats_chain[k], 2 * NB * (b + 1))
                if late(b, 1):
                    wait_apart(pool, xn_ready[k], b, passed)
                pool.tensor_scalar(rstd[k][:], mv[k][:, :, 1], EPS, None, ALU.add).then_inc(rstd_chain[k], 1)
                pool.wait_ge(rstd_chain[k], 2 * b + 1)
                pool.tensor_tensor(rstd[k][:], rstd[k][:], neghalf[:], ALU.pow).then_inc(rstd_chain[k], 1)

            def step(s, par, do_first, do_second):
                if do_first:
                    rstd_of(0, s + 1)
                if do_second:
                    rstd_of(1, s)
                    wait_apart(pool, xn_ready[1], s + 1, passed)
                    pool.tensor_copy(rows[:, blocks(s), 0:D], xn[1][:]).then_inc(rows_kept, 1)

            rstd_of(0, 0)
            pool.tensor_copy(prio[:], count_i[:]).then_inc(consts, 1)
            pool.wait_ge(consts, 6)
            pool.iota(count_i[:].rearrange("p n e -> p (n e)"), pattern=[[0, E], [P, BLOCKS]], base=0,
                      channel_multiplier=0).then_inc(consts, 1)
            pool.wait_ge(consts, 7)
            pool.tensor_copy(steps_P[:].rearrange("p e n -> p (e n)"), count_i[:].rearrange("p n e -> p (n e)")).then_inc(consts, 1)
            pool.wait_ge(consts, 8)
            count_t = later[:].bitcast(mybir.dt.int32)
            pool.iota(count_t, pattern=[[1, TILES], [0, E - 1]], base=0, channel_multiplier=0).then_inc(consts, 1)
            pool.wait_ge(consts, 9)
            pool.tensor_copy(tile_no[:], count_t).then_inc(consts, 1)
            pool.memset(rows[:, :, D + 2:ROW], 0.0).then_inc(consts, 1)
            norm_steps(pool, lambda s, par, f, g: step(s, par, f, g) if not (isinstance(s, int) and s < 0) else None)

            pool.wait_ge(zeroed, 16 * (TILES // ZT))
            pool.wait_ge(route, ROWS_READY)
            for n in range(BLOCKS):
                pool.indirect_dma_start(sorted_in, bass.IndirectOffsetOnAxis(pos_i[:, n:n + 1], 0),
                                        rows[:, n, :], None).then_inc(scattered, 16)

        @block.tensor
        def _(pe):
            cols = lambda n: slice(n * P, (n + 1) * P)

            def turn(bank, src, signal):
                for n in range(NB):
                    last = pe.transpose(bank[:, cols(n)], src(n), ident[:])
                last.then_inc(signal, 1)

            def turn_x(b, par):
                pe.wait_ge(xc_ready, b + 1)
                wait(pe, xn_ready[0], b)
                turn(PA, lambda n: xc[par][:, cols(n)], tokens_filled[0])

            def logits(b, par):
                pe.wait_ge(n_ready, b + 1)
                for n in range(NB):
                    last = pe.matmul(LOG[:, one(NB * b + n), :].rearrange("p o e -> p (o e)"),
                                     nT[par][:, cols(n)], router_w[:], start=True, stop=True,
                                     skip_group_check=True)
                last.then_inc(logits_filled, 1)

            def step(s, par, do_first, do_second):
                if do_second:
                    pe.wait_ge(h_ready, s + 1)
                    wait(pe, xn_ready[1], s)
                    turn(PC, lambda n: hT[par][:, cols(n)], tokens_filled[1])
                    if late(s, 1):
                        logits(s - 1, 1 - par)
                if do_first:
                    pe.wait_ge(xn_ready[0], s + 2)
                    wait(pe, h_ready, s + 1)
                    turn(PB, lambda n: xn[0][:, n, :], turned[0])
                    if not (isinstance(s, int) and s + 2 >= B):
                        turn_x(s + 2, par)
                if do_second:
                    pe.wait_ge(xn_ready[1], s + 1)
                    wait(pe, n_ready, s)
                    turn(PD, lambda n: xn[1][:, n, :], turned[1])

            turn_x(0, 0)
            norm_steps(pe, step)
            logits(B - 1, (B - 1) % 2)

            pe.wait_ge(route, HERE_READY)
            pe.wait_ge(consts, CONSTS)
            flat = here[:].rearrange("p n e -> p (n e)")
            pe.matmul(TOTALS, ones[:], flat, start=True, stop=True).then_inc(counted, 1)
            pe.matmul(RANKS, before[:], flat, start=True, stop=True).then_inc(counted, 1)

            pe.wait_ge(n_kept, B)
            pe.wait_ge(xn_ready[1], B)

            def shared(b, par, do_up, do_down):
                for c in range(HC):
                    if do_up:
                        if late(b, 1):
                            pe.wait_ge(hid_ready, HC * (b - 1) + c + 1)
                        pe.matmul(G[c], shg_w[:, cols(c)], nall[:, b, :], start=True, stop=True)
                        pe.matmul(U[c], shu_w[:, cols(c)], nall[:, b, :], start=True, stop=True).then_inc(gu_filled, 1)
                if do_down:
                    if late(b, 2):
                        pe.wait_ge(shared_added, b - 1)
                    for c in range(HC):
                        pe.wait_ge(hid_ready, HC * (b - 1) + c + 1)
                        last = pe.matmul(OUT, shd_w[:, c, :], hid[1 - par][:, c, :], start=(c == 0), stop=(c == HC - 1))
                    last.then_inc(down_done, 1)

            shared_steps(pe, shared)

            def turn_in(t, k):
                two = k % 2
                if isinstance(t, int):
                    pe.wait_ge(t_loaded[k], 16 * (t // GROUP + 1))
                if late(t, 2):
                    pe.wait_ge(t_n, t - 1)
                pe.transpose(TIN[two], tin[k][:, 0:D], ident[:]).then_inc(t_in, 1)

            def up(t, k, e):
                pe.wait_ge(t_n, t + 1)
                if late(t, 2):
                    pe.wait_ge(t_hid, t - 1)
                w = gu_w[:, one(e), :].rearrange("p o f -> p (o f)")
                pe.matmul(TGU[k % 2], tn[k % 2][:], w, start=True, stop=True).then_inc(t_gu, 1)

            def turn_hidden(t, k):
                two = k % 2
                pe.wait_ge(t_hid, t + 1)
                if late(t, 2):
                    pe.wait_ge(t_hT, t - 1)
                for c in range(HC):
                    last = pe.transpose(THT[two][:, cols(c)], thid[two][:, cols(c)], ident[:])
                last.then_inc(t_turned, 1)

            def down(t, k, e):
                two = k % 2
                pe.wait_ge(t_hT, t + 1)
                if late(t, 2):
                    pe.wait_ge(t_out, t - 1)
                for c in range(HC):
                    w = down_w[:, one(e), c, :].rearrange("p o f -> p (o f)")
                    last = pe.matmul(TY[two], thT[two][:, c, :], w, start=(c == 0), stop=(c == HC - 1))
                last.then_inc(t_down, 1)

            expert_regs = [pe.alloc_register(f"expert{j}") for j in range(GROUP + 2)]

            def load_experts(t0, n):
                pe.reg_load(expert_regs[:n], expert_i[0:1, t0:t0 + n] if isinstance(t0, int)
                            else expert_i[0:1, bass.ds(t0, n)])
                return [pe.snap(r, min_val=0, max_val=E - 1) for r in expert_regs[:n]]

            pe.wait_ge(weights_loaded, 48)
            pe.wait_ge(route, EXPERTS_READY)
            pe.wait_ge(shared_added, B)
            turn_in(0, 0)
            turn_in(1, 1)
            up(0, 0, load_experts(0, 1)[0])

            def group(i, first_group, last_group):
                t = GROUP * i
                lo = 0 if first_group else -1
                experts = load_experts(t + lo, GROUP + (0 if last_group else 1) - lo)
                for k in range(GROUP):
                    if not (last_group and k >= GROUP - 2):
                        n = (k + 2) % GROUP
                        if not isinstance(t, int):
                            pe.wait_ge(t_loaded[n], 16 * (i + 1 + (k + 2) // GROUP))
                        turn_in(t + k + 2, n)
                    if not (last_group and k == GROUP - 1):
                        up(t + k + 1, (k + 1) % GROUP, experts[k + 1 - lo])
                    turn_hidden(t + k, k)
                    if not (first_group and k == 0):
                        down(t + k - 1, (k - 1) % GROUP, experts[k - 1 - lo])
                if last_group:
                    down(t + GROUP - 1, GROUP - 1, experts[GROUP - 1 - lo])

            group(0, True, False)
            with pe.Fori(1, TILES // GROUP - 1) as i:
                group(i, False, False)
            group(TILES // GROUP - 1, False, True)

        @block.scalar
        def _(act):
            def copy_x(b, par):
                if late(b, 2):
                    act.wait_ge(tokens_filled[0], b - 1)
                act.activation(xc[par][:], xT[:, b, :], ACT.Copy).then_inc(xc_ready, 1)

            def step(s, par, do_first, do_second):
                new = 1 - par
                if not isinstance(s, int) or s < B - 2:
                    copy_x(s + 2, par)
                if do_first:
                    if late(s, 1):
                        act.wait_ge(tokens_filled[1], s)
                    act.wait_ge(turned[0], s + 2)
                    if late(s, 1):
                        act.wait_ge(h_kept, s)
                    act.activation(hT[new][:], PB, ACT.Identity, bias=mod[:, FIRST + SHIFT, one(s + 1)],
                                   scale=mod[:, FIRST + SCALE1, one(s + 1)]).then_inc(h_ready, 1)
                if do_second:
                    if late(s, 2):
                        act.wait_ge(logits_filled, s - 1)
                        act.wait_ge(n_kept, s - 1)
                    act.wait_ge(turned[1], s + 1)
                    act.activation(nT[par][:], PD, ACT.Identity, bias=col("ln_b"), scale=col("ln_w")).then_inc(n_ready, 1)
                if do_first:
                    act.wait_ge(h_ready, s + 2)
                    act.activation(hall[:, s + 1, :], hT[new][:], ACT.Copy).then_inc(h_kept, 1)

            copy_x(0, 0)
            norm_steps(act, step)

            act.wait_ge(route, TOP_READY)
            act.activation(th_top[:], top[:], ACT.Tanh, scale=0.5).then_inc(th_ready, 1)

            def shared(b, par, do_up, do_down):
                for c in range(HC if do_up else 0):
                    act.wait_ge(gu_filled, HC * b + c + 1)
                    if late(b, 1):
                        act.wait_ge(silu_ready, HC * (b - 1) + c + 1)
                    act.activation(th[c][:], G[c], ACT.Tanh, scale=0.5).then_inc(tanh_ready, 1)

            shared_steps(act, shared)

            def n_of(t, k):
                two = k % 2
                act.wait_ge(t_in, t + 1)
                if late(t, 2):
                    act.wait_ge(t_gu, t - 1)
                act.activation(tn[two][:], TIN[two], ACT.Identity, bias=col("ln_b"), scale=col("ln_w")).then_inc(t_n, 1)

            def tanh_of(t, k):
                two = k % 2
                act.wait_ge(t_gu, t + 1)
                if late(t, 2):
                    act.wait_ge(t_sil, t - 1)
                act.activation(tth[two][:], TGU[two][:, 0:HID], ACT.Tanh, scale=tin[k][:, D:D + 1]).then_inc(t_th, 1)

            def hidden_of(t, k):
                two = k % 2
                act.wait_ge(t_turned, t + 1)
                if late(t, 2):
                    act.wait_ge(t_down, t - 1)
                act.activation(thT[two][:].rearrange("p c n -> p (c n)"), THT[two], ACT.Copy).then_inc(t_hT, 1)

            def tile(t, k, i):
                if not (isinstance(t, int) and t + 2 >= TILES):
                    n_of(t + 2, (k + 2) % GROUP)
                if not (isinstance(t, int) and t + 1 >= TILES):
                    tanh_of(t + 1, (k + 1) % GROUP)
                hidden_of(t, k)

            n_of(0, 0)
            n_of(1, 1)
            tanh_of(0, 0)
            tile_steps(act, tile)

        @block.vector
        def _(dve):
            done = [0]

            def link(ins):
                ins.then_inc(route, 1)
                done[0] += 1
                dve.wait_ge(route, done[0])

            def norm_stats(k, b):
                dve.wait_ge(tokens_filled[k], b + 1)
                bank = (PA, PC)[k]
                for m in range(NB):
                    dve.bn_stats(stats[k][:, m, :], bank[:, m * P:(m + 1) * P]).then_inc(stats_chain[k], 1)
                dve.wait_ge(stats_chain[k], 2 * NB * b + NB)
                wait(dve, rstd_chain[k], 2 * b)
                wait_apart(dve, xn_ready[k], b, passed)
                for m in range(NB):
                    dve.bn_aggr(mv[k][:, m, :], stats[k][:, m, :]).then_inc(stats_chain[k], 1)

            def normalize(k, b):
                bank = (PA, PC)[k]
                dve.wait_ge(rstd_chain[k], 2 * b + 2)
                dve.wait_ge(stats_chain[k], 2 * NB * (b + 1))
                wait(dve, turned[k], b)
                if k == 1:
                    wait(dve, rows_kept, b)
                for m in range(NB):
                    last = dve.tensor_scalar(xn[k][:, m, :], bank[:, m * P:(m + 1) * P], mv[k][:, m, 0:1],
                                             rstd[k][:, m:m + 1], ALU.subtract, ALU.mult)
                last.then_inc(xn_ready[k], 1)

            def keep_n(b, par):
                dve.wait_ge(n_ready, b + 1)
                dve.tensor_copy(nall[:, b, :], nT[par][:]).then_inc(n_kept, 1)

            def step(s, par, do_first, do_second):
                if do_first:
                    norm_stats(0, s + 1)
                if do_second:
                    norm_stats(1, s)
                    if late(s, 1):
                        keep_n(s - 1, 1 - par)
                if do_first:
                    normalize(0, s + 1)
                if do_second:
                    normalize(1, s)

            norm_steps(dve, step)
            keep_n(B - 1, (B - 1) % 2)

            wide = lambda x: x[:].unsqueeze(2).to_broadcast([P, BLOCKS, E])
            dve.memset(sums[:, 0:1], 0.0).then_inc(init_dve, 1)
            dve.memset(first[:, 0:1], 0.0).then_inc(init_dve, 1)
            dve.wait_ge(logits_filled, B)
            dve.wait_ge(consts, CONSTS)
            link(dve.tensor_reduce(top[:], LOG, AX_X, ALU.max))
            link(dve.tensor_tensor(key[:], LOG, wide(top), ALU.is_equal))
            link(dve.tensor_tensor(key[:], key[:], prio[:], ALU.mult))
            link(dve.tensor_reduce(topkey[:], key[:], AX_X, ALU.max))
            link(dve.tensor_tensor(here[:], key[:], wide(topkey), ALU.is_equal))
            dve.wait_ge(th_ready, 1)
            dve.wait_ge(rows_kept, B)
            link(dve.tensor_scalar(rows[:, :, D], th_top[:], 0.25, 0.25, ALU.mult, ALU.add))
            link(dve.scalar_tensor_tensor(rows[:, :, D + 1], rows[:, :, D], 2.0, rows[:, :, D], ALU.mult, ALU.mult))
            dve.wait_ge(counted, 1)
            link(dve.tensor_copy(totals[:].rearrange("p e n -> p n e"), TOTALS.rearrange("p (n e) -> p n e", e=E)))
            dve.wait_ge(init_dve, 2)
            link(dve.tensor_tensor_scan(sums[:, 1:], totals[:].rearrange("p e n -> p (e n)"), none[:], 0.0,
                                        ALU.add, ALU.add))
            starts = sums[:, 0:E * BLOCKS].rearrange("p (e n) -> p e n", e=E)
            ends = sums[:, 1:].rearrange("p (e n) -> p e n", e=E)
            link(dve.tensor_tensor(count[:], ends[:, :, BLOCKS - 1], starts[:, :, 0], ALU.subtract))
            link(dve.tensor_tensor(over[:], count[:].unsqueeze(2).to_broadcast([P, E, BLOCKS]), steps_P[:], ALU.is_gt))
            link(dve.tensor_reduce(etiles[:], over[:], AX_X, ALU.add))
            link(dve.tensor_tensor_scan(first[:, 1:], etiles[:], none[:, 0:E], 0.0, ALU.add, ALU.add))
            link(dve.scalar_tensor_tensor(shift[:], first[:, 0:E], float(P), starts[:, :, 0], ALU.mult, ALU.subtract))
            dve.wait_ge(counted, 2)
            link(dve.tensor_tensor(place[:], RANKS.rearrange("p (n e) -> p n e", e=E),
                                   starts.rearrange("p e n -> p n e"), ALU.add))
            link(dve.tensor_tensor(place[:], place[:], shift[:].unsqueeze(1).to_broadcast([P, BLOCKS, E]), ALU.add))
            link(dve.tensor_tensor(place[:], place[:], here[:], ALU.mult))
            link(dve.tensor_reduce(pos[:], place[:], AX_X, ALU.add))
            link(dve.tensor_copy(pos_i[:], pos[:]))
            link(dve.tensor_tensor(later[:], tile_no[:], first[:, 1:E].unsqueeze(1).to_broadcast([P, TILES, E - 1]),
                                   ALU.is_ge))
            link(dve.tensor_reduce(expert[:], later[:], AX_X, ALU.add))
            link(dve.tensor_copy(expert_i[:], expert[:]))

            def shared(b, par, do_up, do_down):
                for c in range(HC if do_up else 0):
                    dve.wait_ge(tanh_ready, HC * b + c + 1)
                    dve.scalar_tensor_tensor(sil[c][:], th[c][:], 1.0, G[c], ALU.add, ALU.mult).then_inc(silu_ready, 1)
                    dve.wait_ge(silu_ready, HC * b + c + 1)
                    if late(b, 2):
                        dve.wait_ge(down_done, b - 1)
                    dve.scalar_tensor_tensor(hid[par][:, c, :], sil[c][:], 0.5, U[c], ALU.mult,
                                             ALU.mult).then_inc(hid_ready, 1)
                if do_down:
                    dve.wait_ge(down_done, b)
                    dve.tensor_tensor(hall[:, b - 1, :], hall[:, b - 1, :], OUT, ALU.add).then_inc(shared_added, 1)
                    dve.wait_ge(shared_added, b)
                    dve.scalar_tensor_tensor(xT[:, b - 1, :], hall[:, b - 1, :], mod[:, FIRST + GATE, one(b - 1)],
                                             xT[:, b - 1, :], ALU.mult, ALU.add).then_inc(x_added, 1)

            dve.wait_ge(h_kept, B)
            shared_steps(dve, shared)

            def hidden(t, k):
                two = k % 2
                dve.wait_ge(t_th, t + 1)
                dve.scalar_tensor_tensor(tsil[two][:], tth[two][:], 1.0, TGU[two][:, 0:HID], ALU.add,
                                         ALU.mult).then_inc(t_sil, 1)
                dve.wait_ge(t_sil, t + 1)
                if late(t, 2):
                    dve.wait_ge(t_turned, t - 1)
                dve.scalar_tensor_tensor(thid[two][:], tsil[two][:], tin[k][:, D + 1:D + 2], TGU[two][:, HID:],
                                         ALU.mult, ALU.mult).then_inc(t_hid, 1)

            def output(t, k, i):
                half, two = (k // 2) % 2, k % 2
                dve.wait_ge(t_down, t + 1)
                if two == 0 and late(t, 4):
                    dve.wait_ge(t_stored[half], 16 * (GROUP // 4 * i + k // 4))
                dve.tensor_copy(tout[half][:, two, :], TY[two]).then_inc(t_out, 1)

            def tile(t, k, i):
                if not (isinstance(t, int) and t + 1 >= TILES):
                    hidden(t + 1, (k + 1) % GROUP)
                if late(t, 1):
                    output(t - 1, (k - 1) % GROUP, i)

            hidden(0, 0)
            tile_steps(dve, tile)
            output(TILES - 1, GROUP - 1, TILES // GROUP - 1)


def mixing(nc, out, sb, sem, ps, xT, ident, neghalf, mod0, mod, col, Wmix, WoR, Win2, Wc, w1p, b1p, gcst, pos_i,
           sorted_out):
    GATE0 = 3 + GATE
    back = [sb(f"back{p}", [P, NB, D]) for p in range(2)]
    xc = [sb(f"xc_t{p}", [D, T]) for p in range(2)]
    hp = sb("hp", [D, T + 1])
    xm = [sb(f"xm{p}", [D, T]) for p in range(2)]
    xn = [sb(f"xnt{k}", [P, NB, D]) for k in range(2)]
    stats = [sb(f"stats_t{k}", [P, NB, 6]) for k in range(2)]
    mv = [sb(f"mv_t{k}", [P, NB, 2]) for k in range(2)]
    rstd = [sb(f"rstd_t{k}", [P, NB]) for k in range(2)]
    nmean = [sb(f"nmean_t{k}", [P, NB]) for k in range(2)]
    tdB = sb("tdB", [D, T])
    mx = sb("mx", [D, T + 1])
    num = sb("num", [D, T + 1])
    den = sb("den", [D, T + 1])
    arg = sb("arg", [D, 4, T])
    ex = sb("ex", [D, 4, T])
    mo = sb("mo", [D, T])
    e2v = sb("e2v", [D, T])
    n1, n2 = sb("n1", [D, T]), sb("n2", [D, T])
    d1 = sb("d1", [D, T])
    numer, denom, recd = sb("numer", [D, T]), sb("denom", [D, T]), sb("recd", [D, T])
    thr = sb("thr", [D, T])
    ry, y = sb("ry", [D, T]), sb("y_t", [D, T])
    h2 = sb("h2", [D, T])
    units = sb("s_mlp", [P, T])
    RR = 4
    r = [sb(f"relu{k}", [P, T]) for k in range(RR)]
    xg = [sb(f"xg{p}", [D, T]) for p in range(2)]
    xo = sb("xo", [D, T])
    y_out = [sb(f"y_out{p}", [P, NB, D]) for p in range(2)]

    PA, PB, K, V, R, S, O, O2 = (ps[:, k, :] for k in range(8))
    NORM_IN = (PA, O)

    init_done, init_dve = sem("t_init"), sem("t_init_dve")
    fetched = [sem(f"t_fetched{p}") for p in range(2)]
    back_turned, xc_ready = sem("t_back_turned"), sem("t_xc")
    tokens_filled = [sem(f"t_tokens{k}") for k in range(2)]
    turned = [sem(f"t_turned{k}") for k in range(2)]
    stats_chain = [sem(f"t_stats{k}") for k in range(2)]
    rstd_chain = [sem(f"t_rstd{k}") for k in range(2)]
    xn_ready = [sem(f"t_xn{k}") for k in range(2)]
    h_ready = [sem(f"t_h{k}") for k in range(2)]
    kvr_filled, th_ready, scan_chain, ex_ready = sem("t_kvr"), sem("t_thr"), sem("t_chain"), sem("t_ex")
    pool_done, y_ready, o_filled, xm_ready = sem("t_pool"), sem("t_y"), sem("t_o"), sem("t_xm")
    s_filled, s_ready, relu_ready, relu_used = sem("t_s_filled"), sem("t_s"), sem("t_relu"), sem("t_relu_used")
    xg_ready, xo_ready, xo_turned, yo_ready, stored = sem("t_xg"), sem("t_xo"), sem("t_xo_turned"), sem("t_yo"), sem("t_stored")
    passed = sem("t_passed")
    MX, ARG1, MO, ARG3, DEN, E2V, NUM, N2, DENOM, REC, NUMER, RY = range(1, 13)
    CH = RY
    ARG0, ARG2, D1, N1 = range(1, 5)
    PCH = N1
    YO0, XO0, STORED0, USED0 = 1, 1, 32, 4
    RSTEPS = 4
    EXPS = 3
    before, now = slice(0, T), slice(1, T + 1)

    def one(b):
        return slice(b, b + 1) if isinstance(b, int) else bass.ds(b, 1)

    def late(b, n):
        return not isinstance(b, int) or b >= n

    def steps(eng, step):
        step(-1, 1, True, False, False, False)
        step(0, 0, True, True, False, False)
        step(1, 1, True, True, True, False)
        with eng.Fori(1, B // 2 - 1) as i:
            for q in range(2):
                step(2 * i + q, q, True, True, True, True)
        step(B - 2, 0, True, True, True, True)
        step(B - 1, 1, False, True, True, True)
        step(B, 0, False, False, True, True)
        step(B + 1, 1, False, False, False, True)

    with nc.Block() as block:
        @block.sync
        def _(sp):
            sp.sem_inc(stored, STORED0)

            def store(b, par):
                wait_apart(sp, stored, 16 * b + STORED0, passed)
                wait_apart(sp, yo_ready, b + 1 + YO0, passed)
                sp.dma_start(out[b].rearrange("(n p) f -> p n f", p=P), y_out[par][:]).then_inc(stored, 16)

            steps(sp, lambda s, par, front, mix, mid, end: store(s - 2, par) if end else None)
            sp.wait_ge(stored, 16 * B + STORED0)

        @block.gpsimd
        def _(pool):
            def fetch(b):
                if b >= 2:
                    pool.wait_ge(back_turned, b - 1)
                for n in range(NB):
                    pool.indirect_dma_start(back[b % 2][:, n, :], None, sorted_out,
                                            bass.IndirectOffsetOnAxis(pos_i[:, NB * b + n:NB * b + n + 1], 0)
                                            ).then_inc(fetched[b % 2], 16)

            fetch(0)
            pool.memset(hp[:, 0:1], 0.0).then_inc(init_done, 1)
            pool.memset(mx[:, 0:1], TINY_MX).then_inc(init_done, 1)
            pool.memset(num[:, 0:1], 0.0).then_inc(init_done, 1)
            pool.memset(den[:, 0:1], 0.0).then_inc(init_done, 1)

            def rstd_of(k, b):
                pool.wait_ge(stats_chain[k], 2 * NB * (b + 1))
                wait(pool, xn_ready[k], b)
                pool.tensor_scalar(rstd[k][:], mv[k][:, :, 1], EPS, None, ALU.add).then_inc(rstd_chain[k], 1)
                pool.tensor_scalar(nmean[k][:], mv[k][:, :, 0], -1.0, None, ALU.mult).then_inc(rstd_chain[k], 1)
                pool.wait_ge(rstd_chain[k], RSTEPS * b + 1)
                pool.tensor_tensor(rstd[k][:], rstd[k][:], neghalf[:], ALU.pow).then_inc(rstd_chain[k], 1)
                pool.wait_ge(rstd_chain[k], RSTEPS * b + 3)
                pool.tensor_tensor(nmean[k][:], nmean[k][:], rstd[k][:], ALU.mult).then_inc(rstd_chain[k], 1)

            for s in range(-1, B + 1):
                front, mix, mid = s + 1 < B, 0 <= s < B, s >= 1
                if mix:
                    pool.wait_ge(scan_chain, CH * s + MX)
                    pool.tensor_tensor(arg[:, 0, :], mx[:, before], mx[:, now], ALU.subtract).then_inc(pool_done, 1)
                    pool.wait_ge(scan_chain, CH * s + MO)
                    pool.tensor_tensor(arg[:, 2, :], mx[:, before], mo[:], ALU.subtract).then_inc(pool_done, 1)
                if mid:
                    rstd_of(1, s - 1)
                if mix:
                    pool.wait_ge(ex_ready, EXPS * s + 3)
                    pool.wait_ge(scan_chain, CH * s + DEN)
                    pool.tensor_tensor(d1[:], ex[:, 2, :], den[:, before], ALU.mult).then_inc(pool_done, 1)
                    pool.wait_ge(scan_chain, CH * s + NUM)
                    pool.tensor_tensor(n1[:], ex[:, 2, :], num[:, before], ALU.mult).then_inc(pool_done, 1)
                if front:
                    rstd_of(0, s + 1)
                if mid:
                    pool.wait_ge(xm_ready, s)
                    if s >= 3:
                        pool.wait_ge(xo_ready, s - 2)
                    pool.tensor_scalar(xg[1 - s % 2][:], xm[1 - s % 2][:], gcst[:, s - 1:s], None, ALU.add).then_inc(xg_ready, 1)
                if s + 2 < B:
                    fetch(s + 2)

        @block.tensor
        def _(pe):
            def cols(n):
                return slice(n * P, (n + 1) * P)

            def turn(bank, src, signal):
                for n in range(NB):
                    last = pe.transpose(bank[:, cols(n)], src(n), ident[:])
                last.then_inc(signal, 1)

            def step(s, par, front, mix, mid, end):
                other = 1 - par

                def project(k, bank):
                    pe.matmul(bank, Wmix[:, 2 * k, :], hp[:, 1:T + 1], start=True, stop=False)
                    pe.matmul(bank, Wmix[:, 2 * k + 1, :], hp[:, 0:T], start=False, stop=True).then_inc(kvr_filled, 1)

                def add_units(pairs):
                    for p in pairs:
                        pe.wait_ge(relu_ready, HP * (s - 2) + p + 1)
                        pe.matmul(O2, Wc[:, p, :], r[p % RR][:], start=(p == 0), stop=(p == HP - 1)).then_inc(relu_used, 1)

                if front:
                    pe.wait_ge(fetched[other], 8 * NB * (s + 1 + (2 - other)))
                    wait(pe, xn_ready[0], s + 1)
                    turn(PA, lambda n: back[other][:, n, :], back_turned)
                if mid:
                    pe.wait_ge(xm_ready, s)
                    turn(O, lambda n: xm[other][:, cols(n)], tokens_filled[1])
                if end:
                    pe.wait_ge(yo_ready, s - 2 + YO0)
                    add_units(range(0, 3))
                if front:
                    pe.wait_ge(xc_ready, s + 2)
                    turn(PA, lambda n: xc[other][:, cols(n)], tokens_filled[0])
                if end:
                    add_units(range(3, 4))
                if mid:
                    pe.wait_ge(xn_ready[1], s)
                    wait(pe, s_ready, s - 1)
                    turn(S, lambda n: xn[1][:, n, :], turned[1])
                if end:
                    add_units(range(4, 6))
                if mid:
                    pe.wait_ge(h_ready[1], s)
                    pe.matmul(S, Win2[:].rearrange("p q m -> p (q m)"), h2[:], start=True, stop=True).then_inc(s_filled, 1)
                if front:
                    pe.wait_ge(xn_ready[0], s + 2)
                    wait(pe, h_ready[0], s + 1)
                    turn(PB, lambda n: xn[0][:, n, :], turned[0])
                if end:
                    add_units(range(6, HP))
                if mix:
                    pe.wait_ge(y_ready, s + 1)
                    wait(pe, xn_ready[1], s)
                    pe.matmul(O, WoR[:], y[:], start=True, stop=True).then_inc(o_filled, 1)
                if front:
                    pe.wait_ge(h_ready[0], s + 2)
                    if mix:
                        pe.wait_ge(scan_chain, CH * s + N2)
                        pe.wait_ge(th_ready, s + 1)
                    project(0, K)
                if end:
                    pe.wait_ge(xo_ready, s - 1)
                    turn(O2, lambda n: xo[:, cols(n)], xo_turned)
                if front:
                    project(1, V)
                    project(2, R)

            pe.sem_inc(xo_turned, XO0)
            pe.sem_inc(relu_used, USED0)
            pe.wait_ge(init_done, 4)
            steps(pe, step)

        @block.scalar
        def _(act):
            def normalize(k, b):
                act.wait_ge(rstd_chain[k], RSTEPS * (b + 1))
                wait(act, turned[k], b)
                for n in range(NB):
                    last = act.activation(xn[k][:, n, :], NORM_IN[k][:, n * P:(n + 1) * P], ACT.Identity,
                                          bias=nmean[k][:, n:n + 1], scale=rstd[k][:, n:n + 1])
                last.then_inc(xn_ready[k], 1)

            def step(s, par, front, mix, mid, end):
                def relu(pairs):
                    for p in pairs:
                        act.wait_ge(relu_used, HP * (s - 2) + p - RR + 1 + USED0)
                        act.activation(r[p % RR][:], units[:], ACT.Relu, bias=b1p[:, p:p + 1],
                                       scale=w1p[:, p:p + 1]).then_inc(relu_ready, 1)

                if mix:
                    act.wait_ge(scan_chain, CH * s + ARG1)
                    act.activation(ex[:, 1, :], arg[:, 1, :], ACT.Exp).then_inc(ex_ready, 1)
                    act.wait_ge(pool_done, PCH * s + ARG0)
                    act.activation(ex[:, 0, :], arg[:, 0, :], ACT.Exp, bias=col("ntd")).then_inc(ex_ready, 1)
                if end:
                    act.wait_ge(s_ready, s - 1)
                    relu(range(0, 1))
                if mix:
                    act.wait_ge(pool_done, PCH * s + ARG2)
                    act.wait_ge(scan_chain, CH * s + ARG3)
                    act.activation(ex[:, 2:4, :], arg[:, 2:4, :], ACT.Exp).then_inc(ex_ready, 1)
                if mix:
                    act.wait_ge(kvr_filled, 3 * s + 3)
                    act.activation(thr[:], R, ACT.Tanh, scale=0.5).then_inc(th_ready, 1)
                if end:
                    relu(range(1, 4))
                if mid:
                    normalize(1, s - 1)
                if end:
                    relu(range(4, 5))
                if mid:
                    act.wait_ge(turned[1], s)
                    wait(act, s_filled, s - 1)
                    act.activation(h2[:], S, ACT.Identity, bias=mod[:, 3 + SHIFT, one(s - 1)],
                                   scale=mod[:, 3 + SCALE1, one(s - 1)]).then_inc(h_ready[1], 1)
                if end:
                    relu(range(5, 6))
                if front:
                    normalize(0, s + 1)
                if end:
                    relu(range(6, 7))
                if front:
                    act.wait_ge(turned[0], s + 2)
                    wait(act, kvr_filled, 3 * (s + 1))
                    act.activation(hp[:, 1:T + 1], PB, ACT.Identity, bias=mod[:, SHIFT, one(s + 1)],
                                   scale=mod[:, SCALE1, one(s + 1)]).then_inc(h_ready[0], 1)
                if end:
                    relu(range(7, HP))
                if mid:
                    act.wait_ge(s_filled, s)
                    if late(s, 2):
                        act.wait_ge(relu_ready, HP * (s - 1))
                    act.activation(units[:], S, ACT.Identity, bias=col("bin")).then_inc(s_ready, 1)
                if end:
                    act.wait_ge(xo_turned, s - 1 + XO0)
                    act.wait_ge(stored, 16 * (s - 3) + STORED0)
                    act.activation(y_out[par][:].rearrange("p n f -> p (n f)"), O2, ACT.Copy).then_inc(yo_ready, 1)

            act.sem_inc(yo_ready, YO0)
            steps(act, step)

        @block.vector
        def _(dve):
            dve.memset(mo[:], 1.0).then_inc(init_dve, 1)
            dve.wait_ge(init_dve, 1)
            dve.tensor_scalar(tdB[:], mo[:], col("ntd"), None, ALU.mult).then_inc(init_dve, 1)
            dve.wait_ge(init_dve, 2)
            dve.wait_ge(init_done, 4)

            def norm_stats(k, b):
                dve.wait_ge(tokens_filled[k], b + 1)
                for n in range(NB):
                    dve.bn_stats(stats[k][:, n, :], NORM_IN[k][:, n * P:(n + 1) * P]).then_inc(stats_chain[k], 1)
                dve.wait_ge(stats_chain[k], 2 * NB * b + NB)
                wait_apart(dve, rstd_chain[k], RSTEPS * b, passed)
                for n in range(NB):
                    dve.bn_aggr(mv[k][:, n, :], stats[k][:, n, :]).then_inc(stats_chain[k], 1)

            def step(s, par, front, mix, mid, end):
                def link(ins):
                    ins.then_inc(scan_chain, 1)

                def after(n):
                    dve.wait_ge(scan_chain, CH * s + n)

                if mix:
                    dve.wait_ge(kvr_filled, 3 * s + 1)
                    wait(dve, pool_done, PCH * s)
                    link(dve.tensor_tensor_scan(mx[:, now], tdB[:], K, TINY_MX, ALU.add, ALU.max))
                    after(MX)
                    wait(dve, ex_ready, EXPS * s)
                    link(dve.tensor_tensor(arg[:, 1, :], K, mx[:, now], ALU.subtract))
                    link(dve.scalar_tensor_tensor(mo[:], K, col("tf"), mx[:, before], ALU.add, ALU.max))
                    after(MO)
                    link(dve.scalar_tensor_tensor(arg[:, 3, :], K, col("tf"), mo[:], ALU.add, ALU.subtract))
                if mix:
                    dve.wait_ge(ex_ready, EXPS * s + 2)
                    link(dve.tensor_tensor_scan(den[:, now], ex[:, 0, :], ex[:, 1, :], 0.0, ALU.mult, ALU.add))
                    dve.wait_ge(kvr_filled, 3 * s + 2)
                    link(dve.tensor_tensor(e2v[:], ex[:, 1, :], V, ALU.mult))
                    after(E2V)
                    link(dve.tensor_tensor_scan(num[:, now], ex[:, 0, :], e2v[:], 0.0, ALU.mult, ALU.add))
                if mid:
                    norm_stats(1, s - 1)
                if front:
                    dve.wait_ge(back_turned, s + 2)
                    if late(s, 1):
                        dve.wait_ge(tokens_filled[0], s)
                    dve.scalar_tensor_tensor(xc[1 - par][:], PA, mod0[:, GATE0, one(s + 1)], xT[:, s + 1, :],
                                             ALU.mult, ALU.add).then_inc(xc_ready, 1)
                if mix:
                    dve.wait_ge(ex_ready, EXPS * s + 3)
                    link(dve.tensor_tensor(n2[:], ex[:, 3, :], V, ALU.mult))
                if front:
                    norm_stats(0, s + 1)
                if mix:
                    dve.wait_ge(pool_done, PCH * s + D1)
                    link(dve.tensor_tensor(denom[:], d1[:], ex[:, 3, :], ALU.add))
                    after(DENOM)
                    link(dve.reciprocal(recd[:], denom[:]))
                    dve.wait_ge(pool_done, PCH * s + N1)
                    link(dve.tensor_tensor(numer[:], n1[:], n2[:], ALU.add))
                    after(NUMER)
                    dve.wait_ge(th_ready, s + 1)
                    link(dve.scalar_tensor_tensor(ry[:], thr[:], 1.0, numer[:], ALU.add, ALU.mult))
                    after(RY)
                    wait(dve, o_filled, s)
                    dve.scalar_tensor_tensor(y[:], ry[:], 0.5, recd[:], ALU.mult, ALU.mult).then_inc(y_ready, 1)
                if end:
                    dve.wait_ge(relu_used, HP * (s - 1) + USED0)
                    dve.wait_ge(xg_ready, s - 1)
                    dve.wait_ge(xo_turned, s - 2 + XO0)
                    dve.scalar_tensor_tensor(xo[:], O2, mod[:, 3 + GATE, one(s - 2)], xg[par][:], ALU.mult,
                                             ALU.add).then_inc(xo_ready, 1)
                if mix:
                    dve.wait_ge(o_filled, s + 1)
                    if late(s, 2):
                        dve.wait_ge(xg_ready, s - 1)
                    dve.scalar_tensor_tensor(xm[par][:], O, mod[:, GATE, one(s)], xc[par][:], ALU.mult,
                                             ALU.add).then_inc(xm_ready, 1)

            steps(dve, step)


_INS = ["L0_attn_x", "L0_attn_Wq", "L0_attn_bq", "L0_attn_Wk", "L0_attn_bk", "L0_attn_Wv", "L0_attn_bv",
        "L0_attn_Wo", "L0_attn_bo", "L0_attn_Wq_lsr", "L0_attn_Wk_lsr", "L0_ffn_ln_w", "L0_ffn_ln_b",
        "L0_ffn_router_w", "L0_ffn_gate_w", "L0_ffn_up_w", "L0_ffn_down_w", "L0_ffn_sh_gate",
        "L0_ffn_sh_up", "L0_ffn_sh_down", "L0_c", "L0_wmod", "L1_attn_Wk", "L1_attn_Wv", "L1_attn_Wr",
        "L1_attn_Wo", "L1_attn_time_decay", "L1_attn_time_first", "L1_attn_time_mix_key",
        "L1_attn_time_mix_value", "L1_attn_time_mix_receptance", "L1_ffn_Win", "L1_ffn_bin_", "L1_ffn_W1",
        "L1_ffn_b1", "L1_ffn_W2", "L1_ffn_b2", "L1_ffn_Wout", "L1_ffn_bout", "L1_c", "L1_wmod"]


def kernel(**inputs):
    import numpy as _np
    import concourse.bacc as _bacc
    from concourse import mybir as _mybir
    from concourse.bass_utils import run_bass_kernel_spmd as _run

    nc = _bacc.Bacc("TRN2", target_bir_lowering=False, num_devices=1)
    arrays, args = {}, {}
    for name in _INS:
        x = _np.ascontiguousarray(inputs[name])
        arrays[f"in_{name}_dram"] = x
        args[name] = nc.dram_tensor(f"in_{name}_dram", x.shape, _mybir.dt.from_np(x.dtype), kind="ExternalInput").ap()
    y = nc.dram_tensor("out_dram", (B, T, D), F32, kind="ExternalOutput").ap()
    adaln_kernel(nc, args, y)
    r = _run(nc, [arrays], core_ids=[0])
    return r.results[0]["out_dram"]
```
